# Optimizing a Trainium2 kernel written in Bass

```python
import numpy as np
import jax
import jax.numpy as jnp

def _softmax(x, axis=-1):
    return jax.nn.softmax(x, axis=axis)

def _gelu(x):
    return jax.nn.gelu(x, approximate=True)

def _silu(x):
    return jax.nn.silu(x)

def _sigmoid(x):
    return jax.nn.sigmoid(x)

def _layernorm(x, axis=-1, eps=1e-05):
    m = jnp.mean(x, axis=axis, keepdims=True)
    v = jnp.var(x, axis=axis, keepdims=True)
    return (x - m) / jnp.sqrt(v + eps)

def _scatter_add(tgt, idx, src, axis=0):
    return tgt.at[idx].add(src)

def _segment_sum(src, seg, n):
    return jax.ops.segment_sum(src, seg, n)
kernel_name = 'mk_seq_postln_d1_jaxref_r8_0e9e3f'

def setup_inputs(seed: int=0):
    np.random.seed(seed)
    _w = jnp.asarray

    def _L0_attn_setup():
        import jax, jax.numpy as jnp
        import numpy as np
        H, HK, HD, WIN = (16, 4, 128, 64)
        NEG = -1e+30

        def _local_attn(x, Wq, Wk, Wv, Wo):
            B, T, D = x.shape
            nrep = H // HK
            nb = T // WIN
            scale = 1.0 / np.sqrt(HD)
            q = (x @ Wq).reshape(B, nb, WIN, HK, nrep, HD)
            k = (x @ Wk).reshape(B, nb, WIN, HK, HD)
            v = (x @ Wv).reshape(B, nb, WIN, HK, HD)
            k_prev = jnp.concatenate([jnp.zeros_like(k[:, :1]), k[:, :-1]], axis=1)
            v_prev = jnp.concatenate([jnp.zeros_like(v[:, :1]), v[:, :-1]], axis=1)
            kcat = jnp.concatenate([k_prev, k], axis=2)
            vcat = jnp.concatenate([v_prev, v], axis=2)
            r = jnp.arange(WIN)[:, None]
            c = jnp.arange(2 * WIN)[None, :]
            allowed = jnp.where(c < WIN, c > r, c - WIN <= r)
            first_block = (jnp.arange(nb) == 0)[:, None, None]
            allowed = allowed[None, :, :] & ~(first_block & (c < WIN)[None])
            scores = jnp.einsum('bnqhrd,bnkhd->bnhrqk', q, kcat) * scale
            scores = jnp.where(allowed[None, :, None, None], scores, NEG)
            attn = jax.nn.softmax(scores, axis=-1)
            out = jnp.einsum('bnhrqk,bnkhd->bnqhrd', attn, vcat)
            out = out.reshape(B, T, H * HD)
            return out @ Wo
        key = jax.random.key(seed)
        ks = jax.random.split(key, 5)
        B, T, D = (2, 512, 256)
        s = 1.0 / np.sqrt(D)
        return {'x': jax.random.normal(ks[0], (B, T, D), dtype=jnp.float32), 'Wq': jax.random.normal(ks[1], (D, H * HD), dtype=jnp.float32) * s, 'Wk': jax.random.normal(ks[2], (D, HK * HD), dtype=jnp.float32) * s, 'Wv': jax.random.normal(ks[3], (D, HK * HD), dtype=jnp.float32) * s, 'Wo': jax.random.normal(ks[4], (H * HD, D), dtype=jnp.float32) * s}
    _L0_attn_in = _L0_attn_setup()

    def _L0_ffn_setup():
        import jax, jax.numpy as jnp
        import numpy as np
        NUM_EXPERTS = 8
        TOP_K = 2
        LORA_ALPHA = 2.0
        LORA_RANK = 16
        D_MODEL = 256
        D_HIDDEN = 704
        key = jax.random.key(seed)
        ks = jax.random.split(key, 11)
        B, S, D, H, E, R = (2, 128, D_MODEL, D_HIDDEN, NUM_EXPERTS, LORA_RANK)
        sd = 1.0 / np.sqrt(D)
        sh = 1.0 / np.sqrt(H)
        x = jax.random.normal(ks[0], (B, S, D), jnp.float32)
        gate_w = jax.random.normal(ks[1], (E, D), jnp.float32) * sd
        w_up = jax.random.normal(ks[2], (H, D), jnp.float32) * sd
        w_gate = jax.random.normal(ks[3], (H, D), jnp.float32) * sd
        w_down = jax.random.normal(ks[4], (D, H), jnp.float32) * sh
        up_A = jax.random.normal(ks[5], (E, R, D), jnp.float32) * sd
        up_B = jax.random.normal(ks[6], (E, H, R), jnp.float32) * 0.02
        gate_A = jax.random.normal(ks[7], (E, R, D), jnp.float32) * sd
        gate_B = jax.random.normal(ks[8], (E, H, R), jnp.float32) * 0.02
        down_A = jax.random.normal(ks[9], (E, R, H), jnp.float32) * sh
        down_B = jax.random.normal(ks[10], (E, D, R), jnp.float32) * 0.02
        return {'x': x, 'gate_w': gate_w, 'w_up': w_up, 'w_gate': w_gate, 'w_down': w_down, 'up_A': up_A, 'up_B': up_B, 'gate_A': gate_A, 'gate_B': gate_B, 'down_A': down_A, 'down_B': down_B}
    _L0_ffn_in = _L0_ffn_setup()
    _d = {'L0_attn_x': _L0_attn_in['x'], 'L0_attn_Wq': _L0_attn_in['Wq'], 'L0_attn_Wk': _L0_attn_in['Wk'], 'L0_attn_Wv': _L0_attn_in['Wv'], 'L0_attn_Wo': _L0_attn_in['Wo'], 'L0_ffn_gate_w': _L0_ffn_in['gate_w'], 'L0_ffn_w_up': _L0_ffn_in['w_up'], 'L0_ffn_w_gate': _L0_ffn_in['w_gate'], 'L0_ffn_w_down': _L0_ffn_in['w_down'], 'L0_ffn_up_A': _L0_ffn_in['up_A'], 'L0_ffn_up_B': _L0_ffn_in['up_B'], 'L0_ffn_gate_A': _L0_ffn_in['gate_A'], 'L0_ffn_gate_B': _L0_ffn_in['gate_B'], 'L0_ffn_down_A': _L0_ffn_in['down_A'], 'L0_ffn_down_B': _L0_ffn_in['down_B']}
    _x0 = _d['L0_attn_x']
    _d['L0_attn_x'] = jax.random.normal(jax.random.fold_in(jax.random.key(seed), 1), (4, 1024, 256), dtype=_x0.dtype)
    del _x0
    return _d

def reference(L0_attn_x, L0_attn_Wq, L0_attn_Wk, L0_attn_Wv, L0_attn_Wo, L0_ffn_gate_w, L0_ffn_w_up, L0_ffn_w_gate, L0_ffn_w_down, L0_ffn_up_A, L0_ffn_up_B, L0_ffn_gate_A, L0_ffn_gate_B, L0_ffn_down_A, L0_ffn_down_B):

    def _L0_attn_ref(x, Wq, Wk, Wv, Wo):
        import jax, jax.numpy as jnp
        import numpy as np
        H, HK, HD, WIN = (16, 4, 128, 64)
        NEG = -1e+30

        def _local_attn(x, Wq, Wk, Wv, Wo):
            B, T, D = x.shape
            nrep = H // HK
            nb = T // WIN
            scale = 1.0 / np.sqrt(HD)
            q = (x @ Wq).reshape(B, nb, WIN, HK, nrep, HD)
            k = (x @ Wk).reshape(B, nb, WIN, HK, HD)
            v = (x @ Wv).reshape(B, nb, WIN, HK, HD)
            k_prev = jnp.concatenate([jnp.zeros_like(k[:, :1]), k[:, :-1]], axis=1)
            v_prev = jnp.concatenate([jnp.zeros_like(v[:, :1]), v[:, :-1]], axis=1)
            kcat = jnp.concatenate([k_prev, k], axis=2)
            vcat = jnp.concatenate([v_prev, v], axis=2)
            r = jnp.arange(WIN)[:, None]
            c = jnp.arange(2 * WIN)[None, :]
            allowed = jnp.where(c < WIN, c > r, c - WIN <= r)
            first_block = (jnp.arange(nb) == 0)[:, None, None]
            allowed = allowed[None, :, :] & ~(first_block & (c < WIN)[None])
            scores = jnp.einsum('bnqhrd,bnkhd->bnhrqk', q, kcat) * scale
            scores = jnp.where(allowed[None, :, None, None], scores, NEG)
            attn = jax.nn.softmax(scores, axis=-1)
            out = jnp.einsum('bnhrqk,bnkhd->bnqhrd', attn, vcat)
            out = out.reshape(B, T, H * HD)
            return out @ Wo
        return _local_attn(x, Wq, Wk, Wv, Wo)

    def _L0_ffn_ref(x, gate_w, w_up, w_gate, w_down, up_A, up_B, gate_A, gate_B, down_A, down_B):
        import jax, jax.numpy as jnp
        import numpy as np
        NUM_EXPERTS = 8
        TOP_K = 2
        LORA_ALPHA = 2.0
        LORA_RANK = 16
        D_MODEL = 256
        D_HIDDEN = 704
        B, S, D = x.shape
        H = w_up.shape[0]
        gate_logits = jnp.einsum('bsd,ed->bse', x, gate_w)
        topw, sel = jax.lax.top_k(gate_logits, TOP_K)
        topw = jax.nn.softmax(topw.astype(jnp.float32), axis=1).astype(x.dtype)
        xt = x.reshape(-1, D)
        wf = topw.reshape(-1, TOP_K)
        sf = sel.reshape(-1, TOP_K)
        base_up = xt @ w_up.T
        base_gate = xt @ w_gate.T
        mixed_h = jnp.zeros((xt.shape[0], H), x.dtype)
        lora_down = jnp.zeros_like(xt)
        for e in range(NUM_EXPERTS):
            c = jnp.sum(jnp.where(sf == e, wf, 0.0), axis=1)
            lo_up = LORA_ALPHA * (xt @ up_A[e].T @ up_B[e].T)
            lo_gate = LORA_ALPHA * (xt @ gate_A[e].T @ gate_B[e].T)
            h_e = jax.nn.silu(base_up + lo_up) * (base_gate + lo_gate)
            ch = c[:, None] * h_e
            mixed_h = mixed_h + ch
            lora_down = lora_down + LORA_ALPHA * (ch @ down_A[e].T @ down_B[e].T)
        out = mixed_h @ w_down.T + lora_down
        return out.reshape(B, S, D)
    x = L0_attn_x
    x = _layernorm(x + _L0_attn_ref(x, L0_attn_Wq, L0_attn_Wk, L0_attn_Wv, L0_attn_Wo), axis=-1)
    x = _layernorm(x + _L0_ffn_ref(x, L0_ffn_gate_w, L0_ffn_w_up, L0_ffn_w_gate, L0_ffn_w_down, L0_ffn_up_A, L0_ffn_up_B, L0_ffn_gate_A, L0_ffn_gate_B, L0_ffn_down_A, L0_ffn_down_B), axis=-1)
    return x

_drawn_inputs = setup_inputs


def setup_inputs(seed=0):
    import zlib

    import numpy as np

    out = dict(_drawn_inputs(seed))
    spreads = {}
    factors = {'L0_ffn_gate_w': 8.0,
     'L0_ffn_w_up': 8.0,
     'L0_ffn_w_gate': 8.0,
     'L0_ffn_w_down': 8.0,
     'L0_ffn_up_A': 8.0,
     'L0_ffn_up_B': 8.0,
     'L0_ffn_gate_A': 8.0,
     'L0_ffn_gate_B': 8.0,
     'L0_ffn_down_A': 8.0,
     'L0_ffn_down_B': 8.0}
    for name, (base, spread) in spreads.items():
        noise = np.random.default_rng([zlib.crc32(name.encode()), seed]).standard_normal(out[name].shape)
        drawn = base * np.exp(spread * noise) if base else spread * noise
        out[name] = jnp.asarray(drawn.astype(out[name].dtype))
    for name, factor in factors.items():
        out[name] = (out[name] * factor).astype(out[name].dtype)
    return out
```

```python
from contextlib import ExitStack

import concourse.bass as bass
from concourse import mybir

F32 = mybir.dt.float32
F32R = mybir.dt.float32r
BF16 = mybir.dt.bfloat16
ALU = mybir.AluOpType
ACT = mybir.ActivationFunctionType
AX = mybir.AxisListType

P = 128
D = 256
DC = D // P
B, T = 4, 1024
HEADS, KV, HD, WIN = 16, 4, 128, 64
REP = HEADS // KV
GT = 256
GW = GT // WIN
NG = B * T // GT
GPB = T // GT
TT = GT // P
NT = B * T // P
E, R, HID = 8, 16, 704
HC = -(-HID // P)
HPAD = HC * P
HLAST = HID - (HC - 1) * P
ER = E * R
FFN_SHAPES = [(DC, HID), (DC, HID), (DC, ER), (DC, ER), (1, HID), (1, HID), (HC, ER), (1, D)]
RQ = DC * REP * HD
RAW = max(DC * (HEADS + 2 * KV) * HD, sum(a * b for a, b in FFN_SHAPES))
SCALE = float(HD) ** -0.5
NEG = -1e30
BIG = 3e38
EPS = 1e-5
HI, LO = 0, 1
PARTS = ((HI, HI), (HI, LO), (LO, HI))


def need(eng, sem, count):
    if isinstance(count, int) and count <= 0:
        return
    eng.wait_ge(sem, count)


def carve(buffer, shapes):
    views, at = [], 0
    for a, b in shapes:
        views.append(buffer[:, at:at + a * b].rearrange("p (a b) -> p a b", a=a))
        at += a * b
    return views


def product(eng, out, stationary, moving, chunks, start=True, stop=True):
    last = None
    n = len(chunks) * len(PARTS)
    for k, c in enumerate(chunks):
        for j, (a, b) in enumerate(PARTS):
            m = k * len(PARTS) + j
            last = eng.matmul(out, stationary(a, c), moving(b, c), start=start and m == 0,
                              stop=stop and m == n - 1, skip_group_check=True)
    return last


def attention_phase(nc, sem, raw, x, wq, wk, wv, wo, gate_wt, ffn_loads, x1_dram, logits, ident, ffn_loaded):
    with ExitStack() as ctx:
        def local(name, shape, dt=F32):
            return ctx.enter_context(nc.sbuf_tensor("attn_" + name, shape, dt))

        def bank(name):
            return ctx.enter_context(nc.psum_tensor("attn_" + name, [P, 512], F32))

        raw_wq = [carve(raw[:, g * RQ:], [(DC, REP * HD)])[0] for g in range(KV)]
        raw_wo = [carve(raw[:, g * RQ:], [(REP, D)])[0] for g in range(KV)]
        raw_wk, raw_wv = carve(raw[:, KV * RQ:], [(DC, KV * HD), (DC, KV * HD)])
        wq_sb = local("wq_sb", [P, 2, DC, HEADS * HD], F32R)
        wk_sb = local("wk_sb", [P, 2, DC, KV * HD], F32R)
        wv_sb = local("wv_sb", [P, 2, DC, KV * HD], F32R)
        wo_sb = local("wo_sb", [P, 2, HEADS, D], F32R)
        gate_sb = local("gate_sb", [P, DC, E])

        x_in = local("x_in", [P, TT, D])
        x_res = local("x_res", [P, TT, D])
        xt = local("xt", [P, 2, DC, GT], F32R)
        kt = local("kt", [P, KV, WIN + GT])
        v_sb = local("v_sb", [P, GW, 2, KV * HD], F32R)
        q_sb = local("q_sb", [P, GW, REP, WIN])
        neg_s = local("neg_s", [P, 2 * GW, P])
        neg_max = local("neg_max", [P, 2 * GW])
        row_sum = local("row_sum", [P, 2 * GW])
        spare = local("spare", [P, 2 * KV + 1])
        row_inv = local("row_inv", [P, 2 * GW])
        prob = local("prob", [P, 2 * GW, P])
        pt_sb = local("pt_sb", [P, 2, GW, REP * WIN], F32R)
        o_sb = local("o_sb", [P, 2, 2, TT, REP, P], F32R)
        summed = local("summed", [P, TT, D])
        stats = local("stats", [P, TT, 6])
        mean_var = local("mean_var", [P, TT, 2])
        var_eps = local("var_eps", [P, TT])
        minus_half = local("minus_half", [P, TT])
        rstd = local("rstd", [P, TT])
        x1_cur = local("x1_cur", [P, TT, D])
        x1t = local("x1t", [P, DC, GT])
        mask = local("mask", [P, P])
        mask_first = local("mask_first", [P, P])
        mask_table = local("mask_table", [P, NG, WIN])

        qp = [bank("qp0"), bank("qp1")]
        sp = [bank("sp0"), bank("sp1")]
        po = [bank("po0"), bank("po1")]
        yp = bank("yp")
        mp = bank("mp")

        x_loaded, res_loaded = sem("x_loaded"), sem("res_loaded")
        wk_loaded, wv_loaded, gate_loaded, x1_stored = (
            sem("wk_loaded"), sem("wv_loaded"), sem("gate_loaded"), sem("x1_stored"))
        wq_loaded = [sem(f"wq_loaded{g}") for g in range(KV)]
        wo_loaded = [sem(f"wo_loaded{g}") for g in range(KV)]
        AT_WK, AT_WQ, AT_WV, AT_WO = 1, (2, 4, 5, 6), 3, (7, 8, 9, 10)
        w_hi, w_lo = sem("w_hi"), sem("w_lo")
        ident_ready, masks_ready, filled = sem("ident_ready"), sem("masks_ready"), sem("filled")
        carry_zero = sem("carry_zero")
        half_ready = sem("half_ready")
        xt_done, xt_hi, xt_lo = sem("xt_done"), sem("xt_hi"), sem("xt_lo")
        q_done, q_copied = sem("q_done"), sem("q_copied")
        k_done, k_copied, k_carried = sem("k_done"), sem("k_copied"), sem("k_carried")
        v_done, v_hi, v_lo, v_carried, v_ready = (sem("v_done"), sem("v_hi"), sem("v_lo"),
                                                  sem("v_carried"), sem("v_ready"))
        s_done, max_done, exp_done = sem("s_done"), sem("max_done"), sem("exp_done")
        inv_done, prob_ready = sem("inv_done"), sem("prob_ready")
        pt_done, pt_hi, pt_lo = sem("pt_done"), sem("pt_hi"), sem("pt_lo")
        o_done, o_hi, o_lo = sem("o_done"), sem("o_hi"), sem("o_lo")
        wo_done, y_read = sem("wo_done"), sem("y_read")
        stats_done, mean_done, var_ready, rstd_ready, x1_ready = (
            sem("stats_done"), sem("mean_done"), sem("var_ready"), sem("rstd_ready"), sem("x1_ready"))
        x1t_done, x1t_copied, logit_done, logit_copied = (
            sem("x1t_done"), sem("x1t_copied"), sem("logit_done"), sem("logit_copied"))
        mask_set = sem("mask_set")

        x_tiles = x.rearrange("(n t p) d -> n p t d", t=TT, p=P)
        x1_tiles = x1_dram.rearrange("(n t p) d -> n p t d", t=TT, p=P)

        with nc.Block() as block:

            @block.sync
            def _(sp_):
                def load_x(i):
                    need(sp_, xt_done, i)
                    sp_.dma_start(x_in[:, :, :], x_tiles[i]).then_inc(x_loaded, 16)

                def load_res(i):
                    need(sp_, y_read, i)
                    sp_.dma_start(x_res[:, :, :], x_tiles[i]).then_inc(res_loaded, 16)

                def store_x1(i):
                    sp_.wait_ge(x1_ready, i + 1)
                    sp_.dma_start(x1_tiles[i], x1_cur[:, :, :]).then_inc(x1_stored, 16)

                load_x(0)
                sp_.dma_start(raw_wk, wk.rearrange("(c p) n -> p c n", p=P)).then_inc(wk_loaded, 16)
                wq_rows = wq.rearrange("(c p) n -> p c n", p=P)
                wo_rows = wo.rearrange("(h p) n -> p h n", p=P)
                for g in range(KV):
                    sp_.dma_start(raw_wq[g], wq_rows[:, :, g * REP * HD:(g + 1) * REP * HD]).then_inc(wq_loaded[g], 16)
                    if g == 0:
                        sp_.dma_start(raw_wv, wv.rearrange("(c p) n -> p c n", p=P)).then_inc(wv_loaded, 16)
                sp_.dma_start(gate_sb[:, :, :], gate_wt.rearrange("(c p) n -> p c n", p=P)).then_inc(gate_loaded, 16)
                load_x(1)
                for g in range(KV):
                    sp_.wait_ge(w_lo, AT_WQ[g])
                    sp_.dma_start(raw_wo[g], wo_rows[:, g * REP:(g + 1) * REP, :]).then_inc(wo_loaded[g], 16)
                load_x(2)
                load_res(0)
                sp_.wait_ge(w_lo, AT_WO[-1])
                for out, src in ffn_loads:
                    sp_.dma_start(out, src).then_inc(ffn_loaded, 16)
                with sp_.Fori(1, NG - 2) as i:
                    load_x(i + 2)
                    load_res(i)
                    store_x1(i - 1)
                for i in (NG - 2, NG - 1):
                    load_res(i)
                    store_x1(i - 1)
                store_x1(NG - 1)
                sp_.wait_ge(x1_stored, 16 * NG)
                sp_.wait_ge(ffn_loaded, 16 * len(ffn_loads))

            @block.gpsimd
            def _(pool):
                def then_wait(instruction, count):
                    instruction.then_inc(filled, 1)
                    pool.wait_ge(filled, count)

                then_wait(pool.memset(ident[:, :], 0.0), 1)
                pool.affine_select(out=ident[:, :], in_=ident[:, :], compare_op=ALU.not_equal, fill=1.0,
                                   base=0, pattern=[[-1, P]], channel_multiplier=1).then_inc(ident_ready, 1)
                pool.wait_ge(ident_ready, 1)
                then_wait(pool.memset(mask[:, :], 0.0), 2)
                then_wait(pool.memset(mask_first[:, :], 0.0), 3)
                then_wait(pool.memset(mask_table[:, :, :], 0.0), 4)
                n = 4
                for half in range(2):
                    rows = slice(half * WIN, (half + 1) * WIN)
                    n += 1
                    then_wait(pool.affine_select(
                        out=mask[rows, 0:WIN], in_=mask[rows, 0:WIN], compare_op=ALU.is_gt, fill=NEG, base=0,
                        pattern=[[1, WIN]], channel_multiplier=-1), n)
                    for m in (mask, mask_first):
                        n += 1
                        then_wait(pool.affine_select(
                            out=m[rows, WIN:P], in_=m[rows, WIN:P], compare_op=ALU.is_ge, fill=NEG, base=0,
                            pattern=[[-1, WIN]], channel_multiplier=1), n)
                    table = mask_table[rows, :, :]
                    n += 1
                    then_wait(pool.affine_select(
                        out=table, in_=table, compare_op=ALU.is_gt, fill=NEG, base=0,
                        pattern=[[0, NG], [1, WIN]], channel_multiplier=-1), n)
                first = mask_table[:, :, :].rearrange("p (b g) k -> p b g k", b=B)[:, :, 0, :]
                pool.memset(first, NEG).then_inc(masks_ready, 1)
                pool.wait_ge(masks_ready, 1)
                pool.memset(kt[:, :, 0:WIN], 0.0).then_inc(carry_zero, 1)
                pool.wait_ge(carry_zero, 1)
                pool.memset(v_sb[WIN:P, 0, :, :].bitcast(F32), 0.0).then_inc(carry_zero, 1)
                pool.wait_ge(carry_zero, 2)
                pool.memset(minus_half[:, :], -0.5).then_inc(half_ready, 1)

                def rstd_of(i):
                    pool.wait_ge(var_ready, i + 1)
                    need(pool, x1_ready, i)
                    pool.tensor_tensor(rstd[:, :], var_eps[:, :], minus_half[:, :], ALU.pow).then_inc(rstd_ready, 1)

                pool.wait_ge(half_ready, 1)
                rstd_of(0)
                with pool.Fori(1, NG) as i:
                    rstd_of(i)

            @block.tensor
            def _(pe):
                def transpose_x(i):
                    pe.wait_ge(x_loaded, 16 * (i + 1))
                    need(pe, logit_copied, i - 2)
                    for c in range(DC):
                        for t in range(TT):
                            last = pe.transpose(mp[:, (c * TT + t) * P:(c * TT + t + 1) * P],
                                                x_in[:, t, c * P:(c + 1) * P], ident[:, :])
                    last.then_inc(xt_done, 1)

                def project_q(i, g):
                    s = 4 * i + g
                    if g == 0:
                        pe.wait_ge(xt_lo, i + 1)
                    if isinstance(i, int) and i == 0:
                        pe.wait_ge(w_lo, AT_WQ[g])
                    for b in range(2):
                        need(pe, q_copied, 2 * s + b - 1)
                        if g == 1:
                            need(pe, k_copied, 2 * i + b + 1)
                        if isinstance(i, int) and i == 0:
                            pe.wait_ge(k_copied if g == 0 else v_lo, b + 1)
                        elif g == 2:
                            pe.wait_ge(v_lo, 2 * i + b + 1)
                        for h in range(2 * b, 2 * b + 2):
                            head = REP * g + h
                            last = product(pe, qp[b][:, (h % 2) * GT:(h % 2 + 1) * GT],
                                           lambda a, c: wq_sb[:, a, c, head * HD:(head + 1) * HD],
                                           lambda a, c: xt[:, a, c, :], range(DC))
                        last.then_inc(q_done, 1)

                def project_k(i):
                    if isinstance(i, int) and i == 0:
                        pe.wait_ge(xt_lo, 1)
                        pe.wait_ge(w_lo, AT_WK)
                    for b in range(2):
                        if not (isinstance(i, int) and i == 0):
                            pe.wait_ge(q_copied, 8 * i + b + 1)
                        for g in range(2 * b, 2 * b + 2):
                            last = product(pe, qp[b][:, (g % 2) * GT:(g % 2 + 1) * GT],
                                           lambda a, c: wk_sb[:, a, c, g * HD:(g + 1) * HD],
                                           lambda a, c: xt[:, a, c, :], range(DC))
                        last.then_inc(k_done, 1)

                def project_v(i):
                    for t in range(TT):
                        if isinstance(i, int) and i == 0:
                            pe.wait_ge(w_lo, AT_WV)
                            pe.wait_ge(q_copied, t + 1)
                        else:
                            pe.wait_ge(q_copied, 8 * i + 2 + t + 1)
                        product(pe, qp[t][:, :], lambda a, c: xt[:, a, c, t * P:(t + 1) * P],
                                lambda a, c: wv_sb[:, a, c, :], range(DC)).then_inc(v_done, 1)

                def scores(i, g):
                    s = 4 * i + g
                    for b in range(2):
                        need(pe, max_done, 2 * s + b - 1)
                        pe.wait_ge(q_copied, 2 * s + 2)
                        if g == 0:
                            pe.wait_ge(k_copied, 2 * i + 2)
                        if isinstance(s, int) and s == 0:
                            pe.wait_ge(carry_zero, 2)
                        for t in range(4):
                            w, pair = 2 * b + t // 2, t % 2
                            last = pe.matmul(sp[b][:, t * P:(t + 1) * P],
                                             q_sb[:, w, 2 * pair:2 * pair + 2, :],
                                             kt[:, g, w * WIN:w * WIN + 2 * WIN], start=True, stop=True)
                        last.then_inc(s_done, 1)

                def transpose_prob(i, g):
                    s = 4 * i + g
                    for b in range(2):
                        pe.wait_ge(prob_ready, 2 * s + b + 1)
                        need(pe, o_lo, 2 * s + b - 1)
                        for t in range(4):
                            last = pe.transpose(po[b][:, t * P:(t + 1) * P], prob[:, 4 * b + t, :], ident[:, :])
                        last.then_inc(pt_done, 1)

                def head_out(i, g):
                    s = 4 * i + g
                    for b in range(2):
                        pe.wait_ge(pt_lo, 2 * s + b + 1)
                        if g == 0 and b == 0:
                            pe.wait_ge(v_ready, i + 1)
                        for w in range(2 * b, 2 * b + 2):
                            last = product(pe, po[b][:, (w % 2) * GT:(w % 2 + 1) * GT],
                                           lambda a, c: v_sb[:, w, a, g * HD:(g + 1) * HD],
                                           lambda a, c: pt_sb[:, a, w, :], (0,))
                        last.then_inc(o_done, 1)

                def project_out(i, g):
                    s = 4 * i + g
                    pe.wait_ge(o_lo, 2 * s + 2)
                    if g == 0:
                        need(pe, y_read, i)
                    if isinstance(i, int) and i == 0:
                        pe.wait_ge(w_lo, AT_WO[g])
                    for t in range(TT):
                        for h in range(REP):
                            last = product(pe, yp[:, t * D:(t + 1) * D],
                                           lambda a, c: o_sb[:, g % 2, a, t, h, :],
                                           lambda a, c: wo_sb[:, a, REP * g + h, :], (0,),
                                           start=(g == 0 and t == 0 and h == 0), stop=(g == KV - 1 and h == REP - 1))
                    last.then_inc(wo_done, 1)

                def transpose_x1(i):
                    pe.wait_ge(x1_ready, i + 1)
                    for c in range(DC):
                        for t in range(TT):
                            last = pe.transpose(mp[:, (c * TT + t) * P:(c * TT + t + 1) * P],
                                                x1_cur[:, t, c * P:(c + 1) * P], ident[:, :])
                    last.then_inc(x1t_done, 1)

                def gate_logits(i):
                    pe.wait_ge(x1t_copied, i + 1)
                    for t in range(TT):
                        for c in range(DC):
                            last = pe.matmul(mp[:, t * E:(t + 1) * E], x1t[:, c, t * P:(t + 1) * P],
                                             gate_sb[:, c, :], start=(c == 0), stop=(c == DC - 1))
                    last.then_inc(logit_done, 1)

                def group(i, first, last):
                    for g in range(KV):
                        transpose_prob(i, g)
                        if not (last and g == 3):
                            scores(i + (g + 1) // KV, (g + 1) % KV)
                        if not (last and g >= 2):
                            project_q(i + (g + 2) // KV, (g + 2) % KV)
                        head_out(i, g)
                        if g == 1 and not last:
                            transpose_x(i + 1)
                        if g == 2:
                            if not last:
                                project_k(i + 1)
                                pe.wait_ge(xt_lo, i + 2)
                            if not first:
                                transpose_x1(i - 1)
                        if g == 3:
                            if not last:
                                project_v(i + 1)
                            if not first:
                                gate_logits(i - 1)
                        if not (first and g == 0):
                            project_out(i - (g == 0), (g - 1) % KV)

                pe.wait_ge(ident_ready, 1)
                transpose_x(0)
                project_k(0)
                project_q(0, 0)
                scores(0, 0)
                project_v(0)
                project_q(0, 1)
                group(0, True, False)
                pe.wait_ge(gate_loaded, 16)
                with pe.Fori(1, NG - 1) as i:
                    group(i, False, False)
                group(NG - 1, False, True)
                project_out(NG - 1, KV - 1)
                pe.wait_ge(logit_copied, NG - 1)
                transpose_x1(NG - 1)
                gate_logits(NG - 1)

            @block.scalar
            def _(act):
                def split_hi(out, raw):
                    act.activation(out, raw, ACT.Copy).then_inc(w_hi, 1)

                def prob_hi(i, g):
                    s = 4 * i + g
                    for b in range(2):
                        act.wait_ge(pt_done, 2 * s + b + 1)
                        need(act, o_done, 2 * s + b - 1)
                        act.activation(pt_sb[:, HI, 2 * b:2 * b + 2, :].rearrange("p w n -> p (w n)"),
                                       po[b][:, :], ACT.Copy).then_inc(pt_hi, 1)

                def exps(i, g, b):
                    s = 4 * i + g
                    act.wait_ge(max_done, 2 * s + b + 1)
                    need(act, pt_done, 2 * s + b - 1)
                    for t in range(4):
                        n, w = 4 * b + t, 2 * b + t // 2
                        out, src = prob[:, n, :], neg_s[:, n, :]
                        if w % 2 == 0:
                            out = out.rearrange("p (a k) -> p a k", a=2)[:, ::-1, :]
                            src = src.rearrange("p (a k) -> p a k", a=2)
                        last = act.activation(out, src, ACT.Exp, bias=neg_max[:, n:n + 1], scale=-1.0,
                                              accum_out=row_sum[:, n:n + 1])
                    last.then_inc(exp_done, 1)

                def copy_q(i, g, b):
                    s = 4 * i + g
                    act.wait_ge(q_done, 2 * s + b + 1)
                    need(act, s_done, 2 * s)
                    act.activation(q_sb[:, :, 2 * b:2 * b + 2, :].rearrange("p w h q -> p h w q"),
                                   qp[b][:, :].rearrange("p (h w q) -> p h w q", h=2, w=GW),
                                   ACT.Copy).then_inc(q_copied, 1)

                def out_hi(i, g):
                    s = 4 * i + g
                    for b in range(2):
                        act.wait_ge(o_done, 2 * s + b + 1)
                        need(act, wo_done, s - 1)
                        act.activation(o_sb[:, g % 2, HI, b, :, :].rearrange("p h (w q) -> p w h q", w=2),
                                       po[b][:, :].rearrange("p (w h q) -> p w h q", w=2, h=REP),
                                       ACT.Copy).then_inc(o_hi, 1)

                def xt_hi_of(i):
                    act.wait_ge(xt_done, i + 1)
                    need(act, q_done, 8 * i)
                    act.activation(xt[:, HI, :, :].rearrange("p c n -> p (c n)"), mp[:, :], ACT.Copy).then_inc(xt_hi, 1)

                def copy_k(i):
                    need(act, k_carried, i)
                    for b in range(2):
                        act.wait_ge(k_done, 2 * i + b + 1)
                        act.activation(kt[:, 2 * b:2 * b + 2, WIN:], qp[b][:, :].rearrange("p (g n) -> p g n", g=2),
                                       ACT.Copy).then_inc(k_copied, 1)

                def v_hi_of(i):
                    need(act, v_carried, i)
                    need(act, o_done, 8 * i)
                    for t in range(TT):
                        act.wait_ge(v_done, 2 * i + t + 1)
                        act.activation(v_sb[:, 2 * t + 1, HI, :], qp[t][:, :], ACT.Copy).then_inc(v_hi, 1)

                def copy_x1t(i):
                    act.wait_ge(x1t_done, i + 1)
                    act.activation(x1t[:, :, :].rearrange("p c n -> p (c n)"), mp[:, :], ACT.Copy).then_inc(x1t_copied, 1)

                def group(i, first, last):
                    for g in range(KV):
                        prob_hi(i, g)
                        nxt = (i + (g + 1) // KV, (g + 1) % KV)
                        nxt2 = (i + (g + 2) // KV, (g + 2) % KV)
                        for b in range(2):
                            if not (last and g == 3):
                                exps(*nxt, b)
                            if not (last and g >= 2):
                                copy_q(*nxt2, b)
                        out_hi(i, g)
                        if g == 1 and not last:
                            xt_hi_of(i + 1)
                        if g == 2:
                            if not last:
                                copy_k(i + 1)
                            if not first:
                                copy_x1t(i - 1)
                        if g == 3 and not last:
                            v_hi_of(i + 1)
                        if first:
                            act.wait_ge(wo_loaded[g], 16)
                            split_hi(wo_sb[:, HI, g * REP:(g + 1) * REP, :], raw_wo[g])

                def split_q(g):
                    act.wait_ge(wq_loaded[g], 16)
                    split_hi(wq_sb[:, HI, :, g * REP * HD:(g + 1) * REP * HD], raw_wq[g])

                xt_hi_of(0)
                act.wait_ge(wk_loaded, 16)
                split_hi(wk_sb[:, HI, :, :], raw_wk)
                split_q(0)
                copy_k(0)
                act.wait_ge(wv_loaded, 16)
                split_hi(wv_sb[:, HI, :, :], raw_wv)
                copy_q(0, 0, 0)
                copy_q(0, 0, 1)
                split_q(1)
                exps(0, 0, 0)
                exps(0, 0, 1)
                v_hi_of(0)
                split_q(2)
                copy_q(0, 1, 0)
                copy_q(0, 1, 1)
                split_q(3)
                group(0, True, False)
                with act.Fori(1, NG - 1) as i:
                    group(i, False, False)
                group(NG - 1, False, True)
                copy_x1t(NG - 1)

            @block.vector
            def _(dve):
                def lo_part(out, src, hi):
                    return dve.tensor_tensor(out, src, hi.bitcast(F32), ALU.subtract)

                def stand(n):
                    dve.memset(spare[:, n:n + 1], 0.0)

                def prob_lo(i, g):
                    s = 4 * i + g
                    for b in range(2):
                        dve.wait_ge(pt_hi, 2 * s + b + 1)
                        lo_part(pt_sb[:, LO, 2 * b:2 * b + 2, :].rearrange("p w n -> p (w n)"), po[b][:, :],
                                pt_sb[:, HI, 2 * b:2 * b + 2, :].rearrange("p w n -> p (w n)")).then_inc(pt_lo, 1)

                def maxes(i, g):
                    s = 4 * i + g
                    for b in range(2):
                        dve.wait_ge(s_done, 2 * s + b + 1)
                        need(dve, exp_done, 2 * s + b - 1)
                        if g == 0 and b == 0:
                            dve.wait_ge(mask_set, i + 1)
                        stand(2 * g + b)
                        for t in range(4):
                            n, w = 4 * b + t, 2 * b + t // 2
                            m = mask_first if w == 0 else mask
                            last = dve.tensor_tensor_reduce(
                                out=neg_s[:, n, :], in0=sp[b][:, t * P:(t + 1) * P], in1=m[:, :], scale=-SCALE,
                                scalar=BIG, op0=ALU.add, op1=ALU.min, accum_out=neg_max[:, n:n + 1])
                        last.then_inc(max_done, 1)

                def normalise(i, g):
                    s = 4 * i + g
                    for b in range(2):
                        dve.wait_ge(exp_done, 2 * s + b + 1)
                        dve.reciprocal(row_inv[:, 4 * b:4 * b + 4], row_sum[:, 4 * b:4 * b + 4]).then_inc(inv_done, 1)
                        dve.wait_ge(inv_done, 2 * s + b + 1)
                        tiles = prob[:, 4 * b:4 * b + 4, :]
                        dve.tensor_tensor(tiles, tiles, row_inv[:, 4 * b:4 * b + 4].unsqueeze(2).to_broadcast([P, 4, P]),
                                          ALU.mult).then_inc(prob_ready, 1)

                def out_lo(i, g):
                    s = 4 * i + g
                    for b in range(2):
                        dve.wait_ge(o_hi, 2 * s + b + 1)
                        lo_part(o_sb[:, g % 2, LO, b, :, :].rearrange("p h (w q) -> p w h q", w=2),
                                po[b][:, :].rearrange("p (w h q) -> p w h q", w=2, h=REP),
                                o_sb[:, g % 2, HI, b, :, :].rearrange("p h (w q) -> p w h q", w=2)).then_inc(o_lo, 1)

                def xt_lo_of(i):
                    dve.wait_ge(xt_hi, i + 1)
                    lo_part(xt[:, LO, :, :].rearrange("p c n -> p (c n)"), mp[:, :],
                            xt[:, HI, :, :].rearrange("p c n -> p (c n)")).then_inc(xt_lo, 1)

                def set_mask(i):
                    dve.wait_ge(masks_ready, 1)
                    need(dve, max_done, 8 * i)
                    dve.tensor_copy(mask_first[:, 0:WIN], mask_table[:, i, :] if isinstance(i, int) else
                                    mask_table[:, bass.ds(i, 1), :].rearrange("p a k -> p (a k)")).then_inc(mask_set, 1)

                def carry_k(i):
                    dve.wait_ge(s_done, 8 * i)
                    dve.tensor_copy(kt[:, :, 0:WIN], kt[:, :, GT:]).then_inc(k_carried, 1)

                def carry_v(i):
                    dve.wait_ge(o_done, 8 * i - 1)
                    dve.tensor_copy(v_sb[WIN:P, 0, :, :], v_sb[WIN:P, GW - 1, :, :]).then_inc(v_carried, 1)

                def v_lo_of(i):
                    for t in range(TT):
                        dve.wait_ge(v_hi, 2 * i + t + 1)
                        lo_part(v_sb[:, 2 * t + 1, LO, :], qp[t][:, :], v_sb[:, 2 * t + 1, HI, :]).then_inc(v_lo, 1)
                    dve.wait_ge(v_lo, 2 * i + 2)
                    dve.tensor_copy(v_sb[0:WIN, 0, :, :], v_sb[0:WIN, 1, :, :])
                    dve.tensor_copy(v_sb[0:WIN, 2, :, :], v_sb[0:WIN, 3, :, :])
                    dve.tensor_copy(v_sb[WIN:P, 2, :, :], v_sb[WIN:P, 1, :, :]).then_inc(v_ready, 1)

                def norm_stats(i):
                    dve.wait_ge(wo_done, 4 * i + 4)
                    dve.wait_ge(res_loaded, 16 * (i + 1))
                    dve.tensor_tensor(summed[:, :, :].rearrange("p t d -> p (t d)"), yp[:, :],
                                      x_res[:, :, :].rearrange("p t d -> p (t d)"), ALU.add).then_inc(y_read, 1)
                    dve.wait_ge(y_read, i + 1)
                    for t in range(TT):
                        last = dve.bn_stats(stats[:, t, :], summed[:, t, :])
                    last.then_inc(stats_done, 1)
                    dve.wait_ge(stats_done, i + 1)
                    stand(2 * KV)
                    for t in range(TT):
                        last = dve.bn_aggr(mean_var[:, t, :], stats[:, t, :])
                    last.then_inc(mean_done, 1)
                    dve.wait_ge(mean_done, i + 1)
                    dve.tensor_scalar(var_eps[:, :], mean_var[:, :, 1], EPS, None, ALU.add).then_inc(var_ready, 1)

                def norm_apply(i):
                    dve.wait_ge(rstd_ready, i + 1)
                    need(dve, x1_stored, 16 * i)
                    need(dve, x1t_done, i)
                    for t in range(TT):
                        last = dve.tensor_scalar(x1_cur[:, t, :], summed[:, t, :], mean_var[:, t, 0:1],
                                                 rstd[:, t:t + 1], ALU.subtract, ALU.mult)
                    last.then_inc(x1_ready, 1)

                def copy_logits(i):
                    dve.wait_ge(logit_done, i + 1)
                    dve.tensor_copy(logits[:, bass.ds(i * (TT * E), TT * E)], mp[:, 0:TT * E]).then_inc(logit_copied, 1)

                def group(i, first, last):
                    for g in range(KV):
                        nxt = (i + (g + 1) // KV, (g + 1) % KV)
                        prob_lo(i, g)
                        if not (last and g == 3):
                            maxes(*nxt)
                        if g == 2 and not last:
                            carry_k(i + 1)
                        if g == 1 and not first:
                            norm_stats(i - 1)
                        if not (last and g == 3):
                            normalise(*nxt)
                        if g == 3 and not last:
                            carry_v(i + 1)
                        out_lo(i, g)
                        if g == 1:
                            if not last:
                                xt_lo_of(i + 1)
                            if not first:
                                norm_apply(i - 1)
                        if g == 2 and not last:
                            set_mask(i + 1)
                        if g == 3:
                            if not last:
                                v_lo_of(i + 1)
                            if not first:
                                copy_logits(i - 1)
                        if first:
                            heads = slice(g * REP, (g + 1) * REP)
                            split_lo(wo_sb[:, LO, heads, :], raw_wo[g], wo_sb[:, HI, heads, :], AT_WO[g])

                def split_lo(out, raw, hi, n):
                    dve.wait_ge(w_hi, n)
                    lo_part(out, raw, hi).then_inc(w_lo, 1)

                def split_q(g):
                    cols = slice(g * REP * HD, (g + 1) * REP * HD)
                    split_lo(wq_sb[:, LO, :, cols], raw_wq[g], wq_sb[:, HI, :, cols], AT_WQ[g])

                xt_lo_of(0)
                split_lo(wk_sb[:, LO, :, :], raw_wk, wk_sb[:, HI, :, :], AT_WK)
                split_q(0)
                split_lo(wv_sb[:, LO, :, :], raw_wv, wv_sb[:, HI, :, :], AT_WV)
                set_mask(0)
                split_q(1)
                maxes(0, 0)
                normalise(0, 0)
                v_lo_of(0)
                split_q(2)
                split_q(3)
                group(0, True, False)
                with dve.Fori(1, NG - 1) as i:
                    group(i, False, False)
                group(NG - 1, False, True)
                norm_stats(NG - 1)
                norm_apply(NG - 1)
                copy_logits(NG - 1)


def expert_phase(nc, sem, raw, w_down, x1_dram, out, logits, ident):
    GT2 = 512
    TT2 = GT2 // P
    NG2 = B * T // GT2
    TPB = T // P
    with ExitStack() as ctx:
        def local(name, shape, dt=F32):
            return ctx.enter_context(nc.sbuf_tensor("ffn_" + name, shape, dt))

        def bank(name):
            return ctx.enter_context(nc.psum_tensor("ffn_" + name, [P, 512], F32))

        up_sb = local("up_sb", [P, 2, DC, HPAD], F32R)
        gt_sb = local("gt_sb", [P, 2, DC, HPAD], F32R)
        up_a_sb = local("up_a_sb", [P, 2, DC, ER], F32R)
        gt_a_sb = local("gt_a_sb", [P, 2, DC, ER], F32R)
        up_b_sb = local("up_b_sb", [P, 2, HPAD], F32R)
        gt_b_sb = local("gt_b_sb", [P, 2, HPAD], F32R)
        down_sb = local("down_sb", [P, 2, HC, D], F32R)
        down_a_sb = local("down_a_sb", [P, 2, HC, ER], F32R)
        down_b_sb = local("down_b_sb", [P, 2, D], F32R)
        raw_down = local("raw_down", [P, HC, D])
        raw_up, raw_gt, raw_up_a, raw_gt_a, raw_up_b, raw_gt_b, raw_down_a, raw_down_b = carve(raw, FFN_SHAPES)
        [product_z, c_rows, gated, mixed_sb] = carve(raw, [(4, GT2), (4, GT2), (2, GT2), (1, GT2)])

        x1_in = local("x1_in", [P, TT2, D])
        x1_res = local("x1_res", [P, TT2, D])
        x1t = local("x1t", [P, 2, 2, DC, GT2], F32R)
        z_first = local("z_first", [P, 2, 2, 2, GT2], F32R)
        z_delta = local("z_delta", [P, 2, 2, GT2], F32R)
        mask_rows = local("mask_rows", [P, 2, 2, GT2])
        mask_delta = local("mask_delta", [P, GT2])
        parts = local("parts", [P, 2, 3, 2, GT2], F32R)
        y_masked = local("y_masked", [P, 2, GT2])
        y_parts = local("y_parts", [P, 2, GT2], F32R)
        summed = local("summed", [P, TT2, D])
        stats = local("stats", [P, TT2, 6])
        mean_var = local("mean_var", [P, TT2, 2])
        var_eps = local("var_eps", [P, TT2])
        minus_half = local("minus_half", [P, TT2])
        rstd = local("rstd", [P, TT2])
        spare = local("spare", [P, 1])
        mask_wide = local("mask_wide", [P, 2, TT2, ER], BF16)
        c_wide = local("c_wide", [P, 2, TT2, P])
        ident_bf = local("ident_bf", [P, P], BF16)
        ones = local("ones", [P, P])
        rest = local("rest", [P, NT, E])
        same = local("same", [P, NT, E])
        order = local("order", [P, E])
        chosen = local("chosen", [P, 2, NT, E])
        mask_tok = local("mask_tok", [P, 2, NT, E], BF16)
        top = local("top", [P, 2, NT])
        key = local("key", [P, NT])
        tile_max = local("tile_max", [P, 2 * B])
        seq_max = local("seq_max", [2 * B, 1])
        diag = local("diag", [2 * B, 2 * B])
        tile_sum = local("tile_sum", [P, 2 * B])
        seq_inv = local("seq_inv", [P, 2 * B])
        weight = local("weight", [P, 2, NT])

        pair = [(bank("u0"), bank("g0")), (bank("u1"), bank("g1"))]
        yb = [bank("y0"), bank("y1")]
        ob = [bank("out0"), bank("out1")]

        pad_zero, filled, order_ready, ones_ready, half_ready = (
            sem("pad_zero"), sem("filled2"), sem("order_ready"), sem("ones_ready"), sem("half_ready2"))
        down_loaded, x1_loaded, res_loaded, out_stored = (
            sem("down_loaded"), sem("x1_loaded"), sem("res_loaded2"), sem("out_stored"))
        w_hi, w_lo = sem("w_hi2"), sem("w_lo2")
        route = sem("route")
        max_turned, max_spread, exp_done, sum_spread = (
            sem("max_turned"), sem("max_spread"), sem("exp_done2"), sem("sum_spread"))
        masks_ready, weight_ready = sem("masks_ready2"), sem("weight_ready")
        mask_wide_ready, c_wide_ready = sem("mask_wide_ready"), sem("c_wide_ready")
        x1t_done, x1t_hi, x1t_lo = sem("x1t_done2"), sem("x1t_hi"), sem("x1t_lo")
        mask_done, mask_copied, second_ready = sem("mask_done"), sem("mask_copied"), sem("second_ready")
        c_done, c_copied = sem("c_done"), sem("c_copied")
        z_done, z_masked, z_hi, z_lo = sem("z_done"), sem("z_masked"), sem("z_hi"), sem("z_lo")
        base_done, delta_done, silu_done = sem("base_done"), sem("delta_done"), sem("silu_done")
        gate_done, scale_done, mix_done = sem("gate_done"), sem("scale_done"), sem("mix_done")
        part_hi, part_lo, down_done = sem("part_hi"), sem("part_lo"), sem("down_done")
        y_read, y_hi, y_lo, fold_done = sem("y_read2"), sem("y_hi"), sem("y_lo"), sem("fold_done")
        y_summed, second_diff = sem("y_summed"), sem("second_diff")
        out_read, stats_done, mean_done, var_ready, rstd_ready, norm_done = (
            sem("out_read"), sem("stats_done2"), sem("mean_done2"), sem("var_ready2"), sem("rstd_ready2"),
            sem("norm_done"))

        x1_tiles = x1_dram.rearrange("(n t p) d -> n p t d", t=TT2, p=P)
        out_tiles = out.rearrange("(n t p) d -> n p t d", t=TT2, p=P)

        hid = slice(0, HID)
        last_rows = slice(0, HLAST)
        splits = [
            (lambda a: up_a_sb[:, a, :, :], raw_up_a), (lambda a: gt_a_sb[:, a, :, :], raw_gt_a),
            (lambda a: up_sb[:, a, :, hid], raw_up), (lambda a: gt_sb[:, a, :, hid], raw_gt),
            (lambda a: up_b_sb[:, a, hid], raw_up_b[:, 0, :]), (lambda a: gt_b_sb[:, a, hid], raw_gt_b[:, 0, :]),
            (lambda a: down_a_sb[:, a, 0:HC - 1, :], raw_down_a[:, 0:HC - 1, :]),
            (lambda a: down_a_sb[last_rows, a, HC - 1, :], raw_down_a[last_rows, HC - 1, :]),
            (lambda a: down_b_sb[:, a, :], raw_down_b[:, 0, :]),
            (lambda a: down_sb[:, a, 0:HC - 1, :], raw_down[:, 0:HC - 1, :]),
            (lambda a: down_sb[last_rows, a, HC - 1, :], raw_down[last_rows, HC - 1, :]),
        ]

        pads = [up_sb[:, :, :, HID:], gt_sb[:, :, :, HID:], up_b_sb[:, :, HID:], gt_b_sb[:, :, HID:],
                down_sb[HLAST:P, :, HC - 1, :], down_a_sb[HLAST:P, :, HC - 1, :]]

        def each_group(eng, group):
            group(0, 0)
            group(1, 1)
            with eng.Fori(1, NG2 // 2 - 1) as m:
                group(2 * m, 0)
                group(2 * m + 1, 1)
            group(NG2 - 2, 0)
            group(NG2 - 1, 1)

        with nc.Block() as block:

            @block.sync
            def _(sp_):
                def load_x1(n):
                    need(sp_, x1t_done, n)
                    sp_.dma_start(x1_in[:, :, :], x1_tiles[n]).then_inc(x1_loaded, 16)

                def load_res(n):
                    need(sp_, out_read, n)
                    sp_.dma_start(x1_res[:, :, :], x1_tiles[n]).then_inc(res_loaded, 16)

                def store(n):
                    sp_.wait_ge(norm_done, n + 1)
                    sp_.dma_start(out_tiles[n], summed[:, :, :]).then_inc(out_stored, 16)

                load_x1(0)
                sp_.dma_start(raw_down[:, 0:HC - 1, :],
                              w_down[0:(HC - 1) * P, :].rearrange("(c p) n -> p c n", p=P)).then_inc(down_loaded, 16)
                sp_.dma_start(raw_down[last_rows, HC - 1, :], w_down[(HC - 1) * P:, :]).then_inc(down_loaded, 16)
                load_x1(1)
                load_res(0)
                with sp_.Fori(1, NG2 - 1) as n:
                    load_x1(n + 1)
                    load_res(n)
                    store(n - 1)
                load_res(NG2 - 1)
                store(NG2 - 2)
                store(NG2 - 1)
                sp_.wait_ge(out_stored, 16 * NG2)

            @block.gpsimd
            def _(pool):
                for e in range(E):
                    pool.memset(order[:, e:e + 1], float(E - e)).then_inc(order_ready, 1)
                    pool.wait_ge(order_ready, e + 1)
                pool.memset(ones[:, :], 1.0).then_inc(ones_ready, 1)
                pool.wait_ge(ones_ready, 1)
                pool.tensor_copy(ident_bf[:, :], ident[:, :]).then_inc(ones_ready, 1)
                pool.wait_ge(ones_ready, 2)
                for k, pad in enumerate(pads):
                    pool.memset(pad.bitcast(F32), 0.0).then_inc(pad_zero, 1)
                    pool.wait_ge(pad_zero, k + 1)
                pool.memset(minus_half[:, :], -0.5).then_inc(half_ready, 1)
                pool.wait_ge(half_ready, 1)

                def widen(n):
                    need(pool, mask_done, n)
                    for k in range(2):
                        src = mask_tok[:, k, :, :].rearrange("p t e -> p (t e)")[:, bass.ds(n * (TT2 * E), TT2 * E)]
                        pool.tensor_copy(mask_wide[:, k, :, :].rearrange("p t (e r) -> p (t e) r", r=R),
                                         src.unsqueeze(2).to_broadcast([P, TT2 * E, R])).then_inc(mask_wide_ready, 1)
                    need(pool, c_done, n)
                    if isinstance(n, int) and n == 0:
                        pool.wait_ge(weight_ready, 1)
                    for k in range(2):
                        pool.tensor_copy(c_wide[:, k, :, :],
                                         weight[:, k, bass.ds(n * TT2, TT2)].unsqueeze(2).to_broadcast([P, TT2, P]))\
                            .then_inc(c_wide_ready, 1)

                def rstd_of(n):
                    pool.wait_ge(var_ready, n + 1)
                    need(pool, norm_done, n)
                    pool.tensor_tensor(rstd[:, :], var_eps[:, :], minus_half[:, :], ALU.pow).then_inc(rstd_ready, 1)

                pool.wait_ge(masks_ready, 2)
                widen(0)
                widen(1)
                with pool.Fori(2, NG2) as n:
                    widen(n)
                    rstd_of(n - 2)
                rstd_of(NG2 - 2)
                rstd_of(NG2 - 1)

            @block.tensor
            def _(pe):
                def turn_x1(n, p):
                    pe.wait_ge(x1_loaded, 16 * (n + 1))
                    for c in range(DC):
                        for t in range(TT2):
                            last = pe.transpose(pair[1][c][:, t * P:(t + 1) * P], x1_in[:, t, c * P:(c + 1) * P], ident[:, :])
                    last.then_inc(x1t_done, 1)

                def turn_masks(n, p):
                    pe.wait_ge(mask_wide_ready, 2 * n + 2)
                    for k in range(2):
                        for t in range(TT2):
                            last = pe.matmul(pair[0][k][:, t * P:(t + 1) * P], mask_wide[:, k, t, :], ident_bf[:, :],
                                             start=True, stop=True)
                    last.then_inc(mask_done, 1)

                def turn_weights(n, p):
                    pe.wait_ge(c_wide_ready, 2 * n + 2)
                    for k in range(2):
                        for t in range(TT2):
                            last = pe.transpose(pair[1][k][:, t * P:(t + 1) * P], c_wide[:, k, t, :], ident[:, :])
                    last.then_inc(c_done, 1)

                def low_rank_in(n, p):
                    pe.wait_ge(x1t_lo, 2 * n + 2)
                    for k, w in enumerate((up_a_sb, gt_a_sb)):
                        last = product(pe, pair[0][k][:, :], lambda a, c: w[:, a, c, :],
                                       lambda a, c: x1t[:, p, a, c, :], range(DC))
                    last.then_inc(z_done, 1)

                def base(n, p, j):
                    u = HC * n + j
                    need(pe, gate_done, 2 * u - 2)
                    if j == 0:
                        pe.wait_ge(z_masked, 4 * n + 4)
                        pe.wait_ge(x1t_lo, 2 * n + 2)
                    else:
                        slot = [None, (x1t_lo, 2), (mask_copied, 2), (c_copied, 2)]
                        if j < len(slot):
                            s_, per = slot[j]
                            pe.wait_ge(s_, per * n + per if n_is_last(n) else per * n + 2 * per)
                    cols = slice(j * P, (j + 1) * P)
                    for k, (w, wb) in enumerate(((up_sb, up_b_sb), (gt_sb, gt_b_sb))):
                        product(pe, pair[j % 2][k][:, :], lambda a, c: w[:, a, c, cols],
                                lambda a, c: x1t[:, p, a, c, :], range(DC), stop=False)
                        if j == 0:
                            pe.wait_ge(z_lo, 4 * n + k + 1)
                        last = product(pe, pair[j % 2][k][:, :], lambda a, c: wb[:, a, cols],
                                       lambda a, c: z_first[:, p, k, a, :], (0,), start=False)
                    last.then_inc(base_done, 1)

                def n_is_last(n):
                    return isinstance(n, int) and n == NG2 - 1

                def delta(n, j):
                    u = HC * n + j
                    pe.wait_ge(gate_done, 2 * u + 1)
                    cols = slice(j * P, (j + 1) * P)
                    for k, wb in enumerate((up_b_sb, gt_b_sb)):
                        if j == 0:
                            pe.wait_ge(z_lo, 4 * n + 3 + k)
                        last = product(pe, pair[j % 2][k][:, :], lambda a, c: wb[:, a, cols],
                                       lambda a, c: z_delta[:, k, a, :], (0,), start=False)
                    last.then_inc(delta_done, 1)

                def down_low_rank(n, j):
                    u = HC * n + j
                    if j == 0:
                        need(pe, y_read, 2 * n)
                    for k in range(2):
                        pe.wait_ge(part_lo, 3 * u + k + 1)
                        product(pe, yb[k][:, :], lambda a, c: down_a_sb[:, a, j, :],
                                lambda a, c: parts[:, j % 2, k, a, :], (0,), start=(j == 0), stop=(j == HC - 1))

                def down(n, j):
                    u = HC * n + j
                    if j == 0:
                        need(pe, out_read, n)
                    pe.wait_ge(part_lo, 3 * u + 3)
                    for t in range(TT2):
                        last = product(pe, ob[t // 2][:, (t % 2) * D:(t % 2 + 1) * D],
                                       lambda a, c: parts[:, j % 2, 2, a, t * P:(t + 1) * P],
                                       lambda a, c: down_sb[:, a, j, :], (0,), start=(j == 0 and t % 2 == 0), stop=False)
                    last.then_inc(down_done, 1)

                def fold(n):
                    pe.wait_ge(y_lo, n + 1)
                    for t in range(TT2):
                        last = product(pe, ob[t // 2][:, (t % 2) * D:(t % 2 + 1) * D],
                                       lambda a, c: y_parts[:, a, t * P:(t + 1) * P],
                                       lambda a, c: down_b_sb[:, a, :], (0,), start=False)
                    last.then_inc(fold_done, 1)

                def group(n, p):
                    first = isinstance(n, int) and n == 0
                    last = n_is_last(n)
                    for j in range(HC):
                        u = HC * n + j
                        base(n, p, j)
                        if not last:
                            turn = {0: turn_x1, 1: turn_masks, 2: turn_weights, 5: low_rank_in}.get(j)
                            if turn:
                                need(pe, gate_done, 2 * u)
                                turn(n + 1, 1 - p)
                        if j > 0 or not first:
                            before = (n, j - 1) if j > 0 else (n - 1, HC - 1)
                            down_low_rank(*before)
                            if j == 1:
                                if not first:
                                    fold(n - 1)
                                delta(n, j)
                            down(*before)
                        if j != 1:
                            delta(n, j)

                pe.wait_ge(ones_ready, 2)
                turn_x1(0, 0)
                pe.wait_ge(route, 12)
                pe.transpose(ob[0][0:2 * B, 0:P], tile_max[:, :], ident[:, :]).then_inc(max_turned, 1)
                pe.wait_ge(route, 14)
                pe.matmul(ob[0][:, 128:128 + 2 * B], ones[0:2 * B, :], diag[:, :], start=True, stop=True).then_inc(max_spread, 1)
                turn_masks(0, 0)
                pe.wait_ge(route, 16)
                pe.matmul(ob[1][:, 0:2 * B], ones[:, :], tile_sum[:, :], start=True, stop=True).then_inc(sum_spread, 1)
                pe.wait_ge(w_lo, 2)
                pe.wait_ge(mask_copied, 2)
                low_rank_in(0, 0)
                turn_weights(0, 0)
                pe.wait_ge(w_lo, len(splits))
                pe.wait_ge(pad_zero, len(pads))
                pe.wait_ge(c_copied, 2)
                each_group(pe, group)
                down_low_rank(NG2 - 1, HC - 1)
                down(NG2 - 1, HC - 1)
                fold(NG2 - 1)

            @block.scalar
            def _(act):
                def turned_hi(n, p):
                    for c in range(DC):
                        act.wait_ge(x1t_done, n + 1)
                        act.activation(x1t[:, p, HI, c, :], pair[1][c][:, :], ACT.Copy).then_inc(x1t_hi, 1)

                def copy_masks(n, p):
                    act.wait_ge(mask_done, n + 1)
                    need(act, y_read, 2 * n - 2)
                    act.activation(mask_rows[:, p, 0, :], pair[0][0][:, :], ACT.Copy).then_inc(mask_copied, 1)
                    need(act, z_masked, 4 * n)
                    act.activation(mask_delta[:, :], pair[0][1][:, :], ACT.Copy).then_inc(mask_copied, 1)

                def copy_weights(n, p):
                    act.wait_ge(c_done, n + 1)
                    for k in range(2):
                        act.activation(c_rows[:, 2 * p + k, :], pair[1][k][:, :], ACT.Copy).then_inc(c_copied, 1)

                def z_hi_of(n, p, which):
                    for k in range(2):
                        act.wait_ge(z_masked, 4 * n + 2 * which + k + 1)
                        if which == 0:
                            out_ = z_first[:, p, k, HI, :]
                        else:
                            need(act, delta_done, HC * n)
                            out_ = z_delta[:, k, HI, :]
                        act.activation(out_, product_z[:, 2 * which + k, :], ACT.Copy).then_inc(z_hi, 1)

                def silu(n, j, k):
                    u = HC * n + j
                    if k == 0:
                        act.wait_ge(base_done, u + 1)
                        need(act, mix_done, u)
                        need(act, part_lo, 3 * u - 2)
                    else:
                        act.wait_ge(delta_done, u + 1)
                        need(act, part_lo, 3 * u - 1)
                    act.activation(gated[:, k, :], pair[j % 2][0][:, :], ACT.Silu).then_inc(silu_done, 1)

                def part_hi_of(n, j, k):
                    u = HC * n + j
                    if k < 2:
                        act.wait_ge(scale_done, 2 * u + k + 1)
                    else:
                        act.wait_ge(mix_done, u + 1)
                    need(act, down_done, u - 1)
                    act.activation(parts[:, j % 2, k, HI, :], gated[:, k, :] if k < 2 else mixed_sb[:, 0, :],
                                   ACT.Copy).then_inc(part_hi, 1)

                def y_hi_of(n):
                    act.wait_ge(y_summed, n + 1)
                    need(act, fold_done, n)
                    act.activation(y_parts[:, HI, :], y_masked[:, 0, :], ACT.Copy).then_inc(y_hi, 1)

                def group(n, p):
                    first = isinstance(n, int) and n == 0
                    last = isinstance(n, int) and n == NG2 - 1
                    for j in range(HC):
                        silu(n, j, 0)
                        if not last:
                            turn = {0: turned_hi, 1: copy_masks, 2: copy_weights}.get(j)
                            if turn:
                                turn(n + 1, 1 - p)
                        part_hi_of(n, j, 0)
                        if j == 0 and not first:
                            y_hi_of(n - 1)
                        if j == HC - 1 and not last:
                            z_hi_of(n + 1, 1 - p, 0)
                        silu(n, j, 1)
                        part_hi_of(n, j, 1)
                        part_hi_of(n, j, 2)
                        if j == HC - 1 and not last:
                            z_hi_of(n + 1, 1 - p, 1)

                for k, (out_, raw_) in enumerate(splits):
                    if k == 2:
                        turned_hi(0, 0)
                    if k == 3:
                        act.wait_ge(route, 15)
                        act.activation(top[:, :, :], top[:, :, :], ACT.Exp).then_inc(exp_done, 1)
                    if k == 9:
                        act.wait_ge(down_loaded, 32)
                    act.activation(out_(HI), raw_, ACT.Copy).then_inc(w_hi, 1)
                act.wait_ge(w_lo, len(splits))
                copy_masks(0, 0)
                z_hi_of(0, 0, 0)
                z_hi_of(0, 0, 1)
                copy_weights(0, 0)
                each_group(act, group)
                y_hi_of(NG2 - 1)

            @block.vector
            def _(dve):
                def lo_part(out_, src, hi):
                    return dve.tensor_tensor(out_, src, hi.bitcast(F32), ALU.subtract)

                def turned_lo(n, p):
                    for c in range(DC):
                        dve.wait_ge(x1t_hi, 2 * n + c + 1)
                        lo_part(x1t[:, p, LO, c, :], pair[1][c][:, :], x1t[:, p, HI, c, :]).then_inc(x1t_lo, 1)

                def second_mask(n, p):
                    dve.wait_ge(mask_copied, 2 * n + 2)
                    dve.tensor_tensor(mask_rows[:, p, 1, :], mask_rows[:, p, 0, :], mask_delta[:, :],
                                      ALU.add).then_inc(second_ready, 1)

                def mask_z(n, p):
                    dve.wait_ge(z_done, n + 1)
                    need(dve, z_lo, 4 * n)
                    for which in range(2):
                        m = mask_rows[:, p, 0, :] if which == 0 else mask_delta[:, :]
                        for k in range(2):
                            dve.tensor_tensor(product_z[:, 2 * which + k, :], pair[0][k][:, :], m,
                                              ALU.mult).then_inc(z_masked, 1)

                def z_lo_of(n, p, which):
                    for k in range(2):
                        dve.wait_ge(z_hi, 4 * n + 2 * which + k + 1)
                        both = z_first[:, p, k, :, :] if which == 0 else z_delta[:, k, :, :]
                        lo_part(both[:, LO, :], product_z[:, 2 * which + k, :], both[:, HI, :]).then_inc(z_lo, 1)

                def gate(n, j, k):
                    u = HC * n + j
                    dve.wait_ge(silu_done, 2 * u + k + 1)
                    dve.tensor_tensor(gated[:, k, :], gated[:, k, :], pair[j % 2][1][:, :], ALU.mult).then_inc(gate_done, 1)

                def scale(n, p, j, k):
                    u = HC * n + j
                    dve.wait_ge(gate_done, 2 * u + k + 1)
                    if j == 0:
                        dve.wait_ge(c_copied, 2 * n + 2)
                    dve.tensor_tensor(gated[:, k, :], gated[:, k, :], c_rows[:, 2 * p + k, :], ALU.mult).then_inc(scale_done, 1)

                def mix(n, j):
                    u = HC * n + j
                    dve.wait_ge(scale_done, 2 * u + 2)
                    need(dve, part_hi, 3 * u)
                    need(dve, part_lo, 3 * u)
                    dve.tensor_tensor(mixed_sb[:, 0, :], gated[:, 0, :], gated[:, 1, :], ALU.add).then_inc(mix_done, 1)

                def part_lo_of(n, j, k):
                    u = HC * n + j
                    dve.wait_ge(part_hi, 3 * u + k + 1)
                    lo_part(parts[:, j % 2, k, LO, :], gated[:, k, :] if k < 2 else mixed_sb[:, 0, :],
                            parts[:, j % 2, k, HI, :]).then_inc(part_lo, 1)

                def mask_y(n, p):
                    dve.wait_ge(down_done, HC * n + HC)
                    need(dve, y_lo, n)
                    for k in range(2):
                        dve.tensor_tensor(y_masked[:, k, :], yb[k][:, :], mask_rows[:, p, k, :], ALU.mult).then_inc(y_read, 1)
                    dve.wait_ge(y_read, 2 * n + 2)
                    dve.tensor_tensor(y_masked[:, 0, :], y_masked[:, 0, :], y_masked[:, 1, :], ALU.add).then_inc(y_summed, 1)

                def y_lo_of(n):
                    dve.wait_ge(y_hi, n + 1)
                    lo_part(y_parts[:, LO, :], y_masked[:, 0, :], y_parts[:, HI, :]).then_inc(y_lo, 1)

                def add_out(n):
                    dve.wait_ge(fold_done, n + 1)
                    dve.wait_ge(res_loaded, 16 * (n + 1))
                    need(dve, out_stored, 16 * n)
                    for h in range(2):
                        last = dve.tensor_tensor(summed[:, 2 * h:2 * h + 2, :].rearrange("p t d -> p (t d)"), ob[h][:, :],
                                                 x1_res[:, 2 * h:2 * h + 2, :].rearrange("p t d -> p (t d)"), ALU.add)
                    last.then_inc(out_read, 1)

                def norm_stats(n):
                    dve.wait_ge(out_read, n + 1)
                    for t in range(TT2):
                        last = dve.bn_stats(stats[:, t, :], summed[:, t, :])
                    last.then_inc(stats_done, 1)
                    dve.wait_ge(stats_done, n + 1)
                    dve.memset(spare[:, :], 0.0)
                    for t in range(TT2):
                        last = dve.bn_aggr(mean_var[:, t, :], stats[:, t, :])
                    last.then_inc(mean_done, 1)
                    dve.wait_ge(mean_done, n + 1)
                    dve.tensor_scalar(var_eps[:, :], mean_var[:, :, 1], EPS, None, ALU.add).then_inc(var_ready, 1)

                def norm_apply(n):
                    dve.wait_ge(rstd_ready, n + 1)
                    for t in range(TT2):
                        last = dve.tensor_scalar(summed[:, t, :], summed[:, t, :], mean_var[:, t, 0:1],
                                                 rstd[:, t:t + 1], ALU.subtract, ALU.mult)
                    last.then_inc(norm_done, 1)

                def group(n, p):
                    first = isinstance(n, int) and n == 0
                    last = isinstance(n, int) and n == NG2 - 1
                    for j in range(HC):
                        gate(n, j, 0)
                        scale(n, p, j, 0)
                        if not last and j == 0:
                            turned_lo(n + 1, 1 - p)
                        if not last and j == 1:
                            second_mask(n + 1, 1 - p)
                        if j == 1 and not first:
                            add_out(n - 1)
                        part_lo_of(n, j, 0)
                        if j == 0 and not first:
                            mask_y(n - 1, 1 - p)
                        if j == HC - 1 and not last:
                            mask_z(n + 1, 1 - p)
                            z_lo_of(n + 1, 1 - p, 0)
                        gate(n, j, 1)
                        if j == 0 and not first:
                            y_lo_of(n - 1)
                        scale(n, p, j, 1)
                        mix(n, j)
                        part_lo_of(n, j, 1)
                        part_lo_of(n, j, 2)
                        if j == 1 and not first:
                            norm_stats(n - 1)
                        if j == 2 and not first:
                            norm_apply(n - 1)
                        if j == HC - 1 and not last:
                            z_lo_of(n + 1, 1 - p, 1)

                step = [0]

                def routed(instruction):
                    step[0] += 1
                    instruction.then_inc(route, 1)
                    dve.wait_ge(route, step[0])

                def wide(per_tile):
                    return per_tile.unsqueeze(2).to_broadcast([P, NT, E])

                dve.wait_ge(order_ready, E)
                every = logits[:, :].rearrange("p (t e) -> p t e", e=E)
                orders = order[:, :].unsqueeze(1).to_broadcast([P, NT, E])
                for k, values in enumerate((every, rest[:, :, :])):
                    if k == 1:
                        routed(dve.scalar_tensor_tensor(out=rest[:, :, :], in0=chosen[:, 0, :, :], scalar=-BIG, in1=every,
                                                        op0=ALU.mult, op1=ALU.add))
                    routed(dve.tensor_reduce(top[:, k, :], values, AX.X, ALU.max))
                    routed(dve.tensor_tensor(same[:, :, :], values, wide(top[:, k, :]), ALU.is_equal))
                    routed(dve.tensor_tensor(same[:, :, :], same[:, :, :], orders, ALU.mult))
                    routed(dve.tensor_reduce(key[:, :], same[:, :, :], AX.X, ALU.max))
                    routed(dve.tensor_tensor(chosen[:, k, :, :], same[:, :, :], wide(key[:, :]), ALU.is_equal))
                by_seq = top[:, :, :].rearrange("p k (b t) -> p (k b) t", t=TPB)
                routed(dve.tensor_reduce(tile_max[:, :], by_seq, AX.X, ALU.max))
                dve.tensor_scalar(mask_tok[:, 0, :, :], chosen[:, 0, :, :], 2.0, None, ALU.mult).then_inc(masks_ready, 1)
                dve.tensor_tensor(rest[:, :, :], chosen[:, 1, :, :], chosen[:, 0, :, :], ALU.subtract).then_inc(second_diff, 1)
                dve.wait_ge(second_diff, 1)
                dve.tensor_scalar(mask_tok[:, 1, :, :], rest[:, :, :], 2.0, None, ALU.mult).then_inc(masks_ready, 1)
                dve.wait_ge(max_turned, 1)
                routed(dve.tensor_reduce(seq_max[:, :], ob[0][0:2 * B, 0:P], AX.X, ALU.max))
                routed(dve.tensor_scalar(diag[:, :], ident[0:2 * B, 0:2 * B], seq_max[:, 0:1], None, ALU.mult))
                dve.wait_ge(max_spread, 1)
                routed(dve.tensor_tensor(by_seq, by_seq, ob[0][:, 128:128 + 2 * B].unsqueeze(2).to_broadcast([P, 2 * B, TPB]),
                                         ALU.subtract))
                for k, (out_, raw_) in enumerate(splits):
                    if k == 2:
                        turned_lo(0, 0)
                    if k == 3:
                        dve.wait_ge(exp_done, 1)
                        routed(dve.tensor_reduce(tile_sum[:, :], by_seq, AX.X, ALU.add))
                    if k == 6:
                        dve.wait_ge(sum_spread, 1)
                        routed(dve.reciprocal(seq_inv[:, :], ob[1][:, 0:2 * B]))
                        dve.tensor_tensor(weight[:, :, :].rearrange("p k (b t) -> p (k b) t", t=TPB), by_seq,
                                          seq_inv[:, :].unsqueeze(2).to_broadcast([P, 2 * B, TPB]), ALU.mult).then_inc(weight_ready, 1)
                    dve.wait_ge(w_hi, k + 1)
                    lo_part(out_(LO), raw_, out_(HI)).then_inc(w_lo, 1)
                second_mask(0, 0)
                dve.wait_ge(w_lo, len(splits))
                mask_z(0, 0)
                z_lo_of(0, 0, 0)
                z_lo_of(0, 0, 1)
                each_group(dve, group)
                mask_y(NG2 - 1, 1)
                y_lo_of(NG2 - 1)
                add_out(NG2 - 1)
                norm_stats(NG2 - 1)
                norm_apply(NG2 - 1)


def build(nc, x, wq, wk, wv, wo, gate_wt, w_up, w_gate, w_down, up_a, up_b, gate_a, gate_b, down_a, down_b, out):
    x1_dram = nc.dram_tensor("x1_dram", [B * T, D], F32, kind="Internal").ap()
    with ExitStack() as ctx:
        def sem(name):
            return ctx.enter_context(nc.semaphore(name))

        ident = ctx.enter_context(nc.sbuf_tensor("ident", [P, P], F32))
        logits = ctx.enter_context(nc.sbuf_tensor("logits", [P, NT * E], F32))
        raw = ctx.enter_context(nc.sbuf_tensor("raw", [P, RAW], F32))
        ffn_loaded = sem("ffn_loaded")

        def by_rows(w):
            return w.rearrange("(c p) n -> p c n", p=P)

        whole = (HC - 1) * P
        r_up, r_gate, r_up_a, r_gate_a, r_up_b, r_gate_b, r_down_a, r_down_b = carve(raw, FFN_SHAPES)
        ffn_loads = [
            (r_up, by_rows(w_up)), (r_gate, by_rows(w_gate)), (r_up_a, by_rows(up_a)), (r_gate_a, by_rows(gate_a)),
            (r_up_b[:, 0, :], up_b), (r_gate_b[:, 0, :], gate_b), (r_down_b[:, 0, :], down_b),
            (r_down_a[:, 0:HC - 1, :], by_rows(down_a[0:whole, :])), (r_down_a[0:HLAST, HC - 1, :], down_a[whole:, :]),
        ]
        attention_phase(nc, sem, raw, x, wq, wk, wv, wo, gate_wt, ffn_loads, x1_dram, logits, ident, ffn_loaded)
        expert_phase(nc, sem, raw, w_down, x1_dram, out, logits, ident)


def kernel(**inputs):
    import numpy as np
    import concourse.bacc as bacc
    from concourse.bass_utils import run_bass_kernel_spmd

    def put(name):
        return np.asarray(inputs[name])

    def rows_first(a):
        return a.transpose(0, 2, 1).reshape(ER, a.shape[1])

    arrays = {
        "x": put("L0_attn_x").reshape(B * T, D),
        "wq": put("L0_attn_Wq"), "wk": put("L0_attn_Wk"), "wv": put("L0_attn_Wv"), "wo": put("L0_attn_Wo"),
        "gate_wt": put("L0_ffn_gate_w").T,
        "w_up": put("L0_ffn_w_up").T, "w_gate": put("L0_ffn_w_gate").T, "w_down": put("L0_ffn_w_down").T,
        "up_a": put("L0_ffn_up_A").reshape(ER, D).T, "up_b": rows_first(put("L0_ffn_up_B")),
        "gate_a": put("L0_ffn_gate_A").reshape(ER, D).T, "gate_b": rows_first(put("L0_ffn_gate_B")),
        "down_a": put("L0_ffn_down_A").reshape(ER, HID).T, "down_b": rows_first(put("L0_ffn_down_B")),
    }
    arrays = {name: np.ascontiguousarray(a) for name, a in arrays.items()}
    nc = bacc.Bacc("TRN2", target_bir_lowering=False, num_devices=1)
    args = [nc.dram_tensor(name, a.shape, F32, kind="ExternalInput").ap() for name, a in arrays.items()]
    out = nc.dram_tensor("out", [B * T, D], F32, kind="ExternalOutput").ap()
    build(nc, *args, out)
    result = run_bass_kernel_spmd(nc, [arrays], core_ids=[0])
    return np.asarray(result.results[0]["out"]).reshape(B, T, D)
```

```python
from contextlib import ExitStack

import concourse.bass as bass
from concourse import mybir

F32 = mybir.dt.float32
F32R = mybir.dt.float32r
BF16 = mybir.dt.bfloat16
ALU = mybir.AluOpType
ACT = mybir.ActivationFunctionType
AX = mybir.AxisListType

P = 128
D = 256
DC = D // P
B, T = 4, 1024
HEADS, KV, HD, WIN = 16, 4, 128, 64
REP = HEADS // KV
GT = 256
GW = GT // WIN
NG = B * T // GT
GPB = T // GT
TT = GT // P
NT = B * T // P
E, R, HID = 8, 16, 704
HC = -(-HID // P)
HPAD = HC * P
WHOLE = (HC - 1) * P
HLAST = HID - WHOLE
assert 2 * HLAST == P
ER = E * R
FFN_SHAPES = [(DC, HID), (DC, HID), (DC, ER), (DC, ER), (1, HID), (1, HID), (HC, ER), (1, D)]
RQ = DC * REP * HD
RAW = max(DC * (HEADS + 2 * KV) * HD, sum(a * b for a, b in FFN_SHAPES))
SCALE = float(HD) ** -0.5
NEG = -1e30
BIG = 3e38
EPS = 1e-5
HI, LO = 0, 1
PARTS = ((HI, HI), (HI, LO), (LO, HI))


def need(eng, sem, count):
    if isinstance(count, int) and count <= 0:
        return
    eng.wait_ge(sem, count)


def carve(buffer, shapes):
    views, at = [], 0
    for a, b in shapes:
        views.append(buffer[:, at:at + a * b].rearrange("p (a b) -> p a b", a=a))
        at += a * b
    return views


def product(eng, out, stationary, moving, chunks, start=True, stop=True):
    last = None
    n = len(chunks) * len(PARTS)
    for k, c in enumerate(chunks):
        for j, (a, b) in enumerate(PARTS):
            m = k * len(PARTS) + j
            last = eng.matmul(out, stationary(a, c), moving(b, c), start=start and m == 0,
                              stop=stop and m == n - 1, skip_group_check=True)
    return last


def attention_phase(nc, sem, raw, x, wq, wk, wv, wo, gate_wt, ffn_loads, x1_dram, logits, ident, ffn_loaded):
    with ExitStack() as ctx:
        def local(name, shape, dt=F32):
            return ctx.enter_context(nc.sbuf_tensor("attn_" + name, shape, dt))

        def bank(name):
            return ctx.enter_context(nc.psum_tensor("attn_" + name, [P, 512], F32))

        raw_wq = [carve(raw[:, g * RQ:], [(DC, REP * HD)])[0] for g in range(KV)]
        raw_wo = [carve(raw[:, g * RQ:], [(REP, D)])[0] for g in range(KV)]
        raw_wk, raw_wv = carve(raw[:, KV * RQ:], [(DC, KV * HD), (DC, KV * HD)])
        wq_sb = local("wq_sb", [P, 2, DC, HEADS * HD], F32R)
        wk_sb = local("wk_sb", [P, 2, DC, KV * HD], F32R)
        wv_sb = local("wv_sb", [P, 2, DC, KV * HD], F32R)
        wo_sb = local("wo_sb", [P, 2, HEADS, D], F32R)
        gate_sb = local("gate_sb", [P, DC, E])

        x_in = local("x_in", [P, TT, D])
        x_res = local("x_res", [P, TT, D])
        xt = local("xt", [P, 2, DC, GT], F32R)
        kt = local("kt", [P, KV, WIN + GT])
        v_sb = local("v_sb", [P, GW, 2, KV * HD], F32R)
        q_sb = local("q_sb", [P, GW, REP, WIN])
        neg_s = local("neg_s", [P, 2 * GW, P])
        neg_max = local("neg_max", [P, 2 * GW])
        row_sum = local("row_sum", [P, 2 * GW])
        spare = local("spare", [P, 2 * KV + 1])
        row_inv = local("row_inv", [P, 2 * GW])
        prob = local("prob", [P, 2 * GW, P])
        pt_sb = local("pt_sb", [P, 2, GW, REP * WIN], F32R)
        o_sb = local("o_sb", [P, 2, 2, TT, REP, P], F32R)
        summed = local("summed", [P, TT, D])
        stats = local("stats", [P, TT, 6])
        mean_var = local("mean_var", [P, TT, 2])
        var_eps = local("var_eps", [P, TT])
        minus_half = local("minus_half", [P, TT])
        rstd = local("rstd", [P, TT])
        x1_cur = local("x1_cur", [P, TT, D])
        x1t = local("x1t", [P, DC, GT])
        mask = local("mask", [P, P])
        mask_first = local("mask_first", [P, P])
        mask_table = local("mask_table", [P, NG, WIN])

        qp = [bank("qp0"), bank("qp1")]
        sp = [bank("sp0"), bank("sp1")]
        po = [bank("po0"), bank("po1")]
        yp = bank("yp")
        mp = bank("mp")

        x_loaded, res_loaded = sem("x_loaded"), sem("res_loaded")
        wk_loaded, wv_loaded, gate_loaded, x1_stored = (
            sem("wk_loaded"), sem("wv_loaded"), sem("gate_loaded"), sem("x1_stored"))
        wq_loaded = [sem(f"wq_loaded{g}") for g in range(KV)]
        wo_loaded = [sem(f"wo_loaded{g}") for g in range(KV)]
        AT_WK, AT_WQ, AT_WV, AT_WO = 1, (2, 4, 5, 6), 3, (7, 8, 9, 10)
        w_hi, w_lo = sem("w_hi"), sem("w_lo")
        ident_ready, masks_ready, filled = sem("ident_ready"), sem("masks_ready"), sem("filled")
        carry_zero = sem("carry_zero")
        half_ready = sem("half_ready")
        xt_done, xt_hi, xt_lo = sem("xt_done"), sem("xt_hi"), sem("xt_lo")
        q_done, q_copied = sem("q_done"), sem("q_copied")
        k_done, k_copied, k_carried = sem("k_done"), sem("k_copied"), sem("k_carried")
        v_done, v_hi, v_lo, v_carried, v_ready = (sem("v_done"), sem("v_hi"), sem("v_lo"),
                                                  sem("v_carried"), sem("v_ready"))
        s_done, max_done, exp_done = sem("s_done"), sem("max_done"), sem("exp_done")
        inv_done, prob_ready = sem("inv_done"), sem("prob_ready")
        pt_done, pt_hi, pt_lo = sem("pt_done"), sem("pt_hi"), sem("pt_lo")
        o_done, o_hi, o_lo = sem("o_done"), sem("o_hi"), sem("o_lo")
        wo_done, y_read = sem("wo_done"), sem("y_read")
        stats_done, mean_done, var_ready, rstd_ready, x1_ready = (
            sem("stats_done"), sem("mean_done"), sem("var_ready"), sem("rstd_ready"), sem("x1_ready"))
        x1t_done, x1t_copied, logit_done, logit_copied = (
            sem("x1t_done"), sem("x1t_copied"), sem("logit_done"), sem("logit_copied"))
        mask_set = sem("mask_set")

        x_tiles = x.rearrange("(n t p) d -> n p t d", t=TT, p=P)
        x1_tiles = x1_dram.rearrange("(n t p) d -> n p t d", t=TT, p=P)

        with nc.Block() as block:

            @block.sync
            def _(sp_):
                def load_x(i):
                    need(sp_, xt_done, i)
                    sp_.dma_start(x_in[:, :, :], x_tiles[i]).then_inc(x_loaded, 16)

                def load_res(i):
                    need(sp_, y_read, i)
                    sp_.dma_start(x_res[:, :, :], x_tiles[i]).then_inc(res_loaded, 16)

                def store_x1(i):
                    sp_.wait_ge(x1_ready, i + 1)
                    sp_.dma_start(x1_tiles[i], x1_cur[:, :, :]).then_inc(x1_stored, 16)

                load_x(0)
                sp_.dma_start(raw_wk, wk.rearrange("(c p) n -> p c n", p=P)).then_inc(wk_loaded, 16)
                wq_rows = wq.rearrange("(c p) n -> p c n", p=P)
                wo_rows = wo.rearrange("(h p) n -> p h n", p=P)
                for g in range(KV):
                    sp_.dma_start(raw_wq[g], wq_rows[:, :, g * REP * HD:(g + 1) * REP * HD]).then_inc(wq_loaded[g], 16)
                    if g == 0:
                        sp_.dma_start(raw_wv, wv.rearrange("(c p) n -> p c n", p=P)).then_inc(wv_loaded, 16)
                sp_.dma_start(gate_sb[:, :, :], gate_wt.rearrange("(c p) n -> p c n", p=P)).then_inc(gate_loaded, 16)
                load_x(1)
                for g in range(KV):
                    sp_.wait_ge(w_lo, AT_WQ[g])
                    sp_.dma_start(raw_wo[g], wo_rows[:, g * REP:(g + 1) * REP, :]).then_inc(wo_loaded[g], 16)
                load_x(2)
                load_res(0)
                sp_.wait_ge(w_lo, AT_WO[-1])
                for out, src in ffn_loads:
                    sp_.dma_start(out, src).then_inc(ffn_loaded, 16)
                with sp_.Fori(1, NG - 2) as i:
                    load_x(i + 2)
                    load_res(i)
                    store_x1(i - 1)
                for i in (NG - 2, NG - 1):
                    load_res(i)
                    store_x1(i - 1)
                store_x1(NG - 1)
                sp_.wait_ge(x1_stored, 16 * NG)
                sp_.wait_ge(ffn_loaded, 16 * len(ffn_loads))

            @block.gpsimd
            def _(pool):
                def then_wait(instruction, count):
                    instruction.then_inc(filled, 1)
                    pool.wait_ge(filled, count)

                then_wait(pool.memset(ident[:, :], 0.0), 1)
                pool.affine_select(out=ident[:, :], in_=ident[:, :], compare_op=ALU.not_equal, fill=1.0,
                                   base=0, pattern=[[-1, P]], channel_multiplier=1).then_inc(ident_ready, 1)
                pool.wait_ge(ident_ready, 1)
                then_wait(pool.memset(mask[:, :], 0.0), 2)
                then_wait(pool.memset(mask_first[:, :], 0.0), 3)
                then_wait(pool.memset(mask_table[:, :, :], 0.0), 4)
                n = 4
                for half in range(2):
                    rows = slice(half * WIN, (half + 1) * WIN)
                    n += 1
                    then_wait(pool.affine_select(
                        out=mask[rows, 0:WIN], in_=mask[rows, 0:WIN], compare_op=ALU.is_gt, fill=NEG, base=0,
                        pattern=[[1, WIN]], channel_multiplier=-1), n)
                    for m in (mask, mask_first):
                        n += 1
                        then_wait(pool.affine_select(
                            out=m[rows, WIN:P], in_=m[rows, WIN:P], compare_op=ALU.is_ge, fill=NEG, base=0,
                            pattern=[[-1, WIN]], channel_multiplier=1), n)
                    table = mask_table[rows, :, :]
                    n += 1
                    then_wait(pool.affine_select(
                        out=table, in_=table, compare_op=ALU.is_gt, fill=NEG, base=0,
                        pattern=[[0, NG], [1, WIN]], channel_multiplier=-1), n)
                first = mask_table[:, :, :].rearrange("p (b g) k -> p b g k", b=B)[:, :, 0, :]
                pool.memset(first, NEG).then_inc(masks_ready, 1)
                pool.wait_ge(masks_ready, 1)
                pool.memset(kt[:, :, 0:WIN], 0.0).then_inc(carry_zero, 1)
                pool.wait_ge(carry_zero, 1)
                pool.memset(v_sb[WIN:P, 0, :, :].bitcast(F32), 0.0).then_inc(carry_zero, 1)
                pool.wait_ge(carry_zero, 2)
                pool.memset(minus_half[:, :], -0.5).then_inc(half_ready, 1)

                def rstd_of(i):
                    pool.wait_ge(var_ready, i + 1)
                    need(pool, x1_ready, i)
                    pool.tensor_tensor(rstd[:, :], var_eps[:, :], minus_half[:, :], ALU.pow).then_inc(rstd_ready, 1)

                pool.wait_ge(half_ready, 1)
                rstd_of(0)
                with pool.Fori(1, NG) as i:
                    rstd_of(i)

            @block.tensor
            def _(pe):
                def transpose_x(i):
                    pe.wait_ge(x_loaded, 16 * (i + 1))
                    need(pe, logit_copied, i - 2)
                    for c in range(DC):
                        for t in range(TT):
                            last = pe.transpose(mp[:, (c * TT + t) * P:(c * TT + t + 1) * P],
                                                x_in[:, t, c * P:(c + 1) * P], ident[:, :])
                    last.then_inc(xt_done, 1)

                def project_q(i, g):
                    s = 4 * i + g
                    if g == 0:
                        pe.wait_ge(xt_lo, i + 1)
                    if isinstance(i, int) and i == 0:
                        pe.wait_ge(w_lo, AT_WQ[g])
                    for b in range(2):
                        need(pe, q_copied, 2 * s + b - 1)
                        if g == 1:
                            need(pe, k_copied, 2 * i + b + 1)
                        if isinstance(i, int) and i == 0:
                            pe.wait_ge(k_copied if g == 0 else v_lo, b + 1)
                        elif g == 2:
                            pe.wait_ge(v_lo, 2 * i + b + 1)
                        for h in range(2 * b, 2 * b + 2):
                            head = REP * g + h
                            last = product(pe, qp[b][:, (h % 2) * GT:(h % 2 + 1) * GT],
                                           lambda a, c: wq_sb[:, a, c, head * HD:(head + 1) * HD],
                                           lambda a, c: xt[:, a, c, :], range(DC))
                        last.then_inc(q_done, 1)

                def project_k(i):
                    if isinstance(i, int) and i == 0:
                        pe.wait_ge(xt_lo, 1)
                        pe.wait_ge(w_lo, AT_WK)
                    for b in range(2):
                        if not (isinstance(i, int) and i == 0):
                            pe.wait_ge(q_copied, 8 * i + b + 1)
                        for g in range(2 * b, 2 * b + 2):
                            last = product(pe, qp[b][:, (g % 2) * GT:(g % 2 + 1) * GT],
                                           lambda a, c: wk_sb[:, a, c, g * HD:(g + 1) * HD],
                                           lambda a, c: xt[:, a, c, :], range(DC))
                        last.then_inc(k_done, 1)

                def project_v(i):
                    for t in range(TT):
                        if isinstance(i, int) and i == 0:
                            pe.wait_ge(w_lo, AT_WV)
                            pe.wait_ge(q_copied, t + 1)
                        else:
                            pe.wait_ge(q_copied, 8 * i + 2 + t + 1)
                        product(pe, qp[t][:, :], lambda a, c: xt[:, a, c, t * P:(t + 1) * P],
                                lambda a, c: wv_sb[:, a, c, :], range(DC)).then_inc(v_done, 1)

                def scores(i, g):
                    s = 4 * i + g
                    for b in range(2):
                        need(pe, max_done, 2 * s + b - 1)
                        pe.wait_ge(q_copied, 2 * s + 2)
                        if g == 0:
                            pe.wait_ge(k_copied, 2 * i + 2)
                        if isinstance(s, int) and s == 0:
                            pe.wait_ge(carry_zero, 2)
                        for t in range(4):
                            w, pair = 2 * b + t // 2, t % 2
                            last = pe.matmul(sp[b][:, t * P:(t + 1) * P],
                                             q_sb[:, w, 2 * pair:2 * pair + 2, :],
                                             kt[:, g, w * WIN:w * WIN + 2 * WIN], start=True, stop=True)
                        last.then_inc(s_done, 1)

                def transpose_prob(i, g):
                    s = 4 * i + g
                    for b in range(2):
                        pe.wait_ge(prob_ready, 2 * s + b + 1)
                        need(pe, o_lo, 2 * s + b - 1)
                        for t in range(4):
                            last = pe.transpose(po[b][:, t * P:(t + 1) * P], prob[:, 4 * b + t, :], ident[:, :])
                        last.then_inc(pt_done, 1)

                def head_out(i, g):
                    s = 4 * i + g
                    for b in range(2):
                        pe.wait_ge(pt_lo, 2 * s + b + 1)
                        if g == 0 and b == 0:
                            pe.wait_ge(v_ready, i + 1)
                        for w in range(2 * b, 2 * b + 2):
                            last = product(pe, po[b][:, (w % 2) * GT:(w % 2 + 1) * GT],
                                           lambda a, c: v_sb[:, w, a, g * HD:(g + 1) * HD],
                                           lambda a, c: pt_sb[:, a, w, :], (0,))
                        last.then_inc(o_done, 1)

                def project_out(i, g):
                    s = 4 * i + g
                    pe.wait_ge(o_lo, 2 * s + 2)
                    if g == 0:
                        need(pe, y_read, i)
                    if isinstance(i, int) and i == 0:
                        pe.wait_ge(w_lo, AT_WO[g])
                    for t in range(TT):
                        for h in range(REP):
                            last = product(pe, yp[:, t * D:(t + 1) * D],
                                           lambda a, c: o_sb[:, g % 2, a, t, h, :],
                                           lambda a, c: wo_sb[:, a, REP * g + h, :], (0,),
                                           start=(g == 0 and t == 0 and h == 0), stop=(g == KV - 1 and h == REP - 1))
                    last.then_inc(wo_done, 1)

                def transpose_x1(i):
                    pe.wait_ge(x1_ready, i + 1)
                    for c in range(DC):
                        for t in range(TT):
                            last = pe.transpose(mp[:, (c * TT + t) * P:(c * TT + t + 1) * P],
                                                x1_cur[:, t, c * P:(c + 1) * P], ident[:, :])
                    last.then_inc(x1t_done, 1)

                def gate_logits(i):
                    pe.wait_ge(x1t_copied, i + 1)
                    for t in range(TT):
                        for c in range(DC):
                            last = pe.matmul(mp[:, t * E:(t + 1) * E], x1t[:, c, t * P:(t + 1) * P],
                                             gate_sb[:, c, :], start=(c == 0), stop=(c == DC - 1))
                    last.then_inc(logit_done, 1)

                def group(i, first, last):
                    for g in range(KV):
                        transpose_prob(i, g)
                        if not (last and g == 3):
                            scores(i + (g + 1) // KV, (g + 1) % KV)
                        if not (last and g >= 2):
                            project_q(i + (g + 2) // KV, (g + 2) % KV)
                        head_out(i, g)
                        if g == 1 and not last:
                            transpose_x(i + 1)
                        if g == 2:
                            if not last:
                                project_k(i + 1)
                                pe.wait_ge(xt_lo, i + 2)
                            if not first:
                                transpose_x1(i - 1)
                        if g == 3:
                            if not last:
                                project_v(i + 1)
                            if not first:
                                gate_logits(i - 1)
                        if not (first and g == 0):
                            project_out(i - (g == 0), (g - 1) % KV)

                pe.wait_ge(ident_ready, 1)
                transpose_x(0)
                project_k(0)
                project_q(0, 0)
                scores(0, 0)
                project_v(0)
                project_q(0, 1)
                group(0, True, False)
                pe.wait_ge(gate_loaded, 16)
                with pe.Fori(1, NG - 1) as i:
                    group(i, False, False)
                group(NG - 1, False, True)
                project_out(NG - 1, KV - 1)
                pe.wait_ge(logit_copied, NG - 1)
                transpose_x1(NG - 1)
                gate_logits(NG - 1)

            @block.scalar
            def _(act):
                def split_hi(out, raw):
                    act.activation(out, raw, ACT.Copy).then_inc(w_hi, 1)

                def prob_hi(i, g):
                    s = 4 * i + g
                    for b in range(2):
                        act.wait_ge(pt_done, 2 * s + b + 1)
                        need(act, o_done, 2 * s + b - 1)
                        act.activation(pt_sb[:, HI, 2 * b:2 * b + 2, :].rearrange("p w n -> p (w n)"),
                                       po[b][:, :], ACT.Copy).then_inc(pt_hi, 1)

                def exps(i, g, b):
                    s = 4 * i + g
                    act.wait_ge(max_done, 2 * s + b + 1)
                    need(act, pt_done, 2 * s + b - 1)
                    for t in range(4):
                        n, w = 4 * b + t, 2 * b + t // 2
                        out, src = prob[:, n, :], neg_s[:, n, :]
                        if w % 2 == 0:
                            out = out.rearrange("p (a k) -> p a k", a=2)[:, ::-1, :]
                            src = src.rearrange("p (a k) -> p a k", a=2)
                        last = act.activation(out, src, ACT.Exp, bias=neg_max[:, n:n + 1], scale=-1.0,
                                              accum_out=row_sum[:, n:n + 1])
                    last.then_inc(exp_done, 1)

                def copy_q(i, g, b):
                    s = 4 * i + g
                    act.wait_ge(q_done, 2 * s + b + 1)
                    need(act, s_done, 2 * s)
                    act.activation(q_sb[:, :, 2 * b:2 * b + 2, :].rearrange("p w h q -> p h w q"),
                                   qp[b][:, :].rearrange("p (h w q) -> p h w q", h=2, w=GW),
                                   ACT.Copy).then_inc(q_copied, 1)

                def out_hi(i, g):
                    s = 4 * i + g
                    for b in range(2):
                        act.wait_ge(o_done, 2 * s + b + 1)
                        need(act, wo_done, s - 1)
                        act.activation(o_sb[:, g % 2, HI, b, :, :].rearrange("p h (w q) -> p w h q", w=2),
                                       po[b][:, :].rearrange("p (w h q) -> p w h q", w=2, h=REP),
                                       ACT.Copy).then_inc(o_hi, 1)

                def xt_hi_of(i):
                    act.wait_ge(xt_done, i + 1)
                    need(act, q_done, 8 * i)
                    act.activation(xt[:, HI, :, :].rearrange("p c n -> p (c n)"), mp[:, :], ACT.Copy).then_inc(xt_hi, 1)

                def copy_k(i):
                    need(act, k_carried, i)
                    for b in range(2):
                        act.wait_ge(k_done, 2 * i + b + 1)
                        act.activation(kt[:, 2 * b:2 * b + 2, WIN:], qp[b][:, :].rearrange("p (g n) -> p g n", g=2),
                                       ACT.Copy).then_inc(k_copied, 1)

                def v_hi_of(i):
                    need(act, v_carried, i)
                    need(act, o_done, 8 * i)
                    for t in range(TT):
                        act.wait_ge(v_done, 2 * i + t + 1)
                        act.activation(v_sb[:, 2 * t + 1, HI, :], qp[t][:, :], ACT.Copy).then_inc(v_hi, 1)

                def copy_x1t(i):
                    act.wait_ge(x1t_done, i + 1)
                    act.activation(x1t[:, :, :].rearrange("p c n -> p (c n)"), mp[:, :], ACT.Copy).then_inc(x1t_copied, 1)

                def group(i, first, last):
                    for g in range(KV):
                        prob_hi(i, g)
                        nxt = (i + (g + 1) // KV, (g + 1) % KV)
                        nxt2 = (i + (g + 2) // KV, (g + 2) % KV)
                        for b in range(2):
                            if not (last and g == 3):
                                exps(*nxt, b)
                            if not (last and g >= 2):
                                copy_q(*nxt2, b)
                        out_hi(i, g)
                        if g == 1 and not last:
                            xt_hi_of(i + 1)
                        if g == 2:
                            if not last:
                                copy_k(i + 1)
                            if not first:
                                copy_x1t(i - 1)
                        if g == 3 and not last:
                            v_hi_of(i + 1)
                        if first:
                            act.wait_ge(wo_loaded[g], 16)
                            split_hi(wo_sb[:, HI, g * REP:(g + 1) * REP, :], raw_wo[g])

                def split_q(g):
                    act.wait_ge(wq_loaded[g], 16)
                    split_hi(wq_sb[:, HI, :, g * REP * HD:(g + 1) * REP * HD], raw_wq[g])

                xt_hi_of(0)
                act.wait_ge(wk_loaded, 16)
                split_hi(wk_sb[:, HI, :, :], raw_wk)
                split_q(0)
                copy_k(0)
                act.wait_ge(wv_loaded, 16)
                split_hi(wv_sb[:, HI, :, :], raw_wv)
                copy_q(0, 0, 0)
                copy_q(0, 0, 1)
                split_q(1)
                exps(0, 0, 0)
                exps(0, 0, 1)
                v_hi_of(0)
                split_q(2)
                copy_q(0, 1, 0)
                copy_q(0, 1, 1)
                split_q(3)
                group(0, True, False)
                with act.Fori(1, NG - 1) as i:
                    group(i, False, False)
                group(NG - 1, False, True)
                copy_x1t(NG - 1)

            @block.vector
            def _(dve):
                def lo_part(out, src, hi):
                    return dve.tensor_tensor(out, src, hi.bitcast(F32), ALU.subtract)

                def stand(n):
                    dve.memset(spare[:, n:n + 1], 0.0)

                def prob_lo(i, g):
                    s = 4 * i + g
                    for b in range(2):
                        dve.wait_ge(pt_hi, 2 * s + b + 1)
                        lo_part(pt_sb[:, LO, 2 * b:2 * b + 2, :].rearrange("p w n -> p (w n)"), po[b][:, :],
                                pt_sb[:, HI, 2 * b:2 * b + 2, :].rearrange("p w n -> p (w n)")).then_inc(pt_lo, 1)

                def maxes(i, g):
                    s = 4 * i + g
                    for b in range(2):
                        dve.wait_ge(s_done, 2 * s + b + 1)
                        need(dve, exp_done, 2 * s + b - 1)
                        if g == 0 and b == 0:
                            dve.wait_ge(mask_set, i + 1)
                        stand(2 * g + b)
                        for t in range(4):
                            n, w = 4 * b + t, 2 * b + t // 2
                            m = mask_first if w == 0 else mask
                            last = dve.tensor_tensor_reduce(
                                out=neg_s[:, n, :], in0=sp[b][:, t * P:(t + 1) * P], in1=m[:, :], scale=-SCALE,
                                scalar=BIG, op0=ALU.add, op1=ALU.min, accum_out=neg_max[:, n:n + 1])
                        last.then_inc(max_done, 1)

                def normalise(i, g):
                    s = 4 * i + g
                    for b in range(2):
                        dve.wait_ge(exp_done, 2 * s + b + 1)
                        dve.reciprocal(row_inv[:, 4 * b:4 * b + 4], row_sum[:, 4 * b:4 * b + 4]).then_inc(inv_done, 1)
                        dve.wait_ge(inv_done, 2 * s + b + 1)
                        tiles = prob[:, 4 * b:4 * b + 4, :]
                        dve.tensor_tensor(tiles, tiles, row_inv[:, 4 * b:4 * b + 4].unsqueeze(2).to_broadcast([P, 4, P]),
                                          ALU.mult).then_inc(prob_ready, 1)

                def out_lo(i, g):
                    s = 4 * i + g
                    for b in range(2):
                        dve.wait_ge(o_hi, 2 * s + b + 1)
                        lo_part(o_sb[:, g % 2, LO, b, :, :].rearrange("p h (w q) -> p w h q", w=2),
                                po[b][:, :].rearrange("p (w h q) -> p w h q", w=2, h=REP),
                                o_sb[:, g % 2, HI, b, :, :].rearrange("p h (w q) -> p w h q", w=2)).then_inc(o_lo, 1)

                def xt_lo_of(i):
                    dve.wait_ge(xt_hi, i + 1)
                    lo_part(xt[:, LO, :, :].rearrange("p c n -> p (c n)"), mp[:, :],
                            xt[:, HI, :, :].rearrange("p c n -> p (c n)")).then_inc(xt_lo, 1)

                def set_mask(i):
                    dve.wait_ge(masks_ready, 1)
                    need(dve, max_done, 8 * i)
                    dve.tensor_copy(mask_first[:, 0:WIN], mask_table[:, i, :] if isinstance(i, int) else
                                    mask_table[:, bass.ds(i, 1), :].rearrange("p a k -> p (a k)")).then_inc(mask_set, 1)

                def carry_k(i):
                    dve.wait_ge(s_done, 8 * i)
                    dve.tensor_copy(kt[:, :, 0:WIN], kt[:, :, GT:]).then_inc(k_carried, 1)

                def carry_v(i):
                    dve.wait_ge(o_done, 8 * i - 1)
                    dve.tensor_copy(v_sb[WIN:P, 0, :, :], v_sb[WIN:P, GW - 1, :, :]).then_inc(v_carried, 1)

                def v_lo_of(i):
                    for t in range(TT):
                        dve.wait_ge(v_hi, 2 * i + t + 1)
                        lo_part(v_sb[:, 2 * t + 1, LO, :], qp[t][:, :], v_sb[:, 2 * t + 1, HI, :]).then_inc(v_lo, 1)
                    dve.wait_ge(v_lo, 2 * i + 2)
                    dve.tensor_copy(v_sb[0:WIN, 0, :, :], v_sb[0:WIN, 1, :, :])
                    dve.tensor_copy(v_sb[0:WIN, 2, :, :], v_sb[0:WIN, 3, :, :])
                    dve.tensor_copy(v_sb[WIN:P, 2, :, :], v_sb[WIN:P, 1, :, :]).then_inc(v_ready, 1)

                def norm_stats(i):
                    dve.wait_ge(wo_done, 4 * i + 4)
                    dve.wait_ge(res_loaded, 16 * (i + 1))
                    dve.tensor_tensor(summed[:, :, :].rearrange("p t d -> p (t d)"), yp[:, :],
                                      x_res[:, :, :].rearrange("p t d -> p (t d)"), ALU.add).then_inc(y_read, 1)
                    dve.wait_ge(y_read, i + 1)
                    for t in range(TT):
                        last = dve.bn_stats(stats[:, t, :], summed[:, t, :])
                    last.then_inc(stats_done, 1)
                    dve.wait_ge(stats_done, i + 1)
                    stand(2 * KV)
                    for t in range(TT):
                        last = dve.bn_aggr(mean_var[:, t, :], stats[:, t, :])
                    last.then_inc(mean_done, 1)
                    dve.wait_ge(mean_done, i + 1)
                    dve.tensor_scalar(var_eps[:, :], mean_var[:, :, 1], EPS, None, ALU.add).then_inc(var_ready, 1)

                def norm_apply(i):
                    dve.wait_ge(rstd_ready, i + 1)
                    need(dve, x1_stored, 16 * i)
                    need(dve, x1t_done, i)
                    for t in range(TT):
                        last = dve.tensor_scalar(x1_cur[:, t, :], summed[:, t, :], mean_var[:, t, 0:1],
                                                 rstd[:, t:t + 1], ALU.subtract, ALU.mult)
                    last.then_inc(x1_ready, 1)

                def copy_logits(i):
                    dve.wait_ge(logit_done, i + 1)
                    dve.tensor_copy(logits[:, bass.ds(i * (TT * E), TT * E)], mp[:, 0:TT * E]).then_inc(logit_copied, 1)

                def group(i, first, last):
                    for g in range(KV):
                        nxt = (i + (g + 1) // KV, (g + 1) % KV)
                        prob_lo(i, g)
                        if not (last and g == 3):
                            maxes(*nxt)
                        if g == 2 and not last:
                            carry_k(i + 1)
                        if g == 1 and not first:
                            norm_stats(i - 1)
                        if not (last and g == 3):
                            normalise(*nxt)
                        if g == 3 and not last:
                            carry_v(i + 1)
                        out_lo(i, g)
                        if g == 1:
                            if not last:
                                xt_lo_of(i + 1)
                            if not first:
                                norm_apply(i - 1)
                        if g == 2 and not last:
                            set_mask(i + 1)
                        if g == 3:
                            if not last:
                                v_lo_of(i + 1)
                            if not first:
                                copy_logits(i - 1)
                        if first:
                            heads = slice(g * REP, (g + 1) * REP)
                            split_lo(wo_sb[:, LO, heads, :], raw_wo[g], wo_sb[:, HI, heads, :], AT_WO[g])

                def split_lo(out, raw, hi, n):
                    dve.wait_ge(w_hi, n)
                    lo_part(out, raw, hi).then_inc(w_lo, 1)

                def split_q(g):
                    cols = slice(g * REP * HD, (g + 1) * REP * HD)
                    split_lo(wq_sb[:, LO, :, cols], raw_wq[g], wq_sb[:, HI, :, cols], AT_WQ[g])

                xt_lo_of(0)
                split_lo(wk_sb[:, LO, :, :], raw_wk, wk_sb[:, HI, :, :], AT_WK)
                split_q(0)
                split_lo(wv_sb[:, LO, :, :], raw_wv, wv_sb[:, HI, :, :], AT_WV)
                set_mask(0)
                split_q(1)
                maxes(0, 0)
                normalise(0, 0)
                v_lo_of(0)
                split_q(2)
                split_q(3)
                group(0, True, False)
                with dve.Fori(1, NG - 1) as i:
                    group(i, False, False)
                group(NG - 1, False, True)
                norm_stats(NG - 1)
                norm_apply(NG - 1)
                copy_logits(NG - 1)


def expert_phase(nc, sem, raw, w_down, x1_dram, out, logits, ident):
    GT2 = 512
    TT2 = GT2 // P
    NG2 = B * T // GT2
    TPB = T // P
    with ExitStack() as ctx:
        def local(name, shape, dt=F32):
            return ctx.enter_context(nc.sbuf_tensor("ffn_" + name, shape, dt))

        def bank(name):
            return ctx.enter_context(nc.psum_tensor("ffn_" + name, [P, 512], F32))

        up_sb = local("up_sb", [P, 2, DC, HPAD], F32R)
        gt_sb = local("gt_sb", [P, 2, DC, WHOLE], F32R)
        up_a_sb = local("up_a_sb", [P, 2, DC, ER], F32R)
        gt_a_sb = local("gt_a_sb", [P, 2, DC, ER], F32R)
        up_b_sb = local("up_b_sb", [P, 2, HPAD], F32R)
        gt_b_sb = local("gt_b_sb", [P, 2, HPAD], F32R)
        down_sb = local("down_sb", [P, 2, HC, D], F32R)
        down_a_sb = local("down_a_sb", [P, 2, HC, ER], F32R)
        down_b_sb = local("down_b_sb", [P, 2, D], F32R)
        raw_down = local("raw_down", [P, HC, D])
        raw_up, raw_gt, raw_up_a, raw_gt_a, raw_up_b, raw_gt_b, raw_down_a, raw_down_b = carve(raw, FFN_SHAPES)
        [product_z, c_rows, gated, mixed_sb] = carve(raw, [(4, GT2), (4, GT2), (2, GT2), (1, GT2)])

        x1_in = local("x1_in", [P, TT2, D])
        x1_res = local("x1_res", [P, TT2, D])
        x1t = local("x1t", [P, 2, 2, DC, GT2], F32R)
        z_first = local("z_first", [P, 2, 2, 2, GT2], F32R)
        z_delta = local("z_delta", [P, 2, 2, 2, GT2], F32R)
        mask_rows = local("mask_rows", [P, 2, 2, GT2])
        mask_delta = local("mask_delta", [P, GT2])
        parts = local("parts", [P, 2, 3, 2, GT2], F32R)
        y_masked = local("y_masked", [P, 2, GT2])
        y_parts = local("y_parts", [P, 2, GT2], F32R)
        summed = local("summed", [P, TT2, D])
        stats = local("stats", [P, TT2, 6])
        mean_var = local("mean_var", [P, TT2, 2])
        var_eps = local("var_eps", [P, TT2])
        minus_half = local("minus_half", [P, TT2])
        rstd = local("rstd", [P, TT2])
        spare = local("spare", [P, 1])
        mask_wide = local("mask_wide", [P, 2, TT2, ER], BF16)
        c_wide = local("c_wide", [P, 2, TT2, P])
        ident_bf = local("ident_bf", [P, P], BF16)
        ones = local("ones", [P, P])
        rest = local("rest", [P, NT, E])
        same = local("same", [P, NT, E])
        order = local("order", [P, E])
        chosen = local("chosen", [P, 2, NT, E])
        mask_tok = local("mask_tok", [P, 2, NT, E], BF16)
        top = local("top", [P, 2, NT])
        key = local("key", [P, NT])
        tile_max = local("tile_max", [P, 2 * B])
        seq_max = local("seq_max", [2 * B, 1])
        diag = local("diag", [2 * B, 2 * B])
        tile_sum = local("tile_sum", [P, 2 * B])
        seq_inv = local("seq_inv", [P, 2 * B])
        weight = local("weight", [P, 2, NT])

        pair = [(bank("u0"), bank("g0")), (bank("u1"), bank("g1"))]
        z_bank = [pair[1][1], pair[0][1]]
        yb = [bank("y0"), bank("y1")]
        ob = [bank("out0"), bank("out1")]

        pad_zero, filled, order_ready, ones_ready, half_ready = (
            sem("pad_zero"), sem("filled2"), sem("order_ready"), sem("ones_ready"), sem("half_ready2"))
        down_loaded, x1_loaded, res_loaded, out_stored = (
            sem("down_loaded"), sem("x1_loaded"), sem("res_loaded2"), sem("out_stored"))
        w_hi, w_lo = sem("w_hi2"), sem("w_lo2")
        route = sem("route")
        max_turned, max_spread, exp_done, sum_spread = (
            sem("max_turned"), sem("max_spread"), sem("exp_done2"), sem("sum_spread"))
        masks_ready, weight_ready = sem("masks_ready2"), sem("weight_ready")
        mask_wide_ready, c_wide_ready = sem("mask_wide_ready"), sem("c_wide_ready")
        x1t_done, x1t_hi, x1t_lo = sem("x1t_done2"), sem("x1t_hi"), sem("x1t_lo")
        mask_done, mask_copied, second_ready = sem("mask_done"), sem("mask_copied"), sem("second_ready")
        c_done, c_copied = sem("c_done"), sem("c_copied")
        z_done, z_masked, z_hi, z_lo = sem("z_done"), sem("z_masked"), sem("z_hi"), sem("z_lo")
        z_up_delta_lo, z_gate_delta_lo = sem("z_up_delta_lo"), sem("z_gate_delta_lo")
        base_done, delta_done, silu_done = sem("base_done"), sem("delta_done"), sem("silu_done")
        gate_done, scale_done, mix_done = sem("gate_done"), sem("scale_done"), sem("mix_done")
        part_hi, part_lo, down_done = sem("part_hi"), sem("part_lo"), sem("down_done")
        y_read, y_hi, y_lo, fold_done = sem("y_read2"), sem("y_hi"), sem("y_lo"), sem("fold_done")
        y_summed, second_diff = sem("y_summed"), sem("second_diff")
        out_read, stats_done, mean_done, var_ready, rstd_ready, norm_done = (
            sem("out_read"), sem("stats_done2"), sem("mean_done2"), sem("var_ready2"), sem("rstd_ready2"),
            sem("norm_done"))

        x1_tiles = x1_dram.rearrange("(n t p) d -> n p t d", t=TT2, p=P)
        out_tiles = out.rearrange("(n t p) d -> n p t d", t=TT2, p=P)

        whole, last_gate, last_up = slice(0, WHOLE), slice(WHOLE, WHOLE + HLAST), slice(WHOLE + HLAST, HPAD)
        tail = slice(WHOLE, HID)
        splits = [
            (lambda a: up_a_sb[:, a, :, :], raw_up_a), (lambda a: gt_a_sb[:, a, :, :], raw_gt_a),
            (lambda a: up_sb[:, a, :, whole], raw_up[:, :, whole]), (lambda a: gt_sb[:, a, :, :], raw_gt[:, :, whole]),
            (lambda a: up_sb[:, a, :, last_up], raw_up[:, :, tail]), (lambda a: up_sb[:, a, :, last_gate], raw_gt[:, :, tail]),
            (lambda a: up_b_sb[:, a, whole], raw_up_b[:, 0, whole]), (lambda a: up_b_sb[:, a, last_up], raw_up_b[:, 0, tail]),
            (lambda a: gt_b_sb[:, a, 0:HID], raw_gt_b[:, 0, :]),
            (lambda a: down_a_sb[:, a, :, :], raw_down_a), (lambda a: down_b_sb[:, a, :], raw_down_b[:, 0, :]),
            (lambda a: down_sb[:, a, :, :], raw_down[:, :, :]),
        ]
        SPLIT_LOGITS, SPLIT_SUM, SPLIT_DOWN = 3, 6, len(splits) - 1

        pads = [up_b_sb[:, :, last_gate], gt_b_sb[:, :, last_up]]

        def rows_of(j):
            return slice(0, HLAST if j == HC - 1 else P)

        def sums(j):
            if j == HC - 1:
                return pair[j % 2][0][HLAST:P, :], pair[j % 2][0][0:HLAST, :]
            return pair[j % 2][0][:, :], pair[j % 2][1][:, :]

        def lo_place(j, k):
            if j == HC - 1:
                return parts[HLAST:P, j % 2, k, HI, :]
            return parts[:, j % 2, k, LO, :]

        def down_product(pe, out_, stationary, moving, j, **flags):
            weights_first = flags.pop("weights_first")
            if j < HC - 1:
                return product(pe, out_, lambda a, c: stationary(a, slice(0, P)),
                               lambda a, c: moving(a, slice(0, P)), (0,), **flags)
            half = slice(0, HLAST)
            a, b = (LO, HI) if weights_first else (HI, LO)
            pe.matmul(out_, stationary(HI, slice(0, P)), moving(HI, slice(0, P)), start=flags.get("start", True),
                      stop=False, skip_group_check=True)
            return pe.matmul(out_, stationary(a, half), moving(b, half), start=False, stop=flags.get("stop", True),
                             skip_group_check=True)

        def each_group(eng, group):
            group(0, 0)
            group(1, 1)
            with eng.Fori(1, NG2 // 2 - 1) as m:
                group(2 * m, 0)
                group(2 * m + 1, 1)
            group(NG2 - 2, 0)
            group(NG2 - 1, 1)

        with nc.Block() as block:

            @block.sync
            def _(sp_):
                def load_x1(n):
                    need(sp_, x1t_done, n)
                    sp_.dma_start(x1_in[:, :, :], x1_tiles[n]).then_inc(x1_loaded, 16)

                def load_res(n):
                    need(sp_, out_read, n)
                    sp_.dma_start(x1_res[:, :, :], x1_tiles[n]).then_inc(res_loaded, 16)

                def store(n):
                    sp_.wait_ge(norm_done, n + 1)
                    sp_.dma_start(out_tiles[n], summed[:, :, :]).then_inc(out_stored, 16)

                load_x1(0)
                sp_.dma_start(raw_down[:, 0:HC - 1, :],
                              w_down[0:WHOLE, :].rearrange("(c p) n -> p c n", p=P)).then_inc(down_loaded, 16)
                for half in (slice(0, HLAST), slice(HLAST, P)):
                    sp_.dma_start(raw_down[half, HC - 1, :], w_down[WHOLE:, :]).then_inc(down_loaded, 16)
                load_x1(1)
                load_res(0)
                with sp_.Fori(1, NG2 - 1) as n:
                    load_x1(n + 1)
                    load_res(n)
                    store(n - 1)
                load_res(NG2 - 1)
                store(NG2 - 2)
                store(NG2 - 1)
                sp_.wait_ge(out_stored, 16 * NG2)

            @block.gpsimd
            def _(pool):
                for e in range(E):
                    pool.memset(order[:, e:e + 1], float(E - e)).then_inc(order_ready, 1)
                    pool.wait_ge(order_ready, e + 1)
                pool.memset(ones[:, :], 1.0).then_inc(ones_ready, 1)
                pool.wait_ge(ones_ready, 1)
                pool.tensor_copy(ident_bf[:, :], ident[:, :]).then_inc(ones_ready, 1)
                pool.wait_ge(ones_ready, 2)
                for k, pad in enumerate(pads):
                    pool.memset(pad.bitcast(F32), 0.0).then_inc(pad_zero, 1)
                    pool.wait_ge(pad_zero, k + 1)
                pool.memset(minus_half[:, :], -0.5).then_inc(half_ready, 1)
                pool.wait_ge(half_ready, 1)

                def widen(n):
                    need(pool, mask_done, n)
                    for k in range(2):
                        src = mask_tok[:, k, :, :].rearrange("p t e -> p (t e)")[:, bass.ds(n * (TT2 * E), TT2 * E)]
                        pool.tensor_copy(mask_wide[:, k, :, :].rearrange("p t (e r) -> p (t e) r", r=R),
                                         src.unsqueeze(2).to_broadcast([P, TT2 * E, R])).then_inc(mask_wide_ready, 1)
                    need(pool, c_done, n)
                    if isinstance(n, int) and n == 0:
                        pool.wait_ge(weight_ready, 1)
                    for k in range(2):
                        pool.tensor_copy(c_wide[:, k, :, :],
                                         weight[:, k, bass.ds(n * TT2, TT2)].unsqueeze(2).to_broadcast([P, TT2, P]))\
                            .then_inc(c_wide_ready, 1)

                def rstd_of(n):
                    pool.wait_ge(var_ready, n + 1)
                    need(pool, norm_done, n)
                    pool.tensor_tensor(rstd[:, :], var_eps[:, :], minus_half[:, :], ALU.pow).then_inc(rstd_ready, 1)

                def second_mask(n, p):
                    pool.wait_ge(mask_copied, 2 * n + 2)
                    need(pool, y_read, 2 * n - 2)
                    pool.tensor_tensor(mask_rows[:, p, 1, :], mask_rows[:, p, 0, :], mask_delta[:, :],
                                       ALU.add).then_inc(second_ready, 1)

                def z_delta_lo(n, p):
                    pool.wait_ge(z_hi, 4 * n + 2)
                    pool.tensor_tensor(z_delta[:, p, 0, LO, :], product_z[:, 1, :], z_delta[:, p, 0, HI, :].bitcast(F32),
                                       ALU.subtract).then_inc(z_up_delta_lo, 1)

                def sum_y(n):
                    pool.wait_ge(y_read, 2 * n + 2)
                    pool.tensor_tensor(y_masked[:, 0, :], y_masked[:, 0, :], y_masked[:, 1, :], ALU.add).then_inc(y_summed, 1)

                def group(n, p):
                    first = isinstance(n, int) and n == 0
                    last = isinstance(n, int) and n == NG2 - 1
                    if not first:
                        sum_y(n - 1)
                    if not last:
                        second_mask(n + 1, 1 - p)
                    if not first:
                        rstd_of(n - 1)
                    if not (isinstance(n, int) and n >= NG2 - 2):
                        widen(n + 2)
                    if not last:
                        z_delta_lo(n + 1, 1 - p)

                pool.wait_ge(masks_ready, 2)
                widen(0)
                widen(1)
                second_mask(0, 0)
                z_delta_lo(0, 0)
                each_group(pool, group)
                sum_y(NG2 - 1)
                rstd_of(NG2 - 1)

            @block.tensor
            def _(pe):
                def turn_x1(n, p):
                    pe.wait_ge(x1_loaded, 16 * (n + 1))
                    for c in range(DC):
                        for t in range(TT2):
                            last = pe.transpose(pair[1][c][:, t * P:(t + 1) * P], x1_in[:, t, c * P:(c + 1) * P], ident[:, :])
                    last.then_inc(x1t_done, 1)

                def turn_masks(n, p):
                    pe.wait_ge(mask_wide_ready, 2 * n + 2)
                    for k in range(2):
                        for t in range(TT2):
                            last = pe.matmul(pair[0][k][:, t * P:(t + 1) * P], mask_wide[:, k, t, :], ident_bf[:, :],
                                             start=True, stop=True)
                    last.then_inc(mask_done, 1)

                def turn_weights(n, p):
                    pe.wait_ge(c_wide_ready, 2 * n + 2)
                    for k in range(2):
                        for t in range(TT2):
                            last = pe.transpose(pair[1][k][:, t * P:(t + 1) * P], c_wide[:, k, t, :], ident[:, :])
                    last.then_inc(c_done, 1)

                def low_rank_in(n, p, k):
                    pe.wait_ge(x1t_lo, 2 * n + 2)
                    w = (up_a_sb, gt_a_sb)[k]
                    product(pe, z_bank[k][:, :], lambda a, c: w[:, a, c, :],
                            lambda a, c: x1t[:, p, a, c, :], range(DC)).then_inc(z_done, 1)

                def base(n, p, j):
                    u = HC * n + j
                    need(pe, gate_done, 2 * u - 2)
                    slot = {1: c_copied, 2: mask_copied, 3: x1t_lo}.get(j)
                    if slot:
                        pe.wait_ge(slot, 2 * n + 2 if n_is_last(n) else 2 * n + 4)
                    cols = slice(j * P, (j + 1) * P)
                    if j == HC - 1:
                        product(pe, pair[j % 2][0][:, :], lambda a, c: up_sb[:, a, c, cols],
                                lambda a, c: x1t[:, p, a, c, :], range(DC), stop=False)
                    for k, (w, wb) in enumerate(((up_sb, up_b_sb), (gt_sb, gt_b_sb))):
                        bank_ = pair[j % 2][0 if j == HC - 1 else k]
                        if j == 0 and k == 1:
                            pe.wait_ge(z_masked, 4 * n + 4)
                        if j < HC - 1:
                            product(pe, bank_[:, :], lambda a, c: w[:, a, c, cols],
                                    lambda a, c: x1t[:, p, a, c, :], range(DC), stop=False)
                        if j == 0:
                            pe.wait_ge(z_lo, 2 * n + k + 1)
                        last = product(pe, bank_[:, :], lambda a, c: wb[:, a, cols],
                                       lambda a, c: z_first[:, p, k, a, :], (0,), start=False)
                    last.then_inc(base_done, 1)

                def n_is_last(n):
                    return isinstance(n, int) and n == NG2 - 1

                def delta(n, p, j):
                    u = HC * n + j
                    pe.wait_ge(gate_done, 2 * u + 1)
                    cols = slice(j * P, (j + 1) * P)
                    for k, wb in enumerate((up_b_sb, gt_b_sb)):
                        if j == 0:
                            pe.wait_ge((z_up_delta_lo, z_gate_delta_lo)[k], n + 1)
                        last = product(pe, pair[j % 2][0 if j == HC - 1 else k][:, :], lambda a, c: wb[:, a, cols],
                                       lambda a, c: z_delta[:, p, k, a, :], (0,), start=False)
                    last.then_inc(delta_done, 1)

                def down_low_rank(n, j):
                    u = HC * n + j
                    if j == 0:
                        need(pe, y_read, 2 * n)
                    for k in range(2):
                        pe.wait_ge(part_lo, 3 * u + k + 1)
                        down_product(pe, yb[k][:, :], lambda a, rows: down_a_sb[rows, a, j, :],
                                     lambda a, rows: parts[rows, j % 2, k, a, :], j, weights_first=True,
                                     start=(j == 0), stop=(j == HC - 1))

                def down(n, j):
                    u = HC * n + j
                    if j == 0:
                        need(pe, out_read, n)
                    pe.wait_ge(part_lo, 3 * u + 3)
                    for t in range(TT2):
                        last = down_product(pe, ob[t // 2][:, (t % 2) * D:(t % 2 + 1) * D],
                                            lambda a, rows: parts[rows, j % 2, 2, a, t * P:(t + 1) * P],
                                            lambda a, rows: down_sb[rows, a, j, :], j, weights_first=False,
                                            start=(j == 0 and t % 2 == 0), stop=False)
                    last.then_inc(down_done, 1)

                def fold(n):
                    pe.wait_ge(y_lo, n + 1)
                    for t in range(TT2):
                        last = product(pe, ob[t // 2][:, (t % 2) * D:(t % 2 + 1) * D],
                                       lambda a, c: y_parts[:, a, t * P:(t + 1) * P],
                                       lambda a, c: down_b_sb[:, a, :], (0,), start=False)
                    last.then_inc(fold_done, 1)

                def group(n, p):
                    first = isinstance(n, int) and n == 0
                    last = n_is_last(n)
                    for j in range(HC):
                        u = HC * n + j
                        base(n, p, j)
                        if not last:
                            turn = {0: turn_weights, 1: turn_masks, 2: turn_x1}.get(j)
                            if turn or j >= HC - 2:
                                need(pe, gate_done, 2 * u)
                            if turn:
                                turn(n + 1, 1 - p)
                            elif j >= HC - 2:
                                low_rank_in(n + 1, 1 - p, j - (HC - 2))
                        if j > 0 or not first:
                            before = (n, j - 1) if j > 0 else (n - 1, HC - 1)
                            down_low_rank(*before)
                            if j == 1:
                                if not first:
                                    fold(n - 1)
                                delta(n, p, j)
                            down(*before)
                        if j != 1:
                            delta(n, p, j)

                pe.wait_ge(ones_ready, 2)
                turn_x1(0, 0)
                pe.wait_ge(route, 12)
                pe.transpose(ob[0][0:2 * B, 0:P], tile_max[:, :], ident[:, :]).then_inc(max_turned, 1)
                pe.wait_ge(route, 14)
                pe.matmul(ob[0][:, 128:128 + 2 * B], ones[0:2 * B, :], diag[:, :], start=True, stop=True).then_inc(max_spread, 1)
                turn_masks(0, 0)
                pe.wait_ge(route, 16)
                pe.matmul(ob[1][:, 0:2 * B], ones[:, :], tile_sum[:, :], start=True, stop=True).then_inc(sum_spread, 1)
                pe.wait_ge(w_lo, 2)
                pe.wait_ge(mask_copied, 2)
                low_rank_in(0, 0, 0)
                low_rank_in(0, 0, 1)
                pe.wait_ge(z_masked, 2)
                turn_weights(0, 0)
                pe.wait_ge(w_lo, len(splits))
                pe.wait_ge(pad_zero, len(pads))
                pe.wait_ge(c_copied, 2)
                each_group(pe, group)
                down_low_rank(NG2 - 1, HC - 1)
                down(NG2 - 1, HC - 1)
                fold(NG2 - 1)

            @block.scalar
            def _(act):
                def turned_hi(n, p):
                    for c in range(DC):
                        act.wait_ge(x1t_done, n + 1)
                        act.activation(x1t[:, p, HI, c, :], pair[1][c][:, :], ACT.Copy).then_inc(x1t_hi, 1)

                def copy_masks(n, p):
                    act.wait_ge(mask_done, n + 1)
                    need(act, y_read, 2 * n - 2)
                    act.activation(mask_rows[:, p, 0, :], pair[0][0][:, :], ACT.Copy).then_inc(mask_copied, 1)
                    need(act, z_masked, 4 * n)
                    need(act, second_ready, n)
                    act.activation(mask_delta[:, :], pair[0][1][:, :], ACT.Copy).then_inc(mask_copied, 1)

                def copy_weights(n, p):
                    act.wait_ge(c_done, n + 1)
                    for k in range(2):
                        act.activation(c_rows[:, 2 * p + k, :], pair[1][k][:, :], ACT.Copy).then_inc(c_copied, 1)

                def z_hi_of(n, p, which, k):
                    act.wait_ge(z_masked, 4 * n + 2 * k + which + 1)
                    act.activation((z_first, z_delta)[which][:, p, k, HI, :], product_z[:, 2 * k + which, :], ACT.Copy).then_inc(z_hi, 1)

                def silu(n, j, k):
                    u = HC * n + j
                    if k == 0:
                        act.wait_ge(base_done, u + 1)
                        need(act, mix_done, u)
                        need(act, part_lo, 3 * u - 2)
                    else:
                        act.wait_ge(delta_done, u + 1)
                        need(act, part_lo, 3 * u - 1)
                    act.activation(gated[rows_of(j), k, :], sums(j)[0], ACT.Silu).then_inc(silu_done, 1)

                def part_hi_of(n, j, k):
                    u = HC * n + j
                    if k < 2:
                        act.wait_ge(scale_done, 2 * u + k + 1)
                    else:
                        act.wait_ge(mix_done, u + 1)
                    need(act, down_done, u - 1)
                    rows = rows_of(j)
                    act.activation(parts[rows, j % 2, k, HI, :], gated[rows, k, :] if k < 2 else mixed_sb[rows, 0, :],
                                   ACT.Copy).then_inc(part_hi, 1)

                def y_hi_of(n):
                    act.wait_ge(y_summed, n + 1)
                    need(act, fold_done, n)
                    act.activation(y_parts[:, HI, :], y_masked[:, 0, :], ACT.Copy).then_inc(y_hi, 1)

                def group(n, p):
                    first = isinstance(n, int) and n == 0
                    last = isinstance(n, int) and n == NG2 - 1
                    for j in range(HC):
                        silu(n, j, 0)
                        if not last:
                            turn = {0: copy_weights, 1: copy_masks, 2: turned_hi}.get(j)
                            if turn:
                                turn(n + 1, 1 - p)
                        part_hi_of(n, j, 0)
                        if j >= HC - 2 and not last:
                            z_hi_of(n + 1, 1 - p, 0, j - (HC - 2))
                        silu(n, j, 1)
                        part_hi_of(n, j, 1)
                        part_hi_of(n, j, 2)
                        if j == HC - 2 and not last:
                            z_hi_of(n + 1, 1 - p, 1, 0)
                        if j == 0 and not first:
                            y_hi_of(n - 1)
                        if j == HC - 1 and not last:
                            z_hi_of(n + 1, 1 - p, 1, 1)

                for k, (out_, raw_) in enumerate(splits):
                    if k == 2:
                        turned_hi(0, 0)
                    if k == SPLIT_LOGITS:
                        act.wait_ge(route, 15)
                        act.activation(top[:, :, :], top[:, :, :], ACT.Exp).then_inc(exp_done, 1)
                    if k == SPLIT_DOWN:
                        act.wait_ge(down_loaded, 48)
                    act.activation(out_(HI), raw_, ACT.Copy).then_inc(w_hi, 1)
                act.wait_ge(w_lo, len(splits))
                copy_masks(0, 0)
                for k in range(2):
                    for which in range(2):
                        z_hi_of(0, 0, which, k)
                copy_weights(0, 0)
                each_group(act, group)
                y_hi_of(NG2 - 1)

            @block.vector
            def _(dve):
                def lo_part(out_, src, hi):
                    return dve.tensor_tensor(out_, src, hi.bitcast(F32), ALU.subtract)

                def turned_lo(n, p):
                    for c in range(DC):
                        dve.wait_ge(x1t_hi, 2 * n + c + 1)
                        lo_part(x1t[:, p, LO, c, :], pair[1][c][:, :], x1t[:, p, HI, c, :]).then_inc(x1t_lo, 1)

                def mask_z(n, p, k):
                    dve.wait_ge(z_done, 2 * n + k + 1)
                    if k == 0:
                        need(dve, z_gate_delta_lo, n)
                        need(dve, z_up_delta_lo, n)
                    for which in range(2):
                        m = mask_rows[:, p, 0, :] if which == 0 else mask_delta[:, :]
                        dve.tensor_tensor(product_z[:, 2 * k + which, :], z_bank[k][:, :], m, ALU.mult).then_inc(z_masked, 1)

                def z_lo_of(n, p, which, k):
                    dve.wait_ge(z_hi, 4 * n + 2 * k + which + 1)
                    both = (z_first, z_delta)[which][:, p, k, :, :]
                    done = z_gate_delta_lo if which == 1 else z_lo
                    lo_part(both[:, LO, :], product_z[:, 2 * k + which, :], both[:, HI, :]).then_inc(done, 1)

                def gate(n, j, k):
                    u = HC * n + j
                    dve.wait_ge(silu_done, 2 * u + k + 1)
                    rows = rows_of(j)
                    dve.tensor_tensor(gated[rows, k, :], gated[rows, k, :], sums(j)[1], ALU.mult).then_inc(gate_done, 1)

                def scale(n, p, j, k):
                    u = HC * n + j
                    dve.wait_ge(gate_done, 2 * u + k + 1)
                    if j == 0:
                        dve.wait_ge(c_copied, 2 * n + 2)
                    rows = rows_of(j)
                    dve.tensor_tensor(gated[rows, k, :], gated[rows, k, :], c_rows[rows, 2 * p + k, :],
                                      ALU.mult).then_inc(scale_done, 1)

                def mix(n, j):
                    u = HC * n + j
                    dve.wait_ge(scale_done, 2 * u + 2)
                    need(dve, part_hi, 3 * u)
                    need(dve, part_lo, 3 * u)
                    rows = rows_of(j)
                    dve.tensor_tensor(mixed_sb[rows, 0, :], gated[rows, 0, :], gated[rows, 1, :], ALU.add).then_inc(mix_done, 1)

                def part_lo_of(n, j, k):
                    u = HC * n + j
                    dve.wait_ge(part_hi, 3 * u + k + 1)
                    rows = rows_of(j)
                    lo_part(lo_place(j, k), gated[rows, k, :] if k < 2 else mixed_sb[rows, 0, :],
                            parts[rows, j % 2, k, HI, :]).then_inc(part_lo, 1)

                def mask_y(n, p):
                    dve.wait_ge(down_done, HC * n + HC)
                    need(dve, y_lo, n)
                    for k in range(2):
                        dve.tensor_tensor(y_masked[:, k, :], yb[k][:, :], mask_rows[:, p, k, :], ALU.mult).then_inc(y_read, 1)

                def y_lo_of(n):
                    dve.wait_ge(y_hi, n + 1)
                    lo_part(y_parts[:, LO, :], y_masked[:, 0, :], y_parts[:, HI, :]).then_inc(y_lo, 1)

                def add_out(n):
                    dve.wait_ge(fold_done, n + 1)
                    dve.wait_ge(res_loaded, 16 * (n + 1))
                    need(dve, out_stored, 16 * n)
                    for h in range(2):
                        last = dve.tensor_tensor(summed[:, 2 * h:2 * h + 2, :].rearrange("p t d -> p (t d)"), ob[h][:, :],
                                                 x1_res[:, 2 * h:2 * h + 2, :].rearrange("p t d -> p (t d)"), ALU.add)
                    last.then_inc(out_read, 1)

                def norm_stats(n):
                    dve.wait_ge(out_read, n + 1)
                    for t in range(TT2):
                        last = dve.bn_stats(stats[:, t, :], summed[:, t, :])
                    last.then_inc(stats_done, 1)
                    dve.wait_ge(stats_done, n + 1)
                    dve.memset(spare[:, :], 0.0)
                    for t in range(TT2):
                        last = dve.bn_aggr(mean_var[:, t, :], stats[:, t, :])
                    last.then_inc(mean_done, 1)
                    dve.wait_ge(mean_done, n + 1)
                    dve.tensor_scalar(var_eps[:, :], mean_var[:, :, 1], EPS, None, ALU.add).then_inc(var_ready, 1)

                def norm_apply(n):
                    dve.wait_ge(rstd_ready, n + 1)
                    for t in range(TT2):
                        last = dve.tensor_scalar(summed[:, t, :], summed[:, t, :], mean_var[:, t, 0:1],
                                                 rstd[:, t:t + 1], ALU.subtract, ALU.mult)
                    last.then_inc(norm_done, 1)

                def group(n, p):
                    first = isinstance(n, int) and n == 0
                    last = isinstance(n, int) and n == NG2 - 1
                    for j in range(HC):
                        gate(n, j, 0)
                        scale(n, p, j, 0)
                        if not last and j == 2:
                            turned_lo(n + 1, 1 - p)
                        if j == 1 and not first:
                            add_out(n - 1)
                        part_lo_of(n, j, 0)
                        if j == 0 and not first:
                            mask_y(n - 1, 1 - p)
                        if j >= HC - 2 and not last:
                            mask_z(n + 1, 1 - p, j - (HC - 2))
                        gate(n, j, 1)
                        if j >= HC - 2 and not last:
                            z_lo_of(n + 1, 1 - p, 0, j - (HC - 2))
                        scale(n, p, j, 1)
                        mix(n, j)
                        part_lo_of(n, j, 1)
                        part_lo_of(n, j, 2)
                        if j == 0 and not first:
                            y_lo_of(n - 1)
                        if j == 2 and not first:
                            norm_stats(n - 1)
                        if j == 3 and not first:
                            norm_apply(n - 1)
                        if j == HC - 1 and not last:
                            z_lo_of(n + 1, 1 - p, 1, 1)

                step = [0]

                def routed(instruction):
                    step[0] += 1
                    instruction.then_inc(route, 1)
                    dve.wait_ge(route, step[0])

                def wide(per_tile):
                    return per_tile.unsqueeze(2).to_broadcast([P, NT, E])

                dve.wait_ge(order_ready, E)
                every = logits[:, :].rearrange("p (t e) -> p t e", e=E)
                orders = order[:, :].unsqueeze(1).to_broadcast([P, NT, E])
                for k, values in enumerate((every, rest[:, :, :])):
                    if k == 1:
                        routed(dve.scalar_tensor_tensor(out=rest[:, :, :], in0=chosen[:, 0, :, :], scalar=-BIG, in1=every,
                                                        op0=ALU.mult, op1=ALU.add))
                    routed(dve.tensor_reduce(top[:, k, :], values, AX.X, ALU.max))
                    routed(dve.tensor_tensor(same[:, :, :], values, wide(top[:, k, :]), ALU.is_equal))
                    routed(dve.tensor_tensor(same[:, :, :], same[:, :, :], orders, ALU.mult))
                    routed(dve.tensor_reduce(key[:, :], same[:, :, :], AX.X, ALU.max))
                    routed(dve.tensor_tensor(chosen[:, k, :, :], same[:, :, :], wide(key[:, :]), ALU.is_equal))
                by_seq = top[:, :, :].rearrange("p k (b t) -> p (k b) t", t=TPB)
                routed(dve.tensor_reduce(tile_max[:, :], by_seq, AX.X, ALU.max))
                dve.tensor_scalar(mask_tok[:, 0, :, :], chosen[:, 0, :, :], 2.0, None, ALU.mult).then_inc(masks_ready, 1)
                dve.tensor_tensor(rest[:, :, :], chosen[:, 1, :, :], chosen[:, 0, :, :], ALU.subtract).then_inc(second_diff, 1)
                dve.wait_ge(second_diff, 1)
                dve.tensor_scalar(mask_tok[:, 1, :, :], rest[:, :, :], 2.0, None, ALU.mult).then_inc(masks_ready, 1)
                dve.wait_ge(max_turned, 1)
                routed(dve.tensor_reduce(seq_max[:, :], ob[0][0:2 * B, 0:P], AX.X, ALU.max))
                routed(dve.tensor_scalar(diag[:, :], ident[0:2 * B, 0:2 * B], seq_max[:, 0:1], None, ALU.mult))
                dve.wait_ge(max_spread, 1)
                routed(dve.tensor_tensor(by_seq, by_seq, ob[0][:, 128:128 + 2 * B].unsqueeze(2).to_broadcast([P, 2 * B, TPB]),
                                         ALU.subtract))
                for k, (out_, raw_) in enumerate(splits):
                    if k == 2:
                        turned_lo(0, 0)
                    if k == SPLIT_LOGITS:
                        dve.wait_ge(exp_done, 1)
                        routed(dve.tensor_reduce(tile_sum[:, :], by_seq, AX.X, ALU.add))
                    if k == SPLIT_SUM:
                        dve.wait_ge(sum_spread, 1)
                        routed(dve.reciprocal(seq_inv[:, :], ob[1][:, 0:2 * B]))
                        dve.tensor_tensor(weight[:, :, :].rearrange("p k (b t) -> p (k b) t", t=TPB), by_seq,
                                          seq_inv[:, :].unsqueeze(2).to_broadcast([P, 2 * B, TPB]), ALU.mult).then_inc(weight_ready, 1)
                    dve.wait_ge(w_hi, k + 1)
                    lo_part(out_(LO), raw_, out_(HI)).then_inc(w_lo, 1)
                dve.wait_ge(w_lo, len(splits))
                dve.wait_ge(mask_copied, 2)
                mask_z(0, 0, 0)
                mask_z(0, 0, 1)
                z_lo_of(0, 0, 0, 0)
                z_lo_of(0, 0, 0, 1)
                z_lo_of(0, 0, 1, 1)
                each_group(dve, group)
                mask_y(NG2 - 1, 1)
                y_lo_of(NG2 - 1)
                add_out(NG2 - 1)
                norm_stats(NG2 - 1)
                norm_apply(NG2 - 1)


def build(nc, x, wq, wk, wv, wo, gate_wt, w_up, w_gate, w_down, up_a, up_b, gate_a, gate_b, down_a, down_b, out):
    x1_dram = nc.dram_tensor("x1_dram", [B * T, D], F32, kind="Internal").ap()
    with ExitStack() as ctx:
        def sem(name):
            return ctx.enter_context(nc.semaphore(name))

        ident = ctx.enter_context(nc.sbuf_tensor("ident", [P, P], F32))
        logits = ctx.enter_context(nc.sbuf_tensor("logits", [P, NT * E], F32))
        raw = ctx.enter_context(nc.sbuf_tensor("raw", [P, RAW], F32))
        ffn_loaded = sem("ffn_loaded")

        def by_rows(w):
            return w.rearrange("(c p) n -> p c n", p=P)

        r_up, r_gate, r_up_a, r_gate_a, r_up_b, r_gate_b, r_down_a, r_down_b = carve(raw, FFN_SHAPES)
        ffn_loads = [
            (r_up, by_rows(w_up)), (r_gate, by_rows(w_gate)), (r_up_a, by_rows(up_a)), (r_gate_a, by_rows(gate_a)),
            (r_up_b[:, 0, :], up_b), (r_gate_b[:, 0, :], gate_b), (r_down_b[:, 0, :], down_b),
            (r_down_a[:, 0:HC - 1, :], by_rows(down_a[0:WHOLE, :])),
            (r_down_a[0:HLAST, HC - 1, :], down_a[WHOLE:, :]), (r_down_a[HLAST:P, HC - 1, :], down_a[WHOLE:, :]),
        ]
        attention_phase(nc, sem, raw, x, wq, wk, wv, wo, gate_wt, ffn_loads, x1_dram, logits, ident, ffn_loaded)
        expert_phase(nc, sem, raw, w_down, x1_dram, out, logits, ident)


def kernel(**inputs):
    import numpy as np
    import concourse.bacc as bacc
    from concourse.bass_utils import run_bass_kernel_spmd

    def put(name):
        return np.asarray(inputs[name])

    def rows_first(a):
        return a.transpose(0, 2, 1).reshape(ER, a.shape[1])

    arrays = {
        "x": put("L0_attn_x").reshape(B * T, D),
        "wq": put("L0_attn_Wq"), "wk": put("L0_attn_Wk"), "wv": put("L0_attn_Wv"), "wo": put("L0_attn_Wo"),
        "gate_wt": put("L0_ffn_gate_w").T,
        "w_up": put("L0_ffn_w_up").T, "w_gate": put("L0_ffn_w_gate").T, "w_down": put("L0_ffn_w_down").T,
        "up_a": put("L0_ffn_up_A").reshape(ER, D).T, "up_b": rows_first(put("L0_ffn_up_B")),
        "gate_a": put("L0_ffn_gate_A").reshape(ER, D).T, "gate_b": rows_first(put("L0_ffn_gate_B")),
        "down_a": put("L0_ffn_down_A").reshape(ER, HID).T, "down_b": rows_first(put("L0_ffn_down_B")),
    }
    arrays = {name: np.ascontiguousarray(a) for name, a in arrays.items()}
    nc = bacc.Bacc("TRN2", target_bir_lowering=False, num_devices=1)
    args = [nc.dram_tensor(name, a.shape, F32, kind="ExternalInput").ap() for name, a in arrays.items()]
    out = nc.dram_tensor("out", [B * T, D], F32, kind="ExternalOutput").ap()
    build(nc, *args, out)
    result = run_bass_kernel_spmd(nc, [arrays], core_ids=[0])
    return np.asarray(result.results[0]["out"]).reshape(B, T, D)
```

```python
from contextlib import ExitStack

import concourse.bass as bass
from concourse import mybir

F32 = mybir.dt.float32
F32R = mybir.dt.float32r
BF16 = mybir.dt.bfloat16
ALU = mybir.AluOpType
ACT = mybir.ActivationFunctionType
AX = mybir.AxisListType

P = 128
D = 256
DC = D // P
B, T = 4, 1024
HEADS, KV, HD, WIN = 16, 4, 128, 64
GT2 = 512
TT2 = GT2 // P
REP = HEADS // KV
GT = 256
GW = GT // WIN
NG = B * T // GT
TT = GT // P
NT = B * T // P
E, R, HID = 8, 16, 704
HC = -(-HID // P)
HPAD = HC * P
WHOLE = (HC - 1) * P
HLAST = HID - WHOLE
assert 2 * HLAST == P
ER = E * R
FFN_SHAPES = [(DC, HID), (DC, HID), (DC, ER), (DC, ER), (1, HID), (1, HID), (HC, ER), (1, D), (HC, D)]
RQ = DC * REP * HD
RAW = max(DC * (HEADS + 2 * KV) * HD, sum(a * b for a, b in FFN_SHAPES))
SCALE = float(HD) ** -0.5
NEG = -1e30
BIG = 3e38
EPS = 1e-5
HI, LO = 0, 1
PARTS = ((HI, HI), (HI, LO), (LO, HI))


class Named:
    pass


def need(eng, sem, count):
    if isinstance(count, int) and count <= 0:
        return
    eng.wait_ge(sem, count)


def carve(buffer, shapes):
    views, at = [], 0
    for a, b in shapes:
        views.append(buffer[:, at:at + a * b].rearrange("p (a b) -> p a b", a=a))
        at += a * b
    return views


def product(eng, out, stationary, moving, chunks, start=True, stop=True):
    last = None
    n = len(chunks) * len(PARTS)
    for k, c in enumerate(chunks):
        for j, (a, b) in enumerate(PARTS):
            m = k * len(PARTS) + j
            last = eng.matmul(out, stationary(a, c), moving(b, c), start=start and m == 0,
                              stop=stop and m == n - 1, skip_group_check=True)
    return last


def turn_tiles(pe, banks, tokens, ident):
    last = None
    for c in range(DC):
        for t in range(TT2):
            last = pe.transpose(banks[c][:, t * P:(t + 1) * P], tokens[:, t, c * P:(c + 1) * P], ident[:, :])
    return last


def turn_mask_tiles(pe, banks, mask_wide, ident_bf):
    last = None
    for k in range(2):
        for t in range(TT2):
            last = pe.matmul(banks[k][:, t * P:(t + 1) * P], mask_wide[:, k, t, :], ident_bf[:, :],
                             start=True, stop=True)
    return last


def expert_weights(raw, split_area, up_b, gate_b):
    w = Named()
    w.raw = carve(raw, FFN_SHAPES)
    raw_up, raw_gt, raw_up_a, raw_gt_a, raw_up_b, raw_gt_b, raw_down_a, raw_down_b, raw_down = w.raw

    at = [0]

    def parts(*shape):
        size = 2
        for n in shape:
            size *= n
        view = split_area[:, at[0]:at[0] + size]
        at[0] += size
        if len(shape) == 1:
            return view.rearrange("p (a n) -> p a n", a=2)
        return view.rearrange("p (a c n) -> p a c n", a=2, c=shape[0])

    w.up = parts(DC, HPAD)
    w.gate = parts(DC, WHOLE)
    w.down = parts(HC, D)
    w.up_a, w.gate_a = parts(DC, ER), parts(DC, ER)
    w.down_a = parts(HC, ER)
    w.down_b = parts(D)
    w.up_b, w.gate_b = up_b, gate_b
    start = sum(a * b for a, b in FFN_SHAPES[0:2])
    w.first_mask_wide = raw[:, start:start + 2 * DC * ER].bitcast(BF16).rearrange("p (k t n) -> p k t n", k=2, t=TT2)
    whole, last_gate, last_up = slice(0, WHOLE), slice(WHOLE, WHOLE + HLAST), slice(WHOLE + HLAST, HPAD)
    tail = slice(WHOLE, HID)
    w.pads = [up_b[:, :, last_gate], gate_b[:, :, last_up]]
    w.split_b = [[(lambda a: up_b[:, a, whole], raw_up_b[:, 0, whole]),
                  (lambda a: up_b[:, a, last_up], raw_up_b[:, 0, tail])],
                 [(lambda a: gate_b[:, a, 0:HID], raw_gt_b[:, 0, :])]]
    w.split_low = [[(lambda a: w.up_a[:, a, :, :], raw_up_a), (lambda a: w.gate_a[:, a, :, :], raw_gt_a),
                    (lambda a: w.down_a[:, a, :, :], raw_down_a)],
                   [(lambda a: w.down_b[:, a, :], raw_down_b[:, 0, :])]]
    w.split_up = [(lambda a: w.up[:, a, :, whole], raw_up[:, :, whole])]
    w.split_last = [(lambda a: w.up[:, a, :, last_up], raw_up[:, :, tail]),
                    (lambda a: w.up[:, a, :, last_gate], raw_gt[:, :, tail])]
    w.split_gate = [(lambda a: w.gate[:, a, :, :], raw_gt[:, :, whole])]
    w.raw_down = raw_down
    return w


EARLY = (NG - 3) * TT
ROUTED_EARLY = 5 + 8


def select(dve, keep, step, k, first_tile, end_tile):
    tiles = slice(first_tile, end_tile)
    count = end_tile - first_tile
    top, chosen, mask_tok = keep.top, keep.chosen, keep.mask_tok

    def routed(instruction):
        step[0] += 1
        instruction.then_inc(keep.route, 1)
        dve.wait_ge(keep.route, step[0])

    def wide(per_tile):
        return per_tile.unsqueeze(2).to_broadcast([P, count, E])

    every = keep.logits[:, :].rearrange("p (t e) -> p t e", e=E)[:, tiles, :]
    orders = keep.order[:, :].unsqueeze(1).to_broadcast([P, count, E])
    eq, key = keep.same[:, tiles, :], keep.key[:, tiles]
    if k == 1:
        routed(dve.scalar_tensor_tensor(out=every, in0=chosen[:, 0, tiles, :], scalar=-BIG, in1=every,
                                        op0=ALU.mult, op1=ALU.add))
    routed(dve.tensor_reduce(top[:, k, tiles], every, AX.X, ALU.max))
    routed(dve.tensor_tensor(eq, every, wide(top[:, k, tiles]), ALU.is_equal))
    routed(dve.tensor_tensor(eq, eq, orders, ALU.mult))
    routed(dve.tensor_reduce(key, eq, AX.X, ALU.max))
    routed(dve.tensor_tensor(chosen[:, k, tiles, :], eq, wide(key), ALU.is_equal))
    if k == 1:
        dve.tensor_scalar(mask_tok[:, 0, tiles, :], chosen[:, 0, tiles, :], 2.0, None, ALU.mult)
        routed(dve.tensor_tensor(eq, chosen[:, 1, tiles, :], chosen[:, 0, tiles, :], ALU.subtract))
        routed(dve.tensor_scalar(mask_tok[:, 1, tiles, :], eq, 2.0, None, ALU.mult))


def attention_phase(nc, sem, raw, split_area, experts, x, wq, wk, wv, wo, gate_wt, ffn_loads, x1_dram, keep):
    ident, ffn_loaded = keep.ident, keep.ffn_loaded
    top, mask_tok = keep.top, keep.mask_tok
    with ExitStack() as ctx:
        def local(name, shape, dt=F32):
            return ctx.enter_context(nc.sbuf_tensor("attn_" + name, shape, dt))

        raw_wq = [carve(raw[:, g * RQ:], [(DC, REP * HD)])[0] for g in range(KV)]
        raw_wo = [carve(raw[:, g * RQ:], [(REP, D)])[0] for g in range(KV)]
        raw_wk, raw_wv = carve(raw[:, KV * RQ:], [(DC, KV * HD), (DC, KV * HD)])
        n_q, n_k = 2 * DC * HEADS * HD, 2 * DC * KV * HD
        wq_sb, wk_sb, wv_sb = (split_area[:, a:b].rearrange("p (a c n) -> p a c n", a=2, c=DC)
                               for a, b in ((0, n_q), (n_q, n_q + n_k), (n_q + n_k, n_q + 2 * n_k)))
        wo_sb = local("wo_sb", [P, 2, HEADS, D], F32R)
        gate_sb = local("gate_sb", [P, DC, E])

        x_in = local("x_in", [P, TT, D])
        x_res = local("x_res", [P, TT, D])
        xt = local("xt", [P, 2, DC, GT], F32R)
        kt = local("kt", [P, KV, WIN + GT])
        v_sb = local("v_sb", [P, GW, 2, KV * HD], F32R)
        q_sb = local("q_sb", [P, GW, REP, WIN])
        neg_s = local("neg_s", [P, 2 * GW, P])
        neg_max = local("neg_max", [P, 2 * GW])
        row_sum = local("row_sum", [P, 2 * GW])
        spare = local("spare", [P, 2 * KV + 1])
        row_inv = local("row_inv", [P, 2 * GW])
        prob = local("prob", [P, 2 * GW, P])
        pt_sb = keep.turned[:, :, :].rearrange("p a (w n) -> p a w n", w=GW)
        x1t_first = keep.turned[:, :, :].rearrange("p a (c n) -> p a c n", c=DC)
        o_sb = local("o_sb", [P, 2, 2, TT, REP, P], F32R)
        summed = local("summed", [P, TT, D])
        stats = local("stats", [P, TT, 6])
        mean_var = local("mean_var", [P, TT, 2])
        var_eps = local("var_eps", [P, TT])
        minus_half = keep.minus_half
        rstd = local("rstd", [P, TT])
        x1_cur = keep.x1_cur
        x1t = local("x1t", [P, DC, GT])
        mask = local("mask", [P, P])
        mask_first = local("mask_first", [P, P])
        mask_table = local("mask_table", [P, NG, WIN])
        logits, order = keep.logits, keep.order

        qp = keep.banks[0:2]
        sp = keep.banks[2:4]
        po = keep.banks[4:6]
        yp = keep.banks[6]
        mp = keep.banks[7]

        x_loaded, res_loaded = sem("x_loaded"), sem("res_loaded")
        wk_loaded, wv_loaded, gate_loaded = sem("wk_loaded"), sem("wv_loaded"), sem("gate_loaded")
        x1_stored = keep.x1_stored
        wq_loaded = [sem(f"wq_loaded{g}") for g in range(KV)]
        wo_loaded = [sem(f"wo_loaded{g}") for g in range(KV)]
        AT_WK, AT_WQ, AT_WV, AT_WO = 1, (2, 4, 5, 6), 3, (7, 8, 9, 10)
        w_hi, w_lo = sem("w_hi"), sem("w_lo")
        ident_ready, masks_ready, filled = sem("ident_ready"), sem("masks_ready"), sem("filled")
        carry_zero = sem("carry_zero")
        half_ready = sem("half_ready")
        xt_done, xt_hi, xt_lo = sem("xt_done"), sem("xt_hi"), sem("xt_lo")
        q_done, q_copied = sem("q_done"), sem("q_copied")
        k_done, k_copied, k_carried = sem("k_done"), sem("k_copied"), sem("k_carried")
        v_done, v_hi, v_lo, v_carried, v_ready = (sem("v_done"), sem("v_hi"), sem("v_lo"),
                                                  sem("v_carried"), sem("v_ready"))
        s_done, max_done, exp_done = sem("s_done"), sem("max_done"), sem("exp_done")
        inv_done, prob_ready = sem("inv_done"), sem("prob_ready")
        pt_done, pt_hi, pt_lo = sem("pt_done"), sem("pt_hi"), sem("pt_lo")
        o_done, o_hi, o_lo = sem("o_done"), sem("o_hi"), sem("o_lo")
        wo_done, y_read = sem("wo_done"), sem("y_read")
        stats_done, mean_done, var_ready, rstd_ready, x1_ready = (
            sem("stats_done"), sem("mean_done"), sem("var_ready"), sem("rstd_ready"), sem("x1_ready"))
        x1t_done, x1t_copied, logit_done, logit_copied = (
            sem("x1t_done"), sem("x1t_copied"), sem("logit_done"), sem("logit_copied"))
        mask_set = sem("mask_set")
        consts_ready = sem("consts_ready")
        route, order_ready = keep.route, keep.order_ready
        e_hi, e_lo = sem("e_hi"), sem("e_lo")

        x_tiles = x.rearrange("(n t p) d -> n p t d", t=TT, p=P)
        x1_tiles = x1_dram.rearrange("(n t p) d -> n p t d", t=TT, p=P)

        with nc.Block() as block:

            @block.sync
            def _(sp_):
                def load_x(i):
                    need(sp_, xt_done, i)
                    sp_.dma_start(x_in[:, :, :], x_tiles[i]).then_inc(x_loaded, 16)

                def load_res(i):
                    need(sp_, y_read, i)
                    sp_.dma_start(x_res[:, :, :], x_tiles[i]).then_inc(res_loaded, 16)

                def store_x1(i):
                    sp_.wait_ge(x1_ready, i + 1)
                    sp_.dma_start(x1_tiles[i], x1_cur[:, :, :]).then_inc(x1_stored, 16)

                load_x(0)
                sp_.dma_start(raw_wk, wk.rearrange("(c p) n -> p c n", p=P)).then_inc(wk_loaded, 16)
                wq_rows = wq.rearrange("(c p) n -> p c n", p=P)
                wo_rows = wo.rearrange("(h p) n -> p h n", p=P)
                for g in range(KV):
                    sp_.dma_start(raw_wq[g], wq_rows[:, :, g * REP * HD:(g + 1) * REP * HD]).then_inc(wq_loaded[g], 16)
                    if g == 0:
                        sp_.dma_start(raw_wv, wv.rearrange("(c p) n -> p c n", p=P)).then_inc(wv_loaded, 16)
                sp_.dma_start(gate_sb[:, :, :], gate_wt.rearrange("(c p) n -> p c n", p=P)).then_inc(gate_loaded, 16)
                load_x(1)
                for g in range(KV):
                    sp_.wait_ge(w_lo, AT_WQ[g])
                    sp_.dma_start(raw_wo[g], wo_rows[:, g * REP:(g + 1) * REP, :]).then_inc(wo_loaded[g], 16)
                load_x(2)
                load_res(0)
                sp_.wait_ge(w_lo, AT_WO[-1])
                for out, src in ffn_loads:
                    sp_.dma_start(out, src).then_inc(ffn_loaded, 16)
                with sp_.Fori(1, NG - 2) as i:
                    load_x(i + 2)
                    load_res(i)
                    store_x1(i - 1)
                for i in (NG - 2, NG - 1):
                    load_res(i)
                    store_x1(i - 1)
                sp_.dma_start(keep.x1_in[:, :, :], x1_dram.rearrange("(n t p) d -> n p t d", t=TT2, p=P)[0])\
                    .then_inc(keep.x1_loaded, 16)
                store_x1(NG - 1)
                sp_.wait_ge(ffn_loaded, 16 * len(ffn_loads))

            @block.gpsimd
            def _(pool):
                def then_wait(instruction, count):
                    instruction.then_inc(filled, 1)
                    pool.wait_ge(filled, count)

                then_wait(pool.memset(ident[:, :], 0.0), 1)
                pool.affine_select(out=ident[:, :], in_=ident[:, :], compare_op=ALU.not_equal, fill=1.0,
                                   base=0, pattern=[[-1, P]], channel_multiplier=1).then_inc(ident_ready, 1)
                pool.wait_ge(ident_ready, 1)
                then_wait(pool.memset(mask[:, :], 0.0), 2)
                then_wait(pool.memset(mask_first[:, :], 0.0), 3)
                then_wait(pool.memset(mask_table[:, :, :], 0.0), 4)
                n = 4
                for half in range(2):
                    rows = slice(half * WIN, (half + 1) * WIN)
                    n += 1
                    then_wait(pool.affine_select(
                        out=mask[rows, 0:WIN], in_=mask[rows, 0:WIN], compare_op=ALU.is_gt, fill=NEG, base=0,
                        pattern=[[1, WIN]], channel_multiplier=-1), n)
                    for m in (mask, mask_first):
                        n += 1
                        then_wait(pool.affine_select(
                            out=m[rows, WIN:P], in_=m[rows, WIN:P], compare_op=ALU.is_ge, fill=NEG, base=0,
                            pattern=[[-1, WIN]], channel_multiplier=1), n)
                    table = mask_table[rows, :, :]
                    n += 1
                    then_wait(pool.affine_select(
                        out=table, in_=table, compare_op=ALU.is_gt, fill=NEG, base=0,
                        pattern=[[0, NG], [1, WIN]], channel_multiplier=-1), n)
                first = mask_table[:, :, :].rearrange("p (b g) k -> p b g k", b=B)[:, :, 0, :]
                pool.memset(first, NEG).then_inc(masks_ready, 1)
                pool.wait_ge(masks_ready, 1)
                pool.memset(kt[:, :, 0:WIN], 0.0).then_inc(carry_zero, 1)
                pool.wait_ge(carry_zero, 1)
                pool.memset(v_sb[WIN:P, 0, :, :].bitcast(F32), 0.0).then_inc(carry_zero, 1)
                pool.wait_ge(carry_zero, 2)
                pool.memset(minus_half[:, :], -0.5).then_inc(half_ready, 1)
                pool.wait_ge(half_ready, 1)
                for e in range(E):
                    pool.memset(order[:, e:e + 1], float(E - e)).then_inc(order_ready, 1)
                    pool.wait_ge(order_ready, e + 1)
                pool.memset(keep.ones[:, :], 1.0).then_inc(consts_ready, 1)
                pool.wait_ge(consts_ready, 1)
                pool.tensor_copy(keep.ident_bf[:, :], ident[:, :]).then_inc(consts_ready, 1)
                pool.wait_ge(consts_ready, 2)
                for k, pad in enumerate(experts.pads):
                    pool.memset(pad.bitcast(F32), 0.0).then_inc(consts_ready, 1)
                    pool.wait_ge(consts_ready, 3 + k)

                def rstd_of(i):
                    pool.wait_ge(var_ready, i + 1)
                    need(pool, x1_ready, i)
                    pool.tensor_tensor(rstd[:, :], var_eps[:, :], minus_half[:, 0:TT], ALU.pow).then_inc(rstd_ready, 1)

                rstd_of(0)
                with pool.Fori(1, NG - 1) as i:
                    rstd_of(i)
                pool.wait_ge(route, ROUTED_EARLY)
                pool.wait_ge(e_lo, 2)
                for k in range(2):
                    src = mask_tok[:, k, 0:TT2, :].rearrange("p t e -> p (t e)")
                    pool.tensor_copy(experts.first_mask_wide[:, k, :, :].rearrange("p t (e r) -> p (t e) r", r=R),
                                     src.unsqueeze(2).to_broadcast([P, TT2 * E, R])).then_inc(keep.mask_wide_ready, 1)
                rstd_of(NG - 1)

            @block.tensor
            def _(pe):
                def transpose_x(i):
                    pe.wait_ge(x_loaded, 16 * (i + 1))
                    need(pe, logit_copied, i - 2)
                    for c in range(DC):
                        for t in range(TT):
                            last = pe.transpose(mp[:, (c * TT + t) * P:(c * TT + t + 1) * P],
                                                x_in[:, t, c * P:(c + 1) * P], ident[:, :])
                    last.then_inc(xt_done, 1)

                def project_q(i, g):
                    s = 4 * i + g
                    if g == 0:
                        pe.wait_ge(xt_lo, i + 1)
                    if isinstance(i, int) and i == 0:
                        pe.wait_ge(w_lo, AT_WQ[g])
                    for b in range(2):
                        need(pe, q_copied, 2 * s + b - 1)
                        if g == 1:
                            need(pe, k_copied, 2 * i + b + 1)
                        if isinstance(i, int) and i == 0:
                            pe.wait_ge(k_copied if g == 0 else v_lo, b + 1)
                        elif g == 2:
                            pe.wait_ge(v_lo, 2 * i + b + 1)
                        for h in range(2 * b, 2 * b + 2):
                            head = REP * g + h
                            last = product(pe, qp[b][:, (h % 2) * GT:(h % 2 + 1) * GT],
                                           lambda a, c: wq_sb[:, a, c, head * HD:(head + 1) * HD],
                                           lambda a, c: xt[:, a, c, :], range(DC))
                        last.then_inc(q_done, 1)

                def project_k(i):
                    if isinstance(i, int) and i == 0:
                        pe.wait_ge(xt_lo, 1)
                        pe.wait_ge(w_lo, AT_WK)
                    for b in range(2):
                        if not (isinstance(i, int) and i == 0):
                            pe.wait_ge(q_copied, 8 * i + b + 1)
                        for g in range(2 * b, 2 * b + 2):
                            last = product(pe, qp[b][:, (g % 2) * GT:(g % 2 + 1) * GT],
                                           lambda a, c: wk_sb[:, a, c, g * HD:(g + 1) * HD],
                                           lambda a, c: xt[:, a, c, :], range(DC))
                        last.then_inc(k_done, 1)

                def project_v(i):
                    for t in range(TT):
                        if isinstance(i, int) and i == 0:
                            pe.wait_ge(w_lo, AT_WV)
                            pe.wait_ge(q_copied, t + 1)
                        else:
                            pe.wait_ge(q_copied, 8 * i + 2 + t + 1)
                        product(pe, qp[t][:, :], lambda a, c: xt[:, a, c, t * P:(t + 1) * P],
                                lambda a, c: wv_sb[:, a, c, :], range(DC)).then_inc(v_done, 1)

                def scores(i, g):
                    s = 4 * i + g
                    for b in range(2):
                        need(pe, max_done, 2 * s + b - 1)
                        pe.wait_ge(q_copied, 2 * s + 2)
                        if g == 0:
                            pe.wait_ge(k_copied, 2 * i + 2)
                        if isinstance(s, int) and s == 0:
                            pe.wait_ge(carry_zero, 2)
                        for t in range(4):
                            w, pair = 2 * b + t // 2, t % 2
                            last = pe.matmul(sp[b][:, t * P:(t + 1) * P],
                                             q_sb[:, w, 2 * pair:2 * pair + 2, :],
                                             kt[:, g, w * WIN:w * WIN + 2 * WIN], start=True, stop=True)
                        last.then_inc(s_done, 1)

                def transpose_prob(i, g):
                    s = 4 * i + g
                    for b in range(2):
                        pe.wait_ge(prob_ready, 2 * s + b + 1)
                        need(pe, o_lo, 2 * s + b - 1)
                        for t in range(4):
                            last = pe.transpose(po[b][:, t * P:(t + 1) * P], prob[:, 4 * b + t, :], ident[:, :])
                        last.then_inc(pt_done, 1)

                def head_out(i, g):
                    s = 4 * i + g
                    for b in range(2):
                        pe.wait_ge(pt_lo, 2 * s + b + 1)
                        if g == 0 and b == 0:
                            pe.wait_ge(v_ready, i + 1)
                        for w in range(2 * b, 2 * b + 2):
                            last = product(pe, po[b][:, (w % 2) * GT:(w % 2 + 1) * GT],
                                           lambda a, c: v_sb[:, w, a, g * HD:(g + 1) * HD],
                                           lambda a, c: pt_sb[:, a, w, :], (0,))
                        last.then_inc(o_done, 1)

                def project_out(i, g):
                    s = 4 * i + g
                    pe.wait_ge(o_lo, 2 * s + 2)
                    if g == 0:
                        need(pe, y_read, i)
                    if isinstance(i, int) and i == 0:
                        pe.wait_ge(w_lo, AT_WO[g])
                    for t in range(TT):
                        for h in range(REP):
                            last = product(pe, yp[:, t * D:(t + 1) * D],
                                           lambda a, c: o_sb[:, g % 2, a, t, h, :],
                                           lambda a, c: wo_sb[:, a, REP * g + h, :], (0,),
                                           start=(g == 0 and t == 0 and h == 0), stop=(g == KV - 1 and h == REP - 1))
                    last.then_inc(wo_done, 1)

                def transpose_x1(i):
                    pe.wait_ge(x1_ready, i + 1)
                    for c in range(DC):
                        for t in range(TT):
                            last = pe.transpose(mp[:, (c * TT + t) * P:(c * TT + t + 1) * P],
                                                x1_cur[:, t, c * P:(c + 1) * P], ident[:, :])
                    last.then_inc(x1t_done, 1)

                def gate_logits(i):
                    pe.wait_ge(x1t_copied, i + 1)
                    for t in range(TT):
                        for c in range(DC):
                            last = pe.matmul(mp[:, t * E:(t + 1) * E], x1t[:, c, t * P:(t + 1) * P],
                                             gate_sb[:, c, :], start=(c == 0), stop=(c == DC - 1))
                    last.then_inc(logit_done, 1)

                def group(i, first, last):
                    for g in range(KV):
                        transpose_prob(i, g)
                        if not (last and g == 3):
                            scores(i + (g + 1) // KV, (g + 1) % KV)
                        if not (last and g >= 2):
                            project_q(i + (g + 2) // KV, (g + 2) % KV)
                        head_out(i, g)
                        if g == 1 and not last:
                            transpose_x(i + 1)
                        if g == 2:
                            if not last:
                                project_k(i + 1)
                                pe.wait_ge(xt_lo, i + 2)
                            if not first:
                                transpose_x1(i - 1)
                        if g == 3:
                            if not last:
                                project_v(i + 1)
                            if not first:
                                gate_logits(i - 1)
                        if not (first and g == 0):
                            project_out(i - (g == 0), (g - 1) % KV)

                pe.wait_ge(ident_ready, 1)
                transpose_x(0)
                project_k(0)
                project_q(0, 0)
                scores(0, 0)
                project_v(0)
                project_q(0, 1)
                group(0, True, False)
                pe.wait_ge(gate_loaded, 16)
                with pe.Fori(1, NG - 1) as i:
                    group(i, False, False)
                group(NG - 1, False, True)
                pe.wait_ge(keep.x1_loaded, 16)
                pe.wait_ge(q_copied, 8 * NG)
                turn_tiles(pe, qp, keep.x1_in, ident).then_inc(keep.x1t_done, 1)
                project_out(NG - 1, KV - 1)
                pe.wait_ge(keep.x1t_lo, 2)
                pe.wait_ge(e_lo, 2)
                pe.wait_ge(max_done, 8 * NG)
                for bank, w in ((qp[1], experts.up_a), (sp[1], experts.gate_a)):
                    product(pe, bank[:, :], lambda a, c: w[:, a, c, :],
                            lambda a, c: x1t_first[:, a, c, :], range(DC)).then_inc(keep.z_done, 1)
                pe.wait_ge(keep.mask_wide_ready, 2)
                turn_mask_tiles(pe, (qp[0], po[1]), experts.first_mask_wide, keep.ident_bf).then_inc(keep.mask_done, 1)
                pe.wait_ge(logit_copied, NG - 1)
                transpose_x1(NG - 1)
                gate_logits(NG - 1)

            @block.scalar
            def _(act):
                def split_hi(out, raw):
                    act.activation(out, raw, ACT.Copy).then_inc(w_hi, 1)

                def split_experts(weights):
                    for out, src in weights:
                        act.activation(out(HI), src, ACT.Copy).then_inc(e_hi, 1)

                def prob_hi(i, g):
                    s = 4 * i + g
                    for b in range(2):
                        act.wait_ge(pt_done, 2 * s + b + 1)
                        need(act, o_done, 2 * s + b - 1)
                        act.activation(pt_sb[:, HI, 2 * b:2 * b + 2, :].rearrange("p w n -> p (w n)"),
                                       po[b][:, :], ACT.Copy).then_inc(pt_hi, 1)

                def exps(i, g, b):
                    s = 4 * i + g
                    act.wait_ge(max_done, 2 * s + b + 1)
                    need(act, pt_done, 2 * s + b - 1)
                    for t in range(4):
                        n, w = 4 * b + t, 2 * b + t // 2
                        out, src = prob[:, n, :], neg_s[:, n, :]
                        if w % 2 == 0:
                            out = out.rearrange("p (a k) -> p a k", a=2)[:, ::-1, :]
                            src = src.rearrange("p (a k) -> p a k", a=2)
                        last = act.activation(out, src, ACT.Exp, bias=neg_max[:, n:n + 1], scale=-1.0,
                                              accum_out=row_sum[:, n:n + 1])
                    last.then_inc(exp_done, 1)

                def copy_q(i, g, b):
                    s = 4 * i + g
                    act.wait_ge(q_done, 2 * s + b + 1)
                    need(act, s_done, 2 * s)
                    act.activation(q_sb[:, :, 2 * b:2 * b + 2, :].rearrange("p w h q -> p h w q"),
                                   qp[b][:, :].rearrange("p (h w q) -> p h w q", h=2, w=GW),
                                   ACT.Copy).then_inc(q_copied, 1)

                def out_hi(i, g):
                    s = 4 * i + g
                    for b in range(2):
                        act.wait_ge(o_done, 2 * s + b + 1)
                        need(act, wo_done, s - 1)
                        act.activation(o_sb[:, g % 2, HI, b, :, :].rearrange("p h (w q) -> p w h q", w=2),
                                       po[b][:, :].rearrange("p (w h q) -> p w h q", w=2, h=REP),
                                       ACT.Copy).then_inc(o_hi, 1)

                def xt_hi_of(i):
                    act.wait_ge(xt_done, i + 1)
                    need(act, q_done, 8 * i)
                    act.activation(xt[:, HI, :, :].rearrange("p c n -> p (c n)"), mp[:, :], ACT.Copy).then_inc(xt_hi, 1)

                def copy_k(i):
                    need(act, k_carried, i)
                    for b in range(2):
                        act.wait_ge(k_done, 2 * i + b + 1)
                        act.activation(kt[:, 2 * b:2 * b + 2, WIN:], qp[b][:, :].rearrange("p (g n) -> p g n", g=2),
                                       ACT.Copy).then_inc(k_copied, 1)

                def v_hi_of(i):
                    need(act, v_carried, i)
                    need(act, o_done, 8 * i)
                    for t in range(TT):
                        act.wait_ge(v_done, 2 * i + t + 1)
                        act.activation(v_sb[:, 2 * t + 1, HI, :], qp[t][:, :], ACT.Copy).then_inc(v_hi, 1)

                def copy_x1t(i):
                    act.wait_ge(x1t_done, i + 1)
                    act.activation(x1t[:, :, :].rearrange("p c n -> p (c n)"), mp[:, :], ACT.Copy).then_inc(x1t_copied, 1)

                def group(i, first, last):
                    nearly = isinstance(i, int) and i == NG - 2
                    for g in range(KV):
                        prob_hi(i, g)
                        if last and g == KV - 1:
                            act.wait_ge(q_done, 8 * NG)
                            split_experts(experts.split_up)
                        nxt = (i + (g + 1) // KV, (g + 1) % KV)
                        nxt2 = (i + (g + 2) // KV, (g + 2) % KV)
                        for b in range(2):
                            if not (last and g == 3):
                                exps(*nxt, b)
                            if not (last and g >= 2):
                                copy_q(*nxt2, b)
                        out_hi(i, g)
                        if g == 1 and not last:
                            xt_hi_of(i + 1)
                        if g == 2:
                            if not last:
                                copy_k(i + 1)
                            if not first:
                                copy_x1t(i - 1)
                        if g == 3 and not last:
                            v_hi_of(i + 1)
                        if nearly and g in (1, 3):
                            if g == 1:
                                act.wait_ge(ffn_loaded, 16 * len(ffn_loads))
                            split_experts(experts.split_b[g // 2])
                        if last and g < 2:
                            if g == 0:
                                act.wait_ge(k_done, 2 * NG)
                                act.wait_ge(v_done, 2 * NG)
                            split_experts(experts.split_low[g])
                        if first:
                            act.wait_ge(wo_loaded[g], 16)
                            split_hi(wo_sb[:, HI, g * REP:(g + 1) * REP, :], raw_wo[g])

                def split_q(g):
                    act.wait_ge(wq_loaded[g], 16)
                    split_hi(wq_sb[:, HI, :, g * REP * HD:(g + 1) * REP * HD], raw_wq[g])

                xt_hi_of(0)
                act.wait_ge(wk_loaded, 16)
                split_hi(wk_sb[:, HI, :, :], raw_wk)
                split_q(0)
                copy_k(0)
                act.wait_ge(wv_loaded, 16)
                split_hi(wv_sb[:, HI, :, :], raw_wv)
                copy_q(0, 0, 0)
                copy_q(0, 0, 1)
                split_q(1)
                exps(0, 0, 0)
                v_hi_of(0)
                exps(0, 0, 1)
                split_q(2)
                split_q(3)
                copy_q(0, 1, 0)
                copy_q(0, 1, 1)
                group(0, True, False)
                with act.Fori(1, NG - 2) as i:
                    group(i, False, False)
                group(NG - 2, False, False)
                group(NG - 1, False, True)
                act.wait_ge(o_done, 8 * NG)
                act.wait_ge(keep.x1t_done, 1)
                for c in range(DC):
                    act.activation(x1t_first[:, HI, c, :], qp[c][:, :], ACT.Copy).then_inc(keep.x1t_hi, 1)
                split_experts(experts.split_last)
                split_experts(experts.split_gate)
                copy_x1t(NG - 1)

            @block.vector
            def _(dve):
                def lo_part(out, src, hi):
                    return dve.tensor_tensor(out, src, hi.bitcast(F32), ALU.subtract)

                def stand(n):
                    dve.memset(spare[:, n:n + 1], 0.0)

                def prob_lo(i, g):
                    s = 4 * i + g
                    for b in range(2):
                        dve.wait_ge(pt_hi, 2 * s + b + 1)
                        lo_part(pt_sb[:, LO, 2 * b:2 * b + 2, :].rearrange("p w n -> p (w n)"), po[b][:, :],
                                pt_sb[:, HI, 2 * b:2 * b + 2, :].rearrange("p w n -> p (w n)")).then_inc(pt_lo, 1)

                def maxes(i, g):
                    s = 4 * i + g
                    for b in range(2):
                        dve.wait_ge(s_done, 2 * s + b + 1)
                        need(dve, exp_done, 2 * s + b - 1)
                        if g == 0 and b == 0:
                            dve.wait_ge(mask_set, i + 1)
                        stand(2 * g + b)
                        for t in range(4):
                            n, w = 4 * b + t, 2 * b + t // 2
                            m = mask_first if w == 0 else mask
                            last = dve.tensor_tensor_reduce(
                                out=neg_s[:, n, :], in0=sp[b][:, t * P:(t + 1) * P], in1=m[:, :], scale=-SCALE,
                                scalar=BIG, op0=ALU.add, op1=ALU.min, accum_out=neg_max[:, n:n + 1])
                        last.then_inc(max_done, 1)

                def normalise(i, g, banks=(0, 1)):
                    s = 4 * i + g
                    for b in banks:
                        dve.wait_ge(exp_done, 2 * s + b + 1)
                        dve.reciprocal(row_inv[:, 4 * b:4 * b + 4], row_sum[:, 4 * b:4 * b + 4]).then_inc(inv_done, 1)
                        dve.wait_ge(inv_done, 2 * s + b + 1)
                        tiles = prob[:, 4 * b:4 * b + 4, :]
                        dve.tensor_tensor(tiles, tiles, row_inv[:, 4 * b:4 * b + 4].unsqueeze(2).to_broadcast([P, 4, P]),
                                          ALU.mult).then_inc(prob_ready, 1)

                def out_lo(i, g):
                    s = 4 * i + g
                    for b in range(2):
                        dve.wait_ge(o_hi, 2 * s + b + 1)
                        lo_part(o_sb[:, g % 2, LO, b, :, :].rearrange("p h (w q) -> p w h q", w=2),
                                po[b][:, :].rearrange("p (w h q) -> p w h q", w=2, h=REP),
                                o_sb[:, g % 2, HI, b, :, :].rearrange("p h (w q) -> p w h q", w=2)).then_inc(o_lo, 1)

                def xt_lo_of(i):
                    dve.wait_ge(xt_hi, i + 1)
                    lo_part(xt[:, LO, :, :].rearrange("p c n -> p (c n)"), mp[:, :],
                            xt[:, HI, :, :].rearrange("p c n -> p (c n)")).then_inc(xt_lo, 1)

                def set_mask(i):
                    dve.wait_ge(masks_ready, 1)
                    need(dve, max_done, 8 * i)
                    dve.tensor_copy(mask_first[:, 0:WIN], mask_table[:, i, :] if isinstance(i, int) else
                                    mask_table[:, bass.ds(i, 1), :].rearrange("p a k -> p (a k)")).then_inc(mask_set, 1)

                def carry_k(i):
                    dve.wait_ge(s_done, 8 * i)
                    dve.tensor_copy(kt[:, :, 0:WIN], kt[:, :, GT:]).then_inc(k_carried, 1)

                def carry_v(i):
                    dve.wait_ge(o_done, 8 * i - 1)
                    dve.tensor_copy(v_sb[WIN:P, 0, :, :], v_sb[WIN:P, GW - 1, :, :]).then_inc(v_carried, 1)

                def v_lo_of(i):
                    for t in range(TT):
                        dve.wait_ge(v_hi, 2 * i + t + 1)
                        lo_part(v_sb[:, 2 * t + 1, LO, :], qp[t][:, :], v_sb[:, 2 * t + 1, HI, :]).then_inc(v_lo, 1)

                def v_copies(i):
                    dve.wait_ge(v_lo, 2 * i + 2)
                    dve.tensor_copy(v_sb[0:WIN, 0, :, :], v_sb[0:WIN, 1, :, :])
                    dve.tensor_copy(v_sb[0:WIN, 2, :, :], v_sb[0:WIN, 3, :, :])
                    dve.tensor_copy(v_sb[WIN:P, 2, :, :], v_sb[WIN:P, 1, :, :]).then_inc(v_ready, 1)

                def norm_stats(i):
                    dve.wait_ge(wo_done, 4 * i + 4)
                    dve.wait_ge(res_loaded, 16 * (i + 1))
                    dve.tensor_tensor(summed[:, :, :].rearrange("p t d -> p (t d)"), yp[:, :],
                                      x_res[:, :, :].rearrange("p t d -> p (t d)"), ALU.add).then_inc(y_read, 1)
                    dve.wait_ge(y_read, i + 1)
                    for t in range(TT):
                        last = dve.bn_stats(stats[:, t, :], summed[:, t, :])
                    last.then_inc(stats_done, 1)
                    dve.wait_ge(stats_done, i + 1)
                    stand(2 * KV)
                    for t in range(TT):
                        last = dve.bn_aggr(mean_var[:, t, :], stats[:, t, :])
                    last.then_inc(mean_done, 1)
                    dve.wait_ge(mean_done, i + 1)
                    dve.tensor_scalar(var_eps[:, :], mean_var[:, :, 1], EPS, None, ALU.add).then_inc(var_ready, 1)

                def norm_apply(i):
                    dve.wait_ge(rstd_ready, i + 1)
                    need(dve, x1_stored, 16 * i)
                    need(dve, x1t_done, i)
                    for t in range(TT):
                        last = dve.tensor_scalar(x1_cur[:, t, :], summed[:, t, :], mean_var[:, t, 0:1],
                                                 rstd[:, t:t + 1], ALU.subtract, ALU.mult)
                    last.then_inc(x1_ready, 1)

                def copy_logits(i):
                    dve.wait_ge(logit_done, i + 1)
                    dve.tensor_copy(logits[:, bass.ds(i * (TT * E), TT * E)], mp[:, 0:TT * E]).then_inc(logit_copied, 1)

                def group(i, first, last):
                    for g in range(KV):
                        nxt = (i + (g + 1) // KV, (g + 1) % KV)
                        nearly = isinstance(i, int) and i == NG - 2
                        prob_lo(i, g)
                        if last and g == KV - 1:
                            split_experts(experts.split_up)
                        if not (last and g == 3):
                            maxes(*nxt)
                        if first and g == 0:
                            split_q(3)
                        if g == 2 and not last:
                            carry_k(i + 1)
                        if g == 1 and not first:
                            norm_stats(i - 1)
                        if not (last and g == 3):
                            normalise(*nxt)
                        if g == 3 and not last:
                            carry_v(i + 1)
                        out_lo(i, g)
                        if g == 1:
                            if not last:
                                xt_lo_of(i + 1)
                            if not first:
                                norm_apply(i - 1)
                        if g == 2 and not last:
                            set_mask(i + 1)
                        if g == 3:
                            if not last:
                                v_lo_of(i + 1)
                                v_copies(i + 1)
                            if not first:
                                copy_logits(i - 1)
                        if nearly:
                            if g % 2 == 0:
                                select(dve, keep, step, g // 2, 0, EARLY)
                            else:
                                split_experts(experts.split_b[g // 2])
                        if last and g < 2:
                            split_experts(experts.split_low[g])
                        if first:
                            heads = slice(g * REP, (g + 1) * REP)
                            split_lo(wo_sb[:, LO, heads, :], raw_wo[g], wo_sb[:, HI, heads, :], AT_WO[g])

                step, splits_seen = [0], [0]

                def split_experts(weights):
                    for out, src in weights:
                        splits_seen[0] += 1
                        dve.wait_ge(e_hi, splits_seen[0])
                        lo_part(out(LO), src, out(HI)).then_inc(e_lo, 1)

                def split_lo(out, raw, hi, n):
                    dve.wait_ge(w_hi, n)
                    lo_part(out, raw, hi).then_inc(w_lo, 1)

                def split_q(g):
                    cols = slice(g * REP * HD, (g + 1) * REP * HD)
                    split_lo(wq_sb[:, LO, :, cols], raw_wq[g], wq_sb[:, HI, :, cols], AT_WQ[g])

                xt_lo_of(0)
                split_lo(wk_sb[:, LO, :, :], raw_wk, wk_sb[:, HI, :, :], AT_WK)
                split_q(0)
                split_lo(wv_sb[:, LO, :, :], raw_wv, wv_sb[:, HI, :, :], AT_WV)
                set_mask(0)
                split_q(1)
                maxes(0, 0)
                normalise(0, 0, (0,))
                v_lo_of(0)
                normalise(0, 0, (1,))
                v_copies(0)
                split_q(2)
                group(0, True, False)
                with dve.Fori(1, NG - 2) as i:
                    group(i, False, False)
                dve.wait_ge(order_ready, E)
                group(NG - 2, False, False)
                group(NG - 1, False, True)
                for c in range(DC):
                    dve.wait_ge(keep.x1t_hi, c + 1)
                    lo_part(x1t_first[:, LO, c, :], qp[c][:, :], x1t_first[:, HI, c, :]).then_inc(keep.x1t_lo, 1)
                norm_stats(NG - 1)
                norm_apply(NG - 1)
                split_experts(experts.split_last)
                split_experts(experts.split_gate)
                copy_logits(NG - 1)


def expert_phase(nc, sem, raw, experts, x1_dram, out, keep):
    NG2 = B * T // GT2
    TPB = T // P
    HALF = TT2 // 2
    with ExitStack() as ctx:
        def local(name, shape, dt=F32):
            return ctx.enter_context(nc.sbuf_tensor("ffn_" + name, shape, dt))

        up_sb, gt_sb, down_sb = experts.up, experts.gate, experts.down
        up_a_sb, gt_a_sb, down_a_sb = experts.up_a, experts.gate_a, experts.down_a
        up_b_sb, gt_b_sb, down_b_sb = experts.up_b, experts.gate_b, experts.down_b
        [product_z, c_rows, gated, mixed_sb] = carve(raw, [(4, GT2), (4, GT2), (2, GT2), (1, GT2)])

        ident, x1_in, x1_loaded, top, mask_tok = keep.ident, keep.x1_in, keep.x1_loaded, keep.top, keep.mask_tok
        minus_half, ident_bf, ones = keep.minus_half, keep.ident_bf, keep.ones
        x1_res = local("x1_res", [P, TT2, D])
        x1t = [keep.turned[:, :, :].rearrange("p a (c n) -> p a c n", c=DC), local("x1t", [P, 2, DC, GT2], F32R)]
        z_first = local("z_first", [P, 2, 2, 2, GT2], F32R)
        z_delta = local("z_delta", [P, 2, 2, 2, GT2], F32R)
        mask_rows = local("mask_rows", [P, 2, 2, GT2])
        mask_delta = local("mask_delta", [P, GT2])
        parts = local("parts", [P, 2, 3, 2, GT2], F32R)
        y_masked = local("y_masked", [P, 2, GT2])
        y_parts = local("y_parts", [P, 2, GT2], F32R)
        summed = local("summed", [P, TT2, D])
        stats = local("stats", [P, TT2, 6])
        mean_var = local("mean_var", [P, TT2, 2])
        var_eps = local("var_eps", [P, TT2])
        rstd = local("rstd", [P, TT2])
        spare = local("spare", [P, 1])
        mask_wide = local("mask_wide", [P, 2, TT2, ER], BF16)
        c_wide = local("c_wide", [P, 2, TT2, P])
        tile_max = local("tile_max", [P, 2 * B])
        seq_max = local("seq_max", [2 * B, 1])
        diag = local("diag", [2 * B, 2 * B])
        tile_sum = local("tile_sum", [P, 2 * B])
        seq_inv = local("seq_inv", [P, 2 * B])
        weight = local("weight", [P, 2, NT])

        banks = keep.banks
        pair = [(banks[2], banks[3]), (banks[0], banks[1])]
        z_bank = pair[1][1]
        yb = banks[4:6]
        ob = banks[6:8]

        res_loaded, out_stored = sem("res_loaded2"), sem("out_stored")
        down_hi, down_lo = sem("down_hi"), sem("down_lo")
        soft = sem("soft")
        max_turned, max_spread, exp_done, sum_spread = (
            sem("max_turned"), sem("max_spread"), sem("exp_done2"), sem("sum_spread"))
        weight_ready = sem("weight_ready")
        mask_wide_ready, c_wide_ready = keep.mask_wide_ready, sem("c_wide_ready")
        x1t_done, x1t_hi, x1t_lo = keep.x1t_done, keep.x1t_hi, keep.x1t_lo
        mask_done = keep.mask_done
        mask_copied, second_ready = sem("mask_copied"), sem("second_ready")
        c_done, c_copied = sem("c_done"), sem("c_copied")
        z_done = keep.z_done
        z_masked, z_hi, z_lo = sem("z_masked"), sem("z_hi"), sem("z_lo")
        z_up_delta_lo, z_gate_delta_lo = sem("z_up_delta_lo"), sem("z_gate_delta_lo")
        base_done, delta_done, silu_done = sem("base_done"), sem("delta_done"), sem("silu_done")
        gate_done, scale_done, mix_done = sem("gate_done"), sem("scale_done"), sem("mix_done")
        part_hi, part_lo, down_done = sem("part_hi"), sem("part_lo"), sem("down_done")
        y_done = sem("y_done")
        y_read, y_hi, y_lo, fold_done = sem("y_read2"), sem("y_hi"), sem("y_lo"), sem("fold_done")
        y_summed = sem("y_summed")
        out_read, stats_done, mean_done, var_ready, rstd_ready, norm_done = (
            sem("out_read"), sem("stats_done2"), sem("mean_done2"), sem("var_ready2"), sem("rstd_ready2"),
            sem("norm_done"))

        x1_tiles = x1_dram.rearrange("(n t p) d -> n p t d", t=TT2, p=P)
        out_tiles = out.rearrange("(n t p) d -> n p t d", t=TT2, p=P)

        def rows_of(j):
            return slice(0, HLAST if j == HC - 1 else P)

        def sums(j):
            if j == HC - 1:
                return pair[j % 2][0][HLAST:P, :], pair[j % 2][0][0:HLAST, :]
            return pair[j % 2][0][:, :], pair[j % 2][1][:, :]

        def lo_place(j, k):
            if j == HC - 1:
                return parts[HLAST:P, j % 2, k, HI, :]
            return parts[:, j % 2, k, LO, :]

        def down_product(pe, out_, stationary, moving, j, weights_first, start, stop):
            if j < HC - 1:
                return product(pe, out_, lambda a, c: stationary(a, slice(0, P)),
                               lambda a, c: moving(a, slice(0, P)), (0,), start, stop)
            half = slice(0, HLAST)
            a, b = (LO, HI) if weights_first else (HI, LO)
            pe.matmul(out_, stationary(HI, slice(0, P)), moving(HI, slice(0, P)), start=start,
                      stop=False, skip_group_check=True)
            return pe.matmul(out_, stationary(a, half), moving(b, half), start=False, stop=stop,
                             skip_group_check=True)

        def each_group(eng, group):
            group(0, 0)
            group(1, 1)
            with eng.Fori(1, NG2 // 2 - 1) as m:
                group(2 * m, 0)
                group(2 * m + 1, 1)
            group(NG2 - 2, 0)
            group(NG2 - 1, 1)

        with nc.Block() as block:

            @block.sync
            def _(sp_):
                def load_x1(n):
                    need(sp_, x1t_done, n)
                    sp_.dma_start(x1_in[:, :, :], x1_tiles[n]).then_inc(x1_loaded, 16)

                def load_res(n):
                    need(sp_, out_read, TT2 * n)
                    sp_.dma_start(x1_res[:, :, :], x1_tiles[n]).then_inc(res_loaded, 16)

                def store(n, first=0, end=TT2):
                    sp_.wait_ge(norm_done, TT2 * n + end)
                    sp_.dma_start(out_tiles[n][:, first:end, :], summed[:, first:end, :]).then_inc(out_stored, 16)

                sp_.wait_ge(keep.x1_stored, 16 * NG)
                load_x1(1)
                load_res(0)
                with sp_.Fori(1, NG2 - 1) as n:
                    load_x1(n + 1)
                    load_res(n)
                    store(n - 1)
                load_res(NG2 - 1)
                store(NG2 - 2)
                for half in range(2):
                    store(NG2 - 1, HALF * half, HALF * (half + 1))
                sp_.wait_ge(out_stored, 16 * (NG2 + 1))

            @block.gpsimd
            def _(pool):
                def widen_masks(n):
                    need(pool, mask_done, n)
                    for k in range(2):
                        src = mask_tok[:, k, :, :].rearrange("p t e -> p (t e)")[:, bass.ds(n * (TT2 * E), TT2 * E)]
                        pool.tensor_copy(mask_wide[:, k, :, :].rearrange("p t (e r) -> p (t e) r", r=R),
                                         src.unsqueeze(2).to_broadcast([P, TT2 * E, R])).then_inc(mask_wide_ready, 1)

                def widen_weights(n):
                    need(pool, c_done, n)
                    for k in range(2):
                        pool.tensor_copy(c_wide[:, k, :, :],
                                         weight[:, k, bass.ds(n * TT2, TT2)].unsqueeze(2).to_broadcast([P, TT2, P]))\
                            .then_inc(c_wide_ready, 1)

                def rstd_of(n, first=0, end=TT2):
                    pool.wait_ge(var_ready, TT2 * n + end)
                    need(pool, norm_done, TT2 * n)
                    pool.tensor_tensor(rstd[:, first:end], var_eps[:, first:end], minus_half[:, first:end],
                                       ALU.pow).then_inc(rstd_ready, end - first)

                def second_mask(n, p):
                    pool.wait_ge(mask_copied, 2 * n + 2)
                    need(pool, y_read, 2 * n - 2)
                    pool.tensor_tensor(mask_rows[:, p, 1, :], mask_rows[:, p, 0, :], mask_delta[:, :],
                                       ALU.add).then_inc(second_ready, 1)

                def z_delta_lo(n, p):
                    pool.wait_ge(z_hi, 4 * n + 2)
                    pool.tensor_tensor(z_delta[:, p, 0, LO, :], product_z[:, 1, :], z_delta[:, p, 0, HI, :].bitcast(F32),
                                       ALU.subtract).then_inc(z_up_delta_lo, 1)

                def sum_y(n):
                    pool.wait_ge(y_read, 2 * n + 2)
                    pool.tensor_tensor(y_masked[:, 0, :], y_masked[:, 0, :], y_masked[:, 1, :], ALU.add).then_inc(y_summed, 1)

                def group(n, p):
                    first = isinstance(n, int) and n == 0
                    last = isinstance(n, int) and n == NG2 - 1
                    if not first:
                        sum_y(n - 1)
                    if not last:
                        second_mask(n + 1, 1 - p)
                    if not first:
                        rstd_of(n - 1)
                    if not (isinstance(n, int) and n >= NG2 - 2):
                        widen_masks(n + 2)
                        widen_weights(n + 2)
                    if not last:
                        z_delta_lo(n + 1, 1 - p)

                z_delta_lo(0, 0)
                widen_masks(1)
                second_mask(0, 0)
                pool.wait_ge(weight_ready, 1)
                widen_weights(1)
                each_group(pool, group)
                for half in range(2):
                    rstd_of(NG2 - 1, HALF * half, HALF * (half + 1))

            @block.tensor
            def _(pe):
                def turn_x1(n):
                    pe.wait_ge(x1_loaded, 16 * (n + 1))
                    turn_tiles(pe, pair[1], x1_in, ident).then_inc(x1t_done, 1)

                def turn_masks(n):
                    pe.wait_ge(mask_wide_ready, 2 * n + 2)
                    turn_mask_tiles(pe, pair[0], mask_wide, ident_bf).then_inc(mask_done, 1)

                def turn_weights(n, banks):
                    pe.wait_ge(c_wide_ready, 2 * n + 2)
                    for k in range(2):
                        for t in range(TT2):
                            last = pe.transpose(banks[k][:, t * P:(t + 1) * P], c_wide[:, k, t, :], ident[:, :])
                    last.then_inc(c_done, 1)

                def low_rank_in(n, p, k):
                    if k == 1:
                        pe.wait_ge(z_masked, 4 * n + 2)
                    pe.wait_ge(x1t_lo, 2 * n + 2)
                    w = (up_a_sb, gt_a_sb)[k]
                    product(pe, z_bank[:, :], lambda a, c: w[:, a, c, :],
                            lambda a, c: x1t[p][:, a, c, :], range(DC)).then_inc(z_done, 1)

                def base(n, p, j):
                    u = HC * n + j
                    need(pe, gate_done, 2 * u - 2)
                    slot = {2: mask_copied, 3: x1t_lo, 4: c_copied}.get(j)
                    if slot:
                        pe.wait_ge(slot, 2 * n + 2 if n_is_last(n) else 2 * n + 4)
                    cols = slice(j * P, (j + 1) * P)
                    if j == HC - 1:
                        product(pe, pair[j % 2][0][:, :], lambda a, c: up_sb[:, a, c, cols],
                                lambda a, c: x1t[p][:, a, c, :], range(DC), stop=False)
                    for k, (w, wb) in enumerate(((up_sb, up_b_sb), (gt_sb, gt_b_sb))):
                        bank_ = pair[j % 2][0 if j == HC - 1 else k]
                        if j == 0 and k == 1 and isinstance(n, int) and n == 0:
                            pe.wait_ge(z_masked, 4)
                        if j < HC - 1:
                            product(pe, bank_[:, :], lambda a, c: w[:, a, c, cols],
                                    lambda a, c: x1t[p][:, a, c, :], range(DC), stop=False)
                        if j == 0 and k == 1 and isinstance(n, int) and n == 0:
                            pe.wait_ge(soft, 3)
                            pe.matmul(ob[0][:, P:P + 2 * B], ones[0:2 * B, :], diag[:, :], start=True,
                                      stop=True).then_inc(max_spread, 1)
                        if j == 0:
                            pe.wait_ge(z_lo, 2 * n + k + 1)
                        last = product(pe, bank_[:, :], lambda a, c: wb[:, a, cols],
                                       lambda a, c: z_first[:, p, k, a, :], (0,), start=False)
                        if j == 0 and k == 0 and isinstance(n, int) and n == 0:
                            pe.wait_ge(soft, 1)
                            pe.transpose(ob[0][0:2 * B, 0:P], tile_max[:, :], ident[:, :]).then_inc(max_turned, 1)
                    last.then_inc(base_done, 1)

                def n_is_last(n):
                    return isinstance(n, int) and n == NG2 - 1

                def delta(n, p, j):
                    u = HC * n + j
                    pe.wait_ge(gate_done, 2 * u + 1)
                    cols = slice(j * P, (j + 1) * P)
                    for k, wb in enumerate((up_b_sb, gt_b_sb)):
                        if j == 0:
                            pe.wait_ge((z_up_delta_lo, z_gate_delta_lo)[k], n + 1)
                        last = product(pe, pair[j % 2][0 if j == HC - 1 else k][:, :], lambda a, c: wb[:, a, cols],
                                       lambda a, c: z_delta[:, p, k, a, :], (0,), start=False)
                    last.then_inc(delta_done, 1)

                def down_low_rank(n, j):
                    u = HC * n + j
                    if j == 0:
                        need(pe, y_read, 2 * n)
                    for k in range(2):
                        pe.wait_ge(part_lo, 3 * u + k + 1)
                        last = down_product(pe, yb[k][:, :], lambda a, rows: down_a_sb[rows, a, j, :],
                                            lambda a, rows: parts[rows, j % 2, k, a, :], j, weights_first=True,
                                            start=(j == 0), stop=(j == HC - 1))
                        if j == HC - 1:
                            last.then_inc(y_done, 1)

                def down(n, j):
                    u = HC * n + j
                    if j == 0:
                        need(pe, out_read, TT2 * n - HALF)
                        if isinstance(n, int) and n == 0:
                            pe.wait_ge(c_copied, 2)
                        if isinstance(n, int) and n == 0:
                            pe.wait_ge(down_lo, 1)
                    pe.wait_ge(part_lo, 3 * u + 3)
                    for t in range(TT2):
                        if j == 0 and t == HALF:
                            need(pe, out_read, TT2 * n)
                        last = down_product(pe, ob[t // 2][:, (t % 2) * D:(t % 2 + 1) * D],
                                            lambda a, rows: parts[rows, j % 2, 2, a, t * P:(t + 1) * P],
                                            lambda a, rows: down_sb[rows, a, j, :], j, weights_first=False,
                                            start=(j == 0 and t % 2 == 0), stop=False)
                    last.then_inc(down_done, 1)

                def fold(n):
                    pe.wait_ge(y_lo, n + 1)
                    for t in range(TT2):
                        last = product(pe, ob[t // 2][:, (t % 2) * D:(t % 2 + 1) * D],
                                       lambda a, c: y_parts[:, a, t * P:(t + 1) * P],
                                       lambda a, c: down_b_sb[:, a, :], (0,), start=False)
                        if (t + 1) % HALF == 0:
                            last.then_inc(fold_done, HALF)

                def group(n, p):
                    first = isinstance(n, int) and n == 0
                    last = n_is_last(n)
                    for j in range(HC):
                        u = HC * n + j
                        base(n, p, j)
                        if not last:
                            if j > 0:
                                pe.wait_ge(gate_done, 2 * u)
                            if j == 3:
                                turn_weights(n + 1, pair[0])
                            elif j == 1:
                                turn_masks(n + 1)
                            elif j == 2:
                                turn_x1(n + 1)
                            elif j == HC - 2:
                                low_rank_in(n + 1, 1 - p, 0)
                        if j > 0 or not first:
                            before = (n, j - 1) if j > 0 else (n - 1, HC - 1)
                            down_low_rank(*before)
                            if j == 1:
                                if not first:
                                    fold(n - 1)
                                delta(n, p, j)
                            down(*before)
                        if j == 0 and first:
                            pe.wait_ge(soft, 5)
                            pe.matmul(ob[1][:, 0:2 * B], ones[:, :], tile_sum[:, :], start=True, stop=True).then_inc(sum_spread, 1)
                            turn_weights(0, ob)
                        if j != 1:
                            delta(n, p, j)
                        if j == HC - 2 and not last:
                            low_rank_in(n + 1, 1 - p, 1)

                each_group(pe, group)
                down_low_rank(NG2 - 1, HC - 1)
                down(NG2 - 1, HC - 1)
                fold(NG2 - 1)

            @block.scalar
            def _(act):
                def turned_hi(n, p):
                    for c in range(DC):
                        act.wait_ge(x1t_done, n + 1)
                        act.activation(x1t[p][:, HI, c, :], pair[1][c][:, :], ACT.Copy).then_inc(x1t_hi, 1)

                def copy_masks(n, p, banks=pair[0]):
                    act.wait_ge(mask_done, n + 1)
                    need(act, y_read, 2 * n - 2)
                    act.activation(mask_rows[:, p, 0, :], banks[0][:, :], ACT.Copy).then_inc(mask_copied, 1)
                    need(act, z_masked, 4 * n)
                    need(act, second_ready, n)
                    act.activation(mask_delta[:, :], banks[1][:, :], ACT.Copy).then_inc(mask_copied, 1)

                def copy_weights(n, p, banks):
                    act.wait_ge(c_done, n + 1)
                    for k in range(2):
                        act.activation(c_rows[:, 2 * p + k, :], banks[k][:, :], ACT.Copy).then_inc(c_copied, 1)

                def z_hi_of(n, p, which, k):
                    act.wait_ge(z_masked, 4 * n + 2 * k + which + 1)
                    act.activation((z_first, z_delta)[which][:, p, k, HI, :], product_z[:, 2 * k + which, :], ACT.Copy).then_inc(z_hi, 1)

                def silu(n, j, k):
                    u = HC * n + j
                    if k == 0:
                        act.wait_ge(base_done, u + 1)
                        need(act, mix_done, u)
                        need(act, part_lo, 3 * u - 2)
                    else:
                        act.wait_ge(delta_done, u + 1)
                        need(act, part_lo, 3 * u - 1)
                    act.activation(gated[rows_of(j), k, :], sums(j)[0], ACT.Silu).then_inc(silu_done, 1)

                def part_hi_of(n, j, k):
                    u = HC * n + j
                    if k < 2:
                        act.wait_ge(scale_done, 2 * u + k + 1)
                    else:
                        act.wait_ge(mix_done, u + 1)
                    need(act, down_done, u - 1)
                    rows = rows_of(j)
                    act.activation(parts[rows, j % 2, k, HI, :], gated[rows, k, :] if k < 2 else mixed_sb[rows, 0, :],
                                   ACT.Copy).then_inc(part_hi, 1)

                def y_hi_of(n):
                    act.wait_ge(y_summed, n + 1)
                    need(act, fold_done, TT2 * n)
                    act.activation(y_parts[:, HI, :], y_masked[:, 0, :], ACT.Copy).then_inc(y_hi, 1)

                def group(n, p):
                    first = isinstance(n, int) and n == 0
                    last = isinstance(n, int) and n == NG2 - 1
                    for j in range(HC):
                        silu(n, j, 0)
                        if not last:
                            if j == 3:
                                copy_weights(n + 1, 1 - p, pair[0])
                            elif j == 1:
                                copy_masks(n + 1, 1 - p)
                            elif j == 2:
                                turned_hi(n + 1, 1 - p)
                        if j == 0 and first:
                            copy_weights(0, 0, ob)
                        part_hi_of(n, j, 0)
                        if j == HC - 2 and not last:
                            z_hi_of(n + 1, 1 - p, 0, 0)
                            z_hi_of(n + 1, 1 - p, 1, 0)
                        if j == HC - 1 and not last:
                            z_hi_of(n + 1, 1 - p, 0, 1)
                            z_hi_of(n + 1, 1 - p, 1, 1)
                        silu(n, j, 1)
                        part_hi_of(n, j, 1)
                        part_hi_of(n, j, 2)
                        if j == 0 and not first:
                            y_hi_of(n - 1)

                copy_masks(0, 0, (pair[1][0], yb[1]))
                for k in range(2):
                    for which in range(2):
                        z_hi_of(0, 0, which, k)
                act.activation(down_sb[:, HI, :, :], experts.raw_down, ACT.Copy).then_inc(down_hi, 1)
                act.wait_ge(soft, 4)
                act.activation(top[:, :, :], top[:, :, :], ACT.Exp).then_inc(exp_done, 1)
                each_group(act, group)
                y_hi_of(NG2 - 1)

            @block.vector
            def _(dve):
                def lo_part(out_, src, hi):
                    return dve.tensor_tensor(out_, src, hi.bitcast(F32), ALU.subtract)

                def turned_lo(n, p):
                    for c in range(DC):
                        dve.wait_ge(x1t_hi, 2 * n + c + 1)
                        lo_part(x1t[p][:, LO, c, :], pair[1][c][:, :], x1t[p][:, HI, c, :]).then_inc(x1t_lo, 1)

                def mask_z(n, p, k):
                    dve.wait_ge(z_done, 2 * n + k + 1)
                    if k == 0:
                        need(dve, z_gate_delta_lo, n)
                        need(dve, z_up_delta_lo, n)
                    for which in range(2):
                        m = mask_rows[:, p, 0, :] if which == 0 else mask_delta[:, :]
                        bank = pair[0][1] if k == 1 and isinstance(n, int) and n == 0 else z_bank
                        dve.tensor_tensor(product_z[:, 2 * k + which, :], bank[:, :], m, ALU.mult).then_inc(z_masked, 1)

                def z_lo_of(n, p, which, k):
                    dve.wait_ge(z_hi, 4 * n + 2 * k + which + 1)
                    both = (z_first, z_delta)[which][:, p, k, :, :]
                    done = z_gate_delta_lo if which == 1 else z_lo
                    lo_part(both[:, LO, :], product_z[:, 2 * k + which, :], both[:, HI, :]).then_inc(done, 1)

                def gate(n, j, k):
                    u = HC * n + j
                    dve.wait_ge(silu_done, 2 * u + k + 1)
                    rows = rows_of(j)
                    dve.tensor_tensor(gated[rows, k, :], gated[rows, k, :], sums(j)[1], ALU.mult).then_inc(gate_done, 1)

                def scale(n, p, j, k):
                    u = HC * n + j
                    dve.wait_ge(gate_done, 2 * u + k + 1)
                    if j == 0:
                        dve.wait_ge(c_copied, 2 * n + 2)
                    rows = rows_of(j)
                    dve.tensor_tensor(gated[rows, k, :], gated[rows, k, :], c_rows[rows, 2 * p + k, :],
                                      ALU.mult).then_inc(scale_done, 1)

                def mix(n, j):
                    u = HC * n + j
                    dve.wait_ge(scale_done, 2 * u + 2)
                    need(dve, part_hi, 3 * u)
                    need(dve, part_lo, 3 * u)
                    rows = rows_of(j)
                    dve.tensor_tensor(mixed_sb[rows, 0, :], gated[rows, 0, :], gated[rows, 1, :], ALU.add).then_inc(mix_done, 1)

                def part_lo_of(n, j, k):
                    u = HC * n + j
                    dve.wait_ge(part_hi, 3 * u + k + 1)
                    rows = rows_of(j)
                    lo_part(lo_place(j, k), gated[rows, k, :] if k < 2 else mixed_sb[rows, 0, :],
                            parts[rows, j % 2, k, HI, :]).then_inc(part_lo, 1)

                def mask_y(n, p):
                    need(dve, y_lo, n)
                    for k in range(2):
                        dve.wait_ge(y_done, 2 * n + k + 1)
                        dve.tensor_tensor(y_masked[:, k, :], yb[k][:, :], mask_rows[:, p, k, :], ALU.mult).then_inc(y_read, 1)

                def y_lo_of(n):
                    dve.wait_ge(y_hi, n + 1)
                    lo_part(y_parts[:, LO, :], y_masked[:, 0, :], y_parts[:, HI, :]).then_inc(y_lo, 1)

                def add_out(n, first=0, end=TT2):
                    dve.wait_ge(res_loaded, 16 * (n + 1))
                    need(dve, out_stored, 16 * n)
                    for t in range(first, end, HALF):
                        dve.wait_ge(fold_done, TT2 * n + t + HALF)
                        dve.tensor_tensor(summed[:, t:t + HALF, :].rearrange("p t d -> p (t d)"), ob[t // HALF][:, :],
                                          x1_res[:, t:t + HALF, :].rearrange("p t d -> p (t d)"), ALU.add).then_inc(out_read, HALF)

                def norm_stats(n, first=0, end=TT2):
                    dve.wait_ge(out_read, TT2 * n + end)
                    for t in range(first, end):
                        last = dve.bn_stats(stats[:, t, :], summed[:, t, :])
                    last.then_inc(stats_done, end - first)
                    dve.wait_ge(stats_done, TT2 * n + end)
                    dve.memset(spare[:, :], 0.0)
                    for t in range(first, end):
                        last = dve.bn_aggr(mean_var[:, t, :], stats[:, t, :])
                    last.then_inc(mean_done, end - first)
                    dve.wait_ge(mean_done, TT2 * n + end)
                    dve.tensor_scalar(var_eps[:, first:end], mean_var[:, first:end, 1], EPS, None,
                                      ALU.add).then_inc(var_ready, end - first)

                def norm_apply(n, first=0, end=TT2):
                    dve.wait_ge(rstd_ready, TT2 * n + end)
                    for t in range(first, end):
                        last = dve.tensor_scalar(summed[:, t, :], summed[:, t, :], mean_var[:, t, 0:1],
                                                 rstd[:, t:t + 1], ALU.subtract, ALU.mult)
                    last.then_inc(norm_done, end - first)

                step = [0]

                def softmax_step(instruction):
                    step[0] += 1
                    instruction.then_inc(soft, 1)
                    dve.wait_ge(soft, step[0])

                by_seq = top[:, :, :].rearrange("p k (b t) -> p (k b) t", t=TPB)

                def first_weights():
                    dve.wait_ge(sum_spread, 1)
                    softmax_step(dve.reciprocal(seq_inv[:, :], ob[1][:, 0:2 * B]))
                    dve.tensor_tensor(weight[:, :, :].rearrange("p k (b t) -> p (k b) t", t=TPB), by_seq,
                                      seq_inv[:, :].unsqueeze(2).to_broadcast([P, 2 * B, TPB]), ALU.mult).then_inc(weight_ready, 1)
                    dve.wait_ge(weight_ready, 1)
                    for k in range(2):
                        dve.tensor_copy(c_wide[:, k, :, :], weight[:, k, 0:TT2].unsqueeze(2).to_broadcast([P, TT2, P]))\
                            .then_inc(c_wide_ready, 1)

                def group(n, p):
                    first = isinstance(n, int) and n == 0
                    last = isinstance(n, int) and n == NG2 - 1
                    for j in range(HC):
                        gate(n, j, 0)
                        if first and j == 0:
                            dve.wait_ge(down_hi, 1)
                            lo_part(down_sb[:, LO, :, :], experts.raw_down, down_sb[:, HI, :, :]).then_inc(down_lo, 1)
                        scale(n, p, j, 0)
                        if j == HC - 2 and not last:
                            mask_z(n + 1, 1 - p, 0)
                        if not last and j == 2:
                            turned_lo(n + 1, 1 - p)
                        if j == 1 and not first:
                            add_out(n - 1)
                        part_lo_of(n, j, 0)
                        if j == 0 and not first:
                            mask_y(n - 1, 1 - p)
                        if j == HC - 2 and not last:
                            z_lo_of(n + 1, 1 - p, 0, 0)
                        if j == HC - 1 and not last:
                            z_lo_of(n + 1, 1 - p, 0, 1)
                        gate(n, j, 1)
                        scale(n, p, j, 1)
                        mix(n, j)
                        part_lo_of(n, j, 1)
                        part_lo_of(n, j, 2)
                        if j == 0 and not first:
                            y_lo_of(n - 1)
                        if j == 2 and not first:
                            norm_stats(n - 1)
                        if j == 3 and not first:
                            norm_apply(n - 1)
                        if j == HC - 2 and not last:
                            mask_z(n + 1, 1 - p, 1)
                        if j == HC - 1 and not last:
                            z_lo_of(n + 1, 1 - p, 1, 1)

                routed_steps = [ROUTED_EARLY]
                select(dve, keep, routed_steps, 0, EARLY, NT)
                dve.wait_ge(mask_copied, 2)
                mask_z(0, 0, 0)
                z_lo_of(0, 0, 0, 0)
                mask_z(0, 0, 1)
                select(dve, keep, routed_steps, 1, EARLY, NT)
                softmax_step(dve.tensor_reduce(tile_max[:, :], by_seq, AX.X, ALU.max))
                z_lo_of(0, 0, 0, 1)
                dve.wait_ge(max_turned, 1)
                softmax_step(dve.tensor_reduce(seq_max[:, :], ob[0][0:2 * B, 0:P], AX.X, ALU.max))
                softmax_step(dve.tensor_scalar(diag[:, :], ident[0:2 * B, 0:2 * B], seq_max[:, 0:1], None, ALU.mult))
                z_lo_of(0, 0, 1, 1)
                dve.wait_ge(max_spread, 1)
                seq_maxes = ob[0][:, P:P + 2 * B].unsqueeze(2).to_broadcast([P, 2 * B, TPB])
                softmax_step(dve.tensor_tensor(by_seq, by_seq, seq_maxes, ALU.subtract))
                dve.wait_ge(exp_done, 1)
                softmax_step(dve.tensor_reduce(tile_sum[:, :], by_seq, AX.X, ALU.add))
                first_weights()
                each_group(dve, group)
                mask_y(NG2 - 1, 1)
                dve.wait_ge(y_read, 2 * NG2)
                dve.tensor_tensor(y_masked[:, 0, :], y_masked[:, 0, :], y_masked[:, 1, :], ALU.add).then_inc(y_summed, 1)
                y_lo_of(NG2 - 1)
                for half in range(2):
                    add_out(NG2 - 1, HALF * half, HALF * (half + 1))
                    norm_stats(NG2 - 1, HALF * half, HALF * (half + 1))
                for half in range(2):
                    norm_apply(NG2 - 1, HALF * half, HALF * (half + 1))


def build(nc, x, wq, wk, wv, wo, gate_wt, w_up, w_gate, w_down, up_a, up_b, gate_a, gate_b, down_a, down_b, out):
    x1_dram = nc.dram_tensor("x1_dram", [B * T, D], F32, kind="Internal").ap()
    with ExitStack() as ctx:
        def sem(name):
            return ctx.enter_context(nc.semaphore(name))

        def sbuf(name, shape, dt=F32):
            return ctx.enter_context(nc.sbuf_tensor(name, shape, dt))

        keep = Named()
        keep.ident, keep.ident_bf, keep.ones = sbuf("ident", [P, P]), sbuf("ident_bf", [P, P], BF16), sbuf("ones", [P, P])
        keep.minus_half = sbuf("minus_half", [P, TT2])
        keep.x1_cur = sbuf("x1_cur", [P, TT, D])
        keep.x1_in = sbuf("x1_in", [P, TT2, D])
        keep.turned = sbuf("turned", [P, 2, DC * GT2], F32R)
        keep.logits, keep.same = sbuf("logits", [P, NT * E]), sbuf("same", [P, NT, E])
        keep.chosen = sbuf("chosen", [P, 2, NT, E])
        keep.order, keep.key = sbuf("order", [P, E]), sbuf("key", [P, NT])
        keep.top = sbuf("top", [P, 2, NT])
        keep.mask_tok = sbuf("mask_tok", [P, 2, NT, E], BF16)
        keep.banks = [ctx.enter_context(nc.psum_tensor(f"bank{k}", [P, 512], F32)) for k in range(8)]
        keep.ffn_loaded, keep.x1_loaded, keep.x1_stored = sem("ffn_loaded"), sem("x1_loaded2"), sem("x1_stored")
        keep.route, keep.order_ready = sem("route"), sem("order_ready")
        keep.x1t_done, keep.x1t_hi, keep.x1t_lo = sem("x1t_done2"), sem("x1t_hi"), sem("x1t_lo")
        keep.z_done, keep.mask_wide_ready, keep.mask_done = sem("z_done"), sem("mask_wide_ready"), sem("mask_done")
        raw = sbuf("raw", [P, RAW])
        split_area = sbuf("split_area", [P, 2 * DC * (HEADS + 2 * KV) * HD], F32R)
        experts = expert_weights(raw, split_area, sbuf("up_b_sb", [P, 2, HPAD], F32R), sbuf("gt_b_sb", [P, 2, HPAD], F32R))

        def by_rows(w):
            return w.rearrange("(c p) n -> p c n", p=P)

        r_up, r_gate, r_up_a, r_gate_a, r_up_b, r_gate_b, r_down_a, r_down_b, r_down = experts.raw
        ffn_loads = [
            (r_up, by_rows(w_up)), (r_gate, by_rows(w_gate)), (r_up_a, by_rows(up_a)), (r_gate_a, by_rows(gate_a)),
            (r_up_b[:, 0, :], up_b), (r_gate_b[:, 0, :], gate_b), (r_down_b[:, 0, :], down_b),
        ]
        for r_, w_ in ((r_down_a, down_a), (r_down, w_down)):
            ffn_loads += [(r_[:, 0:HC - 1, :], by_rows(w_[0:WHOLE, :])), (r_[0:HLAST, HC - 1, :], w_[WHOLE:, :]),
                          (r_[HLAST:P, HC - 1, :], w_[WHOLE:, :])]
        attention_phase(nc, sem, raw, split_area, experts, x, wq, wk, wv, wo, gate_wt, ffn_loads, x1_dram, keep)
        expert_phase(nc, sem, raw, experts, x1_dram, out, keep)


def kernel(**inputs):
    import numpy as np
    import concourse.bacc as bacc
    from concourse.bass_utils import run_bass_kernel_spmd

    def put(name):
        return np.asarray(inputs[name])

    def rows_first(a):
        return a.transpose(0, 2, 1).reshape(ER, a.shape[1])

    arrays = {
        "x": put("L0_attn_x").reshape(B * T, D),
        "wq": put("L0_attn_Wq"), "wk": put("L0_attn_Wk"), "wv": put("L0_attn_Wv"), "wo": put("L0_attn_Wo"),
        "gate_wt": put("L0_ffn_gate_w").T,
        "w_up": put("L0_ffn_w_up").T, "w_gate": put("L0_ffn_w_gate").T, "w_down": put("L0_ffn_w_down").T,
        "up_a": put("L0_ffn_up_A").reshape(ER, D).T, "up_b": rows_first(put("L0_ffn_up_B")),
        "gate_a": put("L0_ffn_gate_A").reshape(ER, D).T, "gate_b": rows_first(put("L0_ffn_gate_B")),
        "down_a": put("L0_ffn_down_A").reshape(ER, HID).T, "down_b": rows_first(put("L0_ffn_down_B")),
    }
    arrays = {name: np.ascontiguousarray(a) for name, a in arrays.items()}
    nc = bacc.Bacc("TRN2", target_bir_lowering=False, num_devices=1)
    args = [nc.dram_tensor(name, a.shape, F32, kind="ExternalInput").ap() for name, a in arrays.items()]
    out = nc.dram_tensor("out", [B * T, D], F32, kind="ExternalOutput").ap()
    build(nc, *args, out)
    result = run_bass_kernel_spmd(nc, [arrays], core_ids=[0])
    return np.asarray(result.results[0]["out"]).reshape(B, T, D)
```
